# Optimizing a Trainium2 kernel written in Bass

```python
import numpy as np
import jax
import jax.numpy as jnp

def _softmax(x, axis=-1):
    return jax.nn.softmax(x, axis=axis)

def _gelu(x):
    return jax.nn.gelu(x, approximate=True)

def _silu(x):
    return jax.nn.silu(x)

def _sigmoid(x):
    return jax.nn.sigmoid(x)

def _layernorm(x, axis=-1, eps=1e-05):
    m = jnp.mean(x, axis=axis, keepdims=True)
    v = jnp.var(x, axis=axis, keepdims=True)
    return (x - m) / jnp.sqrt(v + eps)

def _scatter_add(tgt, idx, src, axis=0):
    return tgt.at[idx].add(src)

def _segment_sum(src, seg, n):
    return jax.ops.segment_sum(src, seg, n)
kernel_name = 'mk_xattn_seq_d4_seqx_r8_85b34b'

def setup_inputs(seed: int=0):
    np.random.seed(seed)
    _w = jnp.asarray

    def _rec_inputs():
        import jax
        import jax.numpy as jnp
        _rk = jax.random.key(seed)
        x = -0.0005207 + 1.001 * jax.random.normal(jax.random.fold_in(_rk, 1), (64, 128, 128), jnp.float32)
        _lenS = 128 - jax.random.randint(jax.random.fold_in(_rk, 7), (64,), 0, max(1, 128 // 4) + 1, jnp.int32)
        _lenS2 = 77 - jax.random.randint(jax.random.fold_in(_rk, 8), (64,), 0, max(1, 77 // 4) + 1, jnp.int32)
        _ctx_1024P = jax.random.normal(jax.random.fold_in(_rk, 12), (64, 16, 128), jnp.float32)
        _ctx_1024c = jax.random.dirichlet(jax.random.fold_in(_rk, 512), 0.3 * jnp.ones((16,), jnp.float32), (64, 77))
        _ctx_1024t = jnp.einsum('bsk,bkd->bsd', _ctx_1024c, _ctx_1024P)
        _ctx_1024t = _ctx_1024t * jax.lax.rsqrt(jnp.mean(jnp.square(_ctx_1024t)) + 1e-12) * 0.953939
        ctx_1024 = -0.000514642 + 1.00011 * (_ctx_1024t + 0.3 * jax.random.normal(jax.random.fold_in(_rk, 612), (64, 77, 128), jnp.float32))
        _validS = jnp.arange(128)[None, :] < _lenS[:, None]
        _validS2 = jnp.arange(77)[None, :] < _lenS2[:, None]
        _causal = jnp.tril(jnp.ones((128, 128), dtype=bool))
        mask_1x1xSxS2_ff0 = jnp.where(jnp.ones((1, 1, 128, 77), dtype=bool), 0.0, -1000000000.0).astype(jnp.float32)
        mask_1xSxS2_bk1 = jnp.broadcast_to(_validS2[0:1, None, :], (1, 128, 77))
        return (x, ctx_1024, mask_1x1xSxS2_ff0, mask_1xSxS2_bk1)
    x, ctx_1024, mask_1x1xSxS2_ff0, mask_1xSxS2_bk1 = _rec_inputs()

    def _L0_xattn_setup():
        import jax, jax.numpy as jnp
        import numpy as np
        B, Q, C, H, N, D, F = (1, 256, 256, 128, 16, 64, 512)
        R = Q + C
        EPS = 1e-12
        NEG = 1e+30

        def _layernorm(x, g, b):
            m = jnp.mean(x, axis=-1, keepdims=True)
            v = jnp.mean(jnp.square(x - m), axis=-1, keepdims=True)
            return (x - m) * jax.lax.rsqrt(v + EPS) * g + b

        def _rel_shift(x, klen):
            b, n, q, r = x.shape
            x = x.reshape(b, n, r, q)[:, :, 1:, :].reshape(b, n, q, r - 1)
            return x[:, :, :, :klen]
        key = jax.random.key(seed)
        ks = jax.random.split(key, 16)
        s = 0.02
        return dict(content_stream=jax.random.normal(ks[0], (B, Q, H), jnp.float32), content_mask=jnp.zeros((B, 1, Q, C), jnp.float32), context=jax.random.normal(ks[1], (B, C, H), jnp.float32), position_encoding=jax.random.normal(ks[2], (B, R, H), jnp.float32), content_bias=jax.random.normal(ks[3], (N, D), jnp.float32) * s, position_bias=jax.random.normal(ks[4], (N, D), jnp.float32) * s, segment_encoding=jax.random.normal(ks[5], (2, N, D), jnp.float32) * s, segment_matrix=jax.random.randint(ks[6], (B, Q, C), 0, 2).astype(bool), segment_bias=jax.random.normal(ks[7], (N, D), jnp.float32) * s, Wq=jax.random.normal(ks[8], (H, N, D), jnp.float32) * s, Wk=jax.random.normal(ks[9], (H, N, D), jnp.float32) * s, Wv=jax.random.normal(ks[10], (H, N, D), jnp.float32) * s, Wr=jax.random.normal(ks[11], (H, N, D), jnp.float32) * s, Wo=jax.random.normal(ks[12], (H, N, D), jnp.float32) * s, ln1_gamma=jnp.ones((H,), jnp.float32), ln1_beta=jnp.zeros((H,), jnp.float32), W1=jax.random.normal(ks[13], (H, F), jnp.float32) * s, b1=jnp.zeros((F,), jnp.float32), W2=jax.random.normal(ks[14], (F, H), jnp.float32) * s, b2=jnp.zeros((H,), jnp.float32), ln2_gamma=jnp.ones((H,), jnp.float32), ln2_beta=jnp.zeros((H,), jnp.float32))
    _L0_xattn_all = _L0_xattn_setup()
    _L0_xattn_in = {k: v for k, v in _L0_xattn_all.items() if k in ('position_encoding', 'content_bias', 'position_bias', 'segment_encoding', 'segment_bias', 'Wq', 'Wk', 'Wv', 'Wr', 'Wo', 'ln1_gamma', 'ln1_beta', 'W1', 'b1', 'W2', 'b2', 'ln2_gamma', 'ln2_beta')}
    del _L0_xattn_all

    def _L1_xattn_setup():
        import jax, jax.numpy as jnp
        import numpy as np
        B, Q, KV = (2, 256, 256)
        D_MODEL = 128
        N_HEADS = 16
        D_KV = 64
        EPS = 1e-06
        key = jax.random.key(seed)
        ks = jax.random.split(key, 7)
        s = 0.02
        return {'hidden_states': jax.random.normal(ks[0], (B, Q, D_MODEL), jnp.float32), 'key_value_states': jax.random.normal(ks[1], (B, KV, D_MODEL), jnp.float32), 'wq': jax.random.normal(ks[2], (D_MODEL, N_HEADS * D_KV), jnp.float32) * s, 'wk': jax.random.normal(ks[3], (D_MODEL, N_HEADS * D_KV), jnp.float32) * s, 'wv': jax.random.normal(ks[4], (D_MODEL, N_HEADS * D_KV), jnp.float32) * s, 'wo': jax.random.normal(ks[5], (N_HEADS * D_KV, D_MODEL), jnp.float32) * s, 'norm_w': jnp.ones((D_MODEL,), jnp.float32)}
    _L1_xattn_all = _L1_xattn_setup()
    _L1_xattn_in = {k: v for k, v in _L1_xattn_all.items() if k in ('wq', 'wk', 'wv', 'wo', 'norm_w')}
    del _L1_xattn_all

    def _L2_xattn_setup():
        import jax, jax.numpy as jnp
        import numpy as np
        D_MODEL = 128
        N_HEAD = 16
        D_HEAD = D_MODEL // N_HEAD
        D_FF = 4 * D_MODEL
        B, S = (2, 256)
        LN_EPS = 1e-09

        def _layer_norm(x, g, b):
            mu = jnp.mean(x, axis=-1, keepdims=True)
            var = jnp.mean(jnp.square(x - mu), axis=-1, keepdims=True)
            return (x - mu) * jax.lax.rsqrt(var + LN_EPS) * g + b
        key = jax.random.key(seed)
        ks = jax.random.split(key, 16)
        s = 0.02
        inp = {'q': jax.random.normal(ks[0], (B, S, D_MODEL), jnp.float32), 'kv': jax.random.normal(ks[1], (B, S, D_MODEL), jnp.float32), 'w_q': jax.random.normal(ks[2], (D_MODEL, N_HEAD, D_HEAD), jnp.float32) * s, 'w_k': jax.random.normal(ks[3], (D_MODEL, N_HEAD, D_HEAD), jnp.float32) * s, 'w_v': jax.random.normal(ks[4], (D_MODEL, N_HEAD, D_HEAD), jnp.float32) * s, 'w_r': jax.random.normal(ks[5], (D_MODEL, N_HEAD, D_HEAD), jnp.float32) * s, 'r_w_bias': jax.random.normal(ks[6], (N_HEAD, D_HEAD), jnp.float32) * s, 'r_r_bias': jax.random.normal(ks[7], (N_HEAD, D_HEAD), jnp.float32) * s, 'w_o': jax.random.normal(ks[8], (N_HEAD, D_HEAD, D_MODEL), jnp.float32) * s, 'ln1_g': jnp.ones((D_MODEL,), jnp.float32), 'ln1_b': jnp.zeros((D_MODEL,), jnp.float32), 'ffn_w1': jax.random.normal(ks[9], (D_MODEL, D_FF), jnp.float32) * s, 'ffn_b1': jnp.zeros((D_FF,), jnp.float32), 'ffn_w2': jax.random.normal(ks[10], (D_FF, D_MODEL), jnp.float32) * s, 'ffn_b2': jnp.zeros((D_MODEL,), jnp.float32), 'ln2_g': jnp.ones((D_MODEL,), jnp.float32), 'ln2_b': jnp.zeros((D_MODEL,), jnp.float32), 'pos_emb': jax.random.normal(ks[11], (2 * S - 1, D_MODEL), jnp.float32) * s}
        return inp
    _L2_xattn_all = _L2_xattn_setup()
    _L2_xattn_in = {k: v for k, v in _L2_xattn_all.items() if k in ('w_q', 'w_k', 'w_v', 'w_r', 'r_w_bias', 'r_r_bias', 'w_o', 'ln1_g', 'ln1_b', 'ffn_w1', 'ffn_b1', 'ffn_w2', 'ffn_b2', 'ln2_g', 'ln2_b', 'pos_emb')}
    del _L2_xattn_all

    def _L3_xattn_setup():
        import jax, jax.numpy as jnp
        import numpy as np
        D, H, E, K, DFF = (128, 16, 8, 2, 512)
        B, L, T = (4, 64, 256)
        EPS = 1e-05

        def _xavier(key, shape):
            fan_in, fan_out = (shape[-1], shape[-2])
            a = jnp.sqrt(6.0 / (fan_in + fan_out))
            return jax.random.uniform(key, shape, jnp.float32, -a, a)

        def _ln(x, g, b):
            m = x.mean(-1, keepdims=True)
            v = ((x - m) ** 2).mean(-1, keepdims=True)
            return (x - m) / jnp.sqrt(v + EPS) * g + b

        def _mha(q_in, kv_in, in_w, in_b, out_w, out_b):
            wq, wk, wv = jnp.split(in_w, 3, axis=0)
            bq, bk, bv = jnp.split(in_b, 3, axis=0)
            dh = D // H

            def heads(x, w, b):
                y = x @ w.T + b
                return y.reshape(x.shape[0], x.shape[1], H, dh).transpose(0, 2, 1, 3)
            q = heads(q_in, wq, bq)
            k = heads(kv_in, wk, bk)
            v = heads(kv_in, wv, bv)
            scores = jnp.einsum('bhqd,bhkd->bhqk', q, k) / jnp.sqrt(jnp.float32(dh))
            attn = jax.nn.softmax(scores, axis=-1)
            out = jnp.einsum('bhqk,bhkd->bhqd', attn, v)
            out = out.transpose(0, 2, 1, 3).reshape(q_in.shape[0], q_in.shape[1], D)
            return out @ out_w.T + out_b

        def _fuse_moe(x, ln_g, ln_b, rw, rb, fc1_w, fc1_b, fc2_w, fc2_b):
            h = _ln(x, ln_g, ln_b)
            logits = h @ rw.T + rb
            vals, idx = jax.lax.top_k(logits, K)
            gates = jax.nn.softmax(vals, axis=-1)
            N = x.shape[0] * x.shape[1]
            hf = h.reshape(N, D)
            h1 = jax.nn.gelu(jnp.einsum('nd,efd->enf', hf, fc1_w) + fc1_b[:, None, :], approximate=False)
            eo = jnp.einsum('enf,edf->end', h1, fc2_w) + fc2_b[:, None, :]
            idx_f = idx.reshape(N, K)
            gates_f = gates.reshape(N, K)
            gathered = eo[idx_f, jnp.arange(N)[:, None], :]
            mixed = (gathered * gates_f[..., None]).sum(axis=1).reshape(x.shape)
            return x + mixed
        key = jax.random.key(seed)
        ks = jax.random.split(key, 16)
        inp = {'latents': jax.random.normal(ks[0], (B, L, D), jnp.float32), 'tokens': jax.random.normal(ks[1], (B, T, D), jnp.float32), 'sa_ln_g': jnp.ones((D,)), 'sa_ln_b': jnp.zeros((D,)), 'sa_in_w': _xavier(ks[2], (3 * D, D)), 'sa_in_b': jnp.zeros((3 * D,)), 'sa_out_w': _xavier(ks[3], (D, D)), 'sa_out_b': jnp.zeros((D,)), 'ca_q_ln_g': jnp.ones((D,)), 'ca_q_ln_b': jnp.zeros((D,)), 'ca_kv_ln_g': jnp.ones((D,)), 'ca_kv_ln_b': jnp.zeros((D,)), 'ca_in_w': _xavier(ks[4], (3 * D, D)), 'ca_in_b': jnp.zeros((3 * D,)), 'ca_out_w': _xavier(ks[5], (D, D)), 'ca_out_b': jnp.zeros((D,)), 'moe_ln_g': jnp.ones((D,)), 'moe_ln_b': jnp.zeros((D,)), 'router_w': _xavier(ks[6], (E, D)), 'router_b': jnp.zeros((E,)), 'e_fc1_w': jax.vmap(lambda k: _xavier(k, (DFF, D)))(jax.random.split(ks[7], E)), 'e_fc1_b': jnp.zeros((E, DFF)), 'e_fc2_w': jax.vmap(lambda k: _xavier(k, (D, DFF)))(jax.random.split(ks[8], E)), 'e_fc2_b': jnp.zeros((E, D))}
        return inp
    _L3_xattn_all = _L3_xattn_setup()
    _L3_xattn_in = {k: v for k, v in _L3_xattn_all.items() if k in ('sa_ln_g', 'sa_ln_b', 'sa_in_w', 'sa_in_b', 'sa_out_w', 'sa_out_b', 'ca_q_ln_g', 'ca_q_ln_b', 'ca_kv_ln_g', 'ca_kv_ln_b', 'ca_in_w', 'ca_in_b', 'ca_out_w', 'ca_out_b', 'moe_ln_g', 'moe_ln_b', 'router_w', 'router_b', 'e_fc1_w', 'e_fc1_b', 'e_fc2_w', 'e_fc2_b')}
    del _L3_xattn_all
    return {'x': x, 'ctx_1024': ctx_1024, 'mask_1x1xSxS2_ff0': mask_1x1xSxS2_ff0, 'mask_1xSxS2_bk1': mask_1xSxS2_bk1, 'L0_xattn_position_encoding': _L0_xattn_in['position_encoding'], 'L0_xattn_content_bias': _L0_xattn_in['content_bias'], 'L0_xattn_position_bias': _L0_xattn_in['position_bias'], 'L0_xattn_segment_encoding': _L0_xattn_in['segment_encoding'], 'L0_xattn_segment_bias': _L0_xattn_in['segment_bias'], 'L0_xattn_Wq': _L0_xattn_in['Wq'], 'L0_xattn_Wk': _L0_xattn_in['Wk'], 'L0_xattn_Wv': _L0_xattn_in['Wv'], 'L0_xattn_Wr': _L0_xattn_in['Wr'], 'L0_xattn_Wo': _L0_xattn_in['Wo'], 'L0_xattn_ln1_gamma': _L0_xattn_in['ln1_gamma'], 'L0_xattn_ln1_beta': _L0_xattn_in['ln1_beta'], 'L0_xattn_W1': _L0_xattn_in['W1'], 'L0_xattn_b1': _L0_xattn_in['b1'], 'L0_xattn_W2': _L0_xattn_in['W2'], 'L0_xattn_b2': _L0_xattn_in['b2'], 'L0_xattn_ln2_gamma': _L0_xattn_in['ln2_gamma'], 'L0_xattn_ln2_beta': _L0_xattn_in['ln2_beta'], 'L1_xattn_wq': _L1_xattn_in['wq'], 'L1_xattn_wk': _L1_xattn_in['wk'], 'L1_xattn_wv': _L1_xattn_in['wv'], 'L1_xattn_wo': _L1_xattn_in['wo'], 'L1_xattn_norm_w': _L1_xattn_in['norm_w'], 'L2_xattn_w_q': _L2_xattn_in['w_q'], 'L2_xattn_w_k': _L2_xattn_in['w_k'], 'L2_xattn_w_v': _L2_xattn_in['w_v'], 'L2_xattn_w_r': _L2_xattn_in['w_r'], 'L2_xattn_r_w_bias': _L2_xattn_in['r_w_bias'], 'L2_xattn_r_r_bias': _L2_xattn_in['r_r_bias'], 'L2_xattn_w_o': _L2_xattn_in['w_o'], 'L2_xattn_ln1_g': _L2_xattn_in['ln1_g'], 'L2_xattn_ln1_b': _L2_xattn_in['ln1_b'], 'L2_xattn_ffn_w1': _L2_xattn_in['ffn_w1'], 'L2_xattn_ffn_b1': _L2_xattn_in['ffn_b1'], 'L2_xattn_ffn_w2': _L2_xattn_in['ffn_w2'], 'L2_xattn_ffn_b2': _L2_xattn_in['ffn_b2'], 'L2_xattn_ln2_g': _L2_xattn_in['ln2_g'], 'L2_xattn_ln2_b': _L2_xattn_in['ln2_b'], 'L2_xattn_pos_emb': _L2_xattn_in['pos_emb'], 'L3_xattn_sa_ln_g': _L3_xattn_in['sa_ln_g'], 'L3_xattn_sa_ln_b': _L3_xattn_in['sa_ln_b'], 'L3_xattn_sa_in_w': _L3_xattn_in['sa_in_w'], 'L3_xattn_sa_in_b': _L3_xattn_in['sa_in_b'], 'L3_xattn_sa_out_w': _L3_xattn_in['sa_out_w'], 'L3_xattn_sa_out_b': _L3_xattn_in['sa_out_b'], 'L3_xattn_ca_q_ln_g': _L3_xattn_in['ca_q_ln_g'], 'L3_xattn_ca_q_ln_b': _L3_xattn_in['ca_q_ln_b'], 'L3_xattn_ca_kv_ln_g': _L3_xattn_in['ca_kv_ln_g'], 'L3_xattn_ca_kv_ln_b': _L3_xattn_in['ca_kv_ln_b'], 'L3_xattn_ca_in_w': _L3_xattn_in['ca_in_w'], 'L3_xattn_ca_in_b': _L3_xattn_in['ca_in_b'], 'L3_xattn_ca_out_w': _L3_xattn_in['ca_out_w'], 'L3_xattn_ca_out_b': _L3_xattn_in['ca_out_b'], 'L3_xattn_moe_ln_g': _L3_xattn_in['moe_ln_g'], 'L3_xattn_moe_ln_b': _L3_xattn_in['moe_ln_b'], 'L3_xattn_router_w': _L3_xattn_in['router_w'], 'L3_xattn_router_b': _L3_xattn_in['router_b'], 'L3_xattn_e_fc1_w': _L3_xattn_in['e_fc1_w'], 'L3_xattn_e_fc1_b': _L3_xattn_in['e_fc1_b'], 'L3_xattn_e_fc2_w': _L3_xattn_in['e_fc2_w'], 'L3_xattn_e_fc2_b': _L3_xattn_in['e_fc2_b']}

def reference(x, ctx_1024, mask_1x1xSxS2_ff0, mask_1xSxS2_bk1, L0_xattn_position_encoding, L0_xattn_content_bias, L0_xattn_position_bias, L0_xattn_segment_encoding, L0_xattn_segment_bias, L0_xattn_Wq, L0_xattn_Wk, L0_xattn_Wv, L0_xattn_Wr, L0_xattn_Wo, L0_xattn_ln1_gamma, L0_xattn_ln1_beta, L0_xattn_W1, L0_xattn_b1, L0_xattn_W2, L0_xattn_b2, L0_xattn_ln2_gamma, L0_xattn_ln2_beta, L1_xattn_wq, L1_xattn_wk, L1_xattn_wv, L1_xattn_wo, L1_xattn_norm_w, L2_xattn_w_q, L2_xattn_w_k, L2_xattn_w_v, L2_xattn_w_r, L2_xattn_r_w_bias, L2_xattn_r_r_bias, L2_xattn_w_o, L2_xattn_ln1_g, L2_xattn_ln1_b, L2_xattn_ffn_w1, L2_xattn_ffn_b1, L2_xattn_ffn_w2, L2_xattn_ffn_b2, L2_xattn_ln2_g, L2_xattn_ln2_b, L2_xattn_pos_emb, L3_xattn_sa_ln_g, L3_xattn_sa_ln_b, L3_xattn_sa_in_w, L3_xattn_sa_in_b, L3_xattn_sa_out_w, L3_xattn_sa_out_b, L3_xattn_ca_q_ln_g, L3_xattn_ca_q_ln_b, L3_xattn_ca_kv_ln_g, L3_xattn_ca_kv_ln_b, L3_xattn_ca_in_w, L3_xattn_ca_in_b, L3_xattn_ca_out_w, L3_xattn_ca_out_b, L3_xattn_moe_ln_g, L3_xattn_moe_ln_b, L3_xattn_router_w, L3_xattn_router_b, L3_xattn_e_fc1_w, L3_xattn_e_fc1_b, L3_xattn_e_fc2_w, L3_xattn_e_fc2_b):
    import jax
    import jax.numpy as jnp

    def _L0_xattn_ref(content_stream, content_mask, context, position_encoding, content_bias, position_bias, segment_encoding, segment_matrix, segment_bias, Wq, Wk, Wv, Wr, Wo, ln1_gamma, ln1_beta, W1, b1, W2, b2, ln2_gamma, ln2_beta):
        import jax, jax.numpy as jnp
        import numpy as np
        B, Q, C, H, N, D, F = (1, 256, 256, 128, 16, 64, 512)
        R = Q + C
        EPS = 1e-12
        NEG = 1e+30

        def _layernorm(x, g, b):
            m = jnp.mean(x, axis=-1, keepdims=True)
            v = jnp.mean(jnp.square(x - m), axis=-1, keepdims=True)
            return (x - m) * jax.lax.rsqrt(v + EPS) * g + b

        def _rel_shift(x, klen):
            b, n, q, r = x.shape
            x = x.reshape(b, n, r, q)[:, :, 1:, :].reshape(b, n, q, r - 1)
            return x[:, :, :, :klen]
        q = jnp.einsum('bqh,hnd->bqnd', content_stream, Wq)
        k = jnp.einsum('bch,hnd->bcnd', context, Wk)
        v = jnp.einsum('bch,hnd->bcnd', context, Wv)
        r = jnp.einsum('brh,hnd->brnd', position_encoding, Wr)
        ac = jnp.einsum('bqnd,bcnd->bnqc', q + content_bias, k)
        bd = _rel_shift(jnp.einsum('bqnd,brnd->bnqr', q + position_bias, r), k.shape[1])
        ef = jnp.einsum('bqnd,snd->bnqs', q + segment_bias, segment_encoding)
        ef = jnp.where(segment_matrix[:, None], ef[..., 1:], ef[..., :1])
        scores = (ac + bd + ef) / jnp.sqrt(jnp.float32(D))
        scores = scores - NEG * content_mask
        probs = jax.nn.softmax(scores, axis=-1)
        attn = jnp.einsum('bnqc,bcnd->bqnd', probs, v)
        attn_out = jnp.einsum('bqnd,hnd->bqh', attn, Wo)
        ffn_in = _layernorm(attn_out + content_stream, ln1_gamma, ln1_beta)
        ffn_out = jax.nn.relu(ffn_in @ W1 + b1) @ W2 + b2
        return _layernorm(ffn_out + ffn_in, ln2_gamma, ln2_beta)

    def _L1_xattn_ref(hidden_states, key_value_states, wq, wk, wv, wo, norm_w):
        import jax, jax.numpy as jnp
        import numpy as np
        B, Q, KV = (2, 256, 256)
        D_MODEL = 128
        N_HEADS = 16
        D_KV = 64
        EPS = 1e-06
        var = jnp.mean(jnp.square(hidden_states), axis=-1, keepdims=True)
        normed = hidden_states * jax.lax.rsqrt(var + EPS) * norm_w
        b, q_len, _ = hidden_states.shape
        kv_len = key_value_states.shape[1]

        def split_heads(x):
            return x.reshape(b, -1, N_HEADS, D_KV).transpose(0, 2, 1, 3)
        q = split_heads(normed @ wq)
        k = split_heads(key_value_states @ wk)
        v = split_heads(key_value_states @ wv)
        scores = jnp.einsum('bhqd,bhkd->bhqk', q, k)
        attn = jax.nn.softmax(scores.astype(jnp.float32), axis=-1).astype(scores.dtype)
        ctx = jnp.einsum('bhqk,bhkd->bhqd', attn, v)
        ctx = ctx.transpose(0, 2, 1, 3).reshape(b, q_len, N_HEADS * D_KV)
        attn_out = ctx @ wo
        return hidden_states + attn_out

    def _L2_xattn_ref(q, kv, w_q, w_k, w_v, w_r, r_w_bias, r_r_bias, w_o, ln1_g, ln1_b, ffn_w1, ffn_b1, ffn_w2, ffn_b2, ln2_g, ln2_b, pos_emb):
        import jax, jax.numpy as jnp
        import numpy as np
        D_MODEL = 128
        N_HEAD = 16
        D_HEAD = D_MODEL // N_HEAD
        D_FF = 4 * D_MODEL
        B, S = (2, 256)
        LN_EPS = 1e-09

        def _layer_norm(x, g, b):
            mu = jnp.mean(x, axis=-1, keepdims=True)
            var = jnp.mean(jnp.square(x - mu), axis=-1, keepdims=True)
            return (x - mu) * jax.lax.rsqrt(var + LN_EPS) * g + b
        Bq, Q, _ = q.shape
        K = kv.shape[1]
        scale = 1.0 / jnp.sqrt(jnp.asarray(D_HEAD, q.dtype))
        q_head = jnp.einsum('bqd,dhe->bqhe', q, w_q)
        k_head = jnp.einsum('bkd,dhe->bkhe', kv, w_k)
        v_head = jnp.einsum('bkd,dhe->bkhe', kv, w_v)
        content = jnp.einsum('bqhe,bkhe->bhqk', q_head + r_w_bias, k_head)
        r_head = jnp.einsum('rd,dhe->rhe', pos_emb, w_r)
        pos = jnp.einsum('bqhe,rhe->bhqr', q_head + r_r_bias, r_head)
        rel_idx = jnp.arange(K)[None, :] - jnp.arange(Q)[:, None] + (K - 1)
        pos_shift = jnp.take_along_axis(pos, rel_idx[None, None], axis=3)
        attn = jax.nn.softmax((content + pos_shift) * scale, axis=-1)
        ctx = jnp.einsum('bhqk,bkhe->bqhe', attn, v_head)
        attn_out = jnp.einsum('bqhe,hed->bqd', ctx, w_o)
        h = _layer_norm(q + attn_out, ln1_g, ln1_b)
        u = jax.nn.gelu(h @ ffn_w1 + ffn_b1)
        y = u @ ffn_w2 + ffn_b2
        return _layer_norm(h + y, ln2_g, ln2_b)

    def _L3_xattn_ref(latents, tokens, sa_ln_g, sa_ln_b, sa_in_w, sa_in_b, sa_out_w, sa_out_b, ca_q_ln_g, ca_q_ln_b, ca_kv_ln_g, ca_kv_ln_b, ca_in_w, ca_in_b, ca_out_w, ca_out_b, moe_ln_g, moe_ln_b, router_w, router_b, e_fc1_w, e_fc1_b, e_fc2_w, e_fc2_b):
        import jax, jax.numpy as jnp
        import numpy as np
        D, H, E, K, DFF = (128, 16, 8, 2, 512)
        B, L, T = (4, 64, 256)
        EPS = 1e-05

        def _xavier(key, shape):
            fan_in, fan_out = (shape[-1], shape[-2])
            a = jnp.sqrt(6.0 / (fan_in + fan_out))
            return jax.random.uniform(key, shape, jnp.float32, -a, a)

        def _ln(x, g, b):
            m = x.mean(-1, keepdims=True)
            v = ((x - m) ** 2).mean(-1, keepdims=True)
            return (x - m) / jnp.sqrt(v + EPS) * g + b

        def _mha(q_in, kv_in, in_w, in_b, out_w, out_b):
            wq, wk, wv = jnp.split(in_w, 3, axis=0)
            bq, bk, bv = jnp.split(in_b, 3, axis=0)
            dh = D // H

            def heads(x, w, b):
                y = x @ w.T + b
                return y.reshape(x.shape[0], x.shape[1], H, dh).transpose(0, 2, 1, 3)
            q = heads(q_in, wq, bq)
            k = heads(kv_in, wk, bk)
            v = heads(kv_in, wv, bv)
            scores = jnp.einsum('bhqd,bhkd->bhqk', q, k) / jnp.sqrt(jnp.float32(dh))
            attn = jax.nn.softmax(scores, axis=-1)
            out = jnp.einsum('bhqk,bhkd->bhqd', attn, v)
            out = out.transpose(0, 2, 1, 3).reshape(q_in.shape[0], q_in.shape[1], D)
            return out @ out_w.T + out_b

        def _fuse_moe(x, ln_g, ln_b, rw, rb, fc1_w, fc1_b, fc2_w, fc2_b):
            h = _ln(x, ln_g, ln_b)
            logits = h @ rw.T + rb
            vals, idx = jax.lax.top_k(logits, K)
            gates = jax.nn.softmax(vals, axis=-1)
            N = x.shape[0] * x.shape[1]
            hf = h.reshape(N, D)
            h1 = jax.nn.gelu(jnp.einsum('nd,efd->enf', hf, fc1_w) + fc1_b[:, None, :], approximate=False)
            eo = jnp.einsum('enf,edf->end', h1, fc2_w) + fc2_b[:, None, :]
            idx_f = idx.reshape(N, K)
            gates_f = gates.reshape(N, K)
            gathered = eo[idx_f, jnp.arange(N)[:, None], :]
            mixed = (gathered * gates_f[..., None]).sum(axis=1).reshape(x.shape)
            return x + mixed
        q = _ln(latents, sa_ln_g, sa_ln_b)
        x = latents + _mha(q, q, sa_in_w, sa_in_b, sa_out_w, sa_out_b)
        qc = _ln(x, ca_q_ln_g, ca_q_ln_b)
        kv = _ln(tokens, ca_kv_ln_g, ca_kv_ln_b)
        x = x + _mha(qc, kv, ca_in_w, ca_in_b, ca_out_w, ca_out_b)
        return _fuse_moe(x, moe_ln_g, moe_ln_b, router_w, router_b, e_fc1_w, e_fc1_b, e_fc2_w, e_fc2_b)
    x = _L0_xattn_ref(x, mask_1x1xSxS2_ff0, ctx_1024, L0_xattn_position_encoding, L0_xattn_content_bias, L0_xattn_position_bias, L0_xattn_segment_encoding, mask_1xSxS2_bk1, L0_xattn_segment_bias, L0_xattn_Wq, L0_xattn_Wk, L0_xattn_Wv, L0_xattn_Wr, L0_xattn_Wo, L0_xattn_ln1_gamma, L0_xattn_ln1_beta, L0_xattn_W1, L0_xattn_b1, L0_xattn_W2, L0_xattn_b2, L0_xattn_ln2_gamma, L0_xattn_ln2_beta)
    x = _L1_xattn_ref(x, ctx_1024, L1_xattn_wq, L1_xattn_wk, L1_xattn_wv, L1_xattn_wo, L1_xattn_norm_w)
    x = _L2_xattn_ref(x, ctx_1024, L2_xattn_w_q, L2_xattn_w_k, L2_xattn_w_v, L2_xattn_w_r, L2_xattn_r_w_bias, L2_xattn_r_r_bias, L2_xattn_w_o, L2_xattn_ln1_g, L2_xattn_ln1_b, L2_xattn_ffn_w1, L2_xattn_ffn_b1, L2_xattn_ffn_w2, L2_xattn_ffn_b2, L2_xattn_ln2_g, L2_xattn_ln2_b, L2_xattn_pos_emb)
    x = _L3_xattn_ref(x, ctx_1024, L3_xattn_sa_ln_g, L3_xattn_sa_ln_b, L3_xattn_sa_in_w, L3_xattn_sa_in_b, L3_xattn_sa_out_w, L3_xattn_sa_out_b, L3_xattn_ca_q_ln_g, L3_xattn_ca_q_ln_b, L3_xattn_ca_kv_ln_g, L3_xattn_ca_kv_ln_b, L3_xattn_ca_in_w, L3_xattn_ca_in_b, L3_xattn_ca_out_w, L3_xattn_ca_out_b, L3_xattn_moe_ln_g, L3_xattn_moe_ln_b, L3_xattn_router_w, L3_xattn_router_b, L3_xattn_e_fc1_w, L3_xattn_e_fc1_b, L3_xattn_e_fc2_w, L3_xattn_e_fc2_b)
    return x

_drawn_inputs = setup_inputs


def setup_inputs(seed=0):
    import zlib

    import numpy as np

    out = dict(_drawn_inputs(seed))
    spreads = {'L0_xattn_ln1_gamma': (1.0, 0.2),
     'L0_xattn_ln1_beta': (0.0, 0.1),
     'L0_xattn_b1': (0.0, 0.1),
     'L0_xattn_b2': (0.0, 0.1),
     'L0_xattn_ln2_gamma': (1.0, 0.2),
     'L0_xattn_ln2_beta': (0.0, 0.1),
     'L1_xattn_norm_w': (1.0, 0.6),
     'L2_xattn_ln1_g': (1.0, 0.2),
     'L2_xattn_ln1_b': (0.0, 0.1),
     'L2_xattn_ffn_b1': (0.0, 0.1),
     'L2_xattn_ffn_b2': (0.0, 0.1),
     'L2_xattn_ln2_g': (1.0, 0.2),
     'L2_xattn_ln2_b': (0.0, 0.1),
     'L3_xattn_sa_ln_g': (1.0, 0.2),
     'L3_xattn_sa_ln_b': (0.0, 0.1),
     'L3_xattn_sa_in_b': (0.0, 0.1),
     'L3_xattn_sa_out_b': (0.0, 0.1),
     'L3_xattn_ca_q_ln_g': (1.0, 0.2),
     'L3_xattn_ca_q_ln_b': (0.0, 0.397),
     'L3_xattn_ca_kv_ln_g': (1.0, 0.2),
     'L3_xattn_ca_kv_ln_b': (0.0, 0.1),
     'L3_xattn_ca_in_b': (0.0, 0.1),
     'L3_xattn_ca_out_b': (0.0, 0.1),
     'L3_xattn_moe_ln_g': (1.0, 0.2),
     'L3_xattn_moe_ln_b': (0.0, 0.1),
     'L3_xattn_router_b': (0.0, 0.1),
     'L3_xattn_e_fc1_b': (0.0, 0.1),
     'L3_xattn_e_fc2_b': (0.0, 0.1)}
    factors = {'L0_xattn_position_encoding': 8.0,
     'L0_xattn_content_bias': 35.72,
     'L0_xattn_position_bias': 8.0,
     'L0_xattn_segment_encoding': 186.764,
     'L0_xattn_segment_bias': 200.0,
     'L0_xattn_Wq': 6.755,
     'L0_xattn_Wk': 7.961,
     'L0_xattn_Wr': 8.0,
     'L2_xattn_w_q': 8.0,
     'L2_xattn_w_k': 8.0,
     'L2_xattn_w_r': 26.6,
     'L2_xattn_r_w_bias': 37.415,
     'L2_xattn_r_r_bias': 64.0,
     'L2_xattn_pos_emb': 25.239}
    for name, (base, spread) in spreads.items():
        noise = np.random.default_rng([zlib.crc32(name.encode()), seed]).standard_normal(out[name].shape)
        drawn = base * np.exp(spread * noise) if base else spread * noise
        out[name] = jnp.asarray(drawn.astype(out[name].dtype))
    for name, factor in factors.items():
        out[name] = (out[name] * factor).astype(out[name].dtype)
    return out
```

```python
from contextlib import ExitStack

import concourse.bass as bass
import numpy as np
from concourse import mybir

ALU = mybir.AluOpType
ACT = mybir.ActivationFunctionType
F32 = mybir.dt.float32
U8 = mybir.dt.uint8
U32 = mybir.dt.uint32
AX_X = mybir.AxisListType.X

P = 128
S2 = 77
H = 16
G = 4
QUAD = 4
FF = 4
E = 8
ROW = 1280
ROW0 = 8
WIN = S2 + 1
RP = 205
NEG = 1e30
NB = 4


class Signal:

    def __init__(self, handle, per_turn):
        self.sem, self.per_turn, self.made = handle, per_turn, 0

    def at(self, turn, k):
        assert k <= self.per_turn
        return turn * self.per_turn + max(k, 0)


class Phase:

    def __init__(self, nc, name):
        self.nc, self.name, self.stack, self.sems = nc, name, ExitStack(), []

    def sbuf(self, name, shape, dtype=F32):
        return self.stack.enter_context(self.nc.sbuf_tensor(f"{self.name}_{name}", shape, dtype))

    def psum(self, name):
        return self.stack.enter_context(self.nc.psum_tensor(f"{self.name}_{name}", [P, 512], F32))

    def sem(self, name):
        s = self.nc.alloc_semaphore(f"{self.name}_{name}")
        self.sems.append(s)
        return s

    def counter(self, name, per_turn):
        return Signal(self.sem(name), per_turn)

    def close(self):
        self.stack.close()
        self.nc.clear_and_free_semaphores(self.sems)
        self.nc.all_engine_barrier()


def over(ap, axis, n):
    u = ap.unsqueeze(axis)
    shape = list(u.shape)
    shape[axis] = n
    return u.broadcast_to(shape)


def make_identity(nc, pool, ident, zeroed, made):
    nc.gpsimd.memset(ident[:], 0.0).then_inc(zeroed, 1)
    pool.wait_ge(zeroed, 1)
    nc.gpsimd.affine_select(out=ident[:], in_=ident[:], compare_op=ALU.not_equal, fill=1.0, base=0,
                            pattern=[[-1, P]], channel_multiplier=1).then_inc(made, 1)


class Steps:

    def __init__(self, eng, count, turn):
        self.eng, self.count, self.turn, self.k = eng, count, turn, 0

    def __call__(self, ins):
        self.k += 1
        ins.then_inc(self.count.sem, 1)
        self.eng.wait_ge(self.count.sem, self.count.at(self.turn, self.k))

    def end(self):
        assert self.k == self.count.per_turn, (self.k, self.count.per_turn)


def attention_phase(nc, name, turns, x_in, x_out, w, *, dim, keys, ctxT=None, ctx=None, pos=None,
                    pre=None, kv_bias=False, post=None, scale=1.0, segments=None):
    big = dim == 64
    NQ = 8 if big else 1
    W = 2 * keys if big else G * keys
    GK = G * keys
    self_kv = ctxT is None and ctx is None
    ph = Phase(nc, name)
    sb = ph.sbuf

    ident = sb("ident", [P, P])
    halfs = sb("halfs", [P, QUAD])
    wq = sb("wq", [P, NQ * P])
    wk = sb("wk", [P, NQ * P])
    wv = sb("wv", [P, NQ * P])
    wo = sb("wo", [P, (NQ if big else G) * P])
    bq = sb("bq", [P, NQ]) if "bq" in w else None
    bk = sb("bk", [P, NQ]) if "bk" in w else None
    bv = sb("bv", [P, P]) if "bv" in w else None
    bo = sb("bo", [P, P]) if "bo" in w else None
    xs = sb("xs", [P, 1]) if "xs" in w else None
    xb = sb("xb", [P, 1]) if "xb" in w else None
    cs = sb("cs", [P, 1]) if "cs" in w else None
    cb = sb("cb", [P, 1]) if "cb" in w else None
    own = None if big else sb("own", [P, H])
    if post:
        w1 = sb("w1", [P, FF * P])
        b1 = sb("b1", [P, FF])
        w2 = sb("w2", [P, FF, P])
        rows = sb("rows", [P, 5, P])
    if segments:
        seg_w = sb("seg_w", [P, H])
        seg_c = sb("seg_c", [P, H])
        seg_m8 = sb("seg_m8", [P, S2], U8)
        seg_m = sb("seg_m", [P, S2])
        neg_m = sb("neg_m", [P, S2])

    x_raw = sb("x_raw", [P, QUAD, P])
    x_res = sb("x_res", [P, QUAD, P])
    x_nrm = sb("x_nrm", [P, QUAD, P]) if pre else x_res
    x_sq = sb("x_sq", [P, QUAD, P])
    stat = sb("stat", [P, 8, QUAD])
    xT = sb("xT", [P, QUAD * P])
    if ctx is not None:
        c_raw = sb("c_raw", [keys, QUAD, P])
        c_nrm = sb("c_nrm", [keys, QUAD, P])
        kvT = sb("kvT", [P, QUAD * keys])
    elif self_kv:
        kvT = xT
    else:
        kvT = sb("kvT", [P, QUAD * keys])
    qT = sb("qT", [P, NQ, QUAD * P])
    if big:
        k_bd = sb("k_bd", [P, NQ, QUAD, 2 * keys])
        v_sb = sb("v_sb", [keys, QUAD, NQ * P])
        VW = dim
    else:
        kT = sb("kT", [P, QUAD, keys])
        k_bd = sb("k_bd", [P, 2, H, keys])
        v_sb = sb("v_sb", [keys, QUAD, H, 32])
        VW = 32
    if pos is not None:
        p_sb = sb("p_sb", [P, 2, H * WIN])
    if segments:
        seg_d = sb("seg_d", [P, QUAD, H])
        seg_t = sb("seg_t", [P, H, S2])
    sc = sb("sc", [P, NB, GK])
    ex = sb("ex", [P, NB, GK])
    pr = sb("pr", [P, NB, GK])
    mx = sb("mx", [P, NB, G])
    sm = sb("sm", [P, NB, G])
    rc = sb("rc", [P, NB, G])
    pT = sb("pT", [keys, 2, G * P])
    oT = sb("oT", [P, 2, 2 * P if big else P])
    h = sb("h", [P, QUAD, P])
    y = sb("y", [P, QUAD, P]) if post else None
    x_new = sb("x_new", [P, QUAD, P]) if post else h
    if post:
        yT = sb("yT", [P, QUAD * P])
        u = sb("u", [P, FF, QUAD * P])
    OC = 2 if big else 1

    psS = [ph.psum("psS0"), ph.psum("psS1")]
    psT = [ph.psum("psT0"), ph.psum("psT1")]
    psO = [ph.psum("psO0"), ph.psum("psO1")]
    psA = ph.psum("psA")
    psM = ph.psum("psM")

    UN = 4 * QUAD
    zeroed = ph.sem("zeroed")
    consts = ph.sem("consts_made")
    w_in = ph.sem("weights_loaded")
    m_done = ph.sem("mask_terms_made")
    apart = ph.sem("apart")
    x_in_s = ph.counter("x_loaded", 16)
    c_in_s = ph.counter("ctx_loaded", 16)
    pos_in = [ph.counter(f"pos_loaded{i}", 16 * 2) for i in range(2)]
    kept = ph.counter("x_kept", 1)
    NS = {"ln": 7, "rms": 4, None: 0}[pre] + (7 if ctx is not None else 0)
    steps = ph.counter("vector_steps", NS + (21 if post else 1 if bo is None else 2))
    powers = ph.counter("inverse_roots", (1 if pre else 0) + (1 if ctx is not None else 0) + (2 if post else 0))
    normed = ph.counter("x_normed", 1)
    c_normed = ph.counter("ctx_normed", 1)
    turned = ph.counter("transposed", 1 + (1 if ctx is not None else 0) + (1 if segments else 0) + (1 if post else 0))
    turned_out = ph.counter("transposed_copied", 1 + (1 if ctx is not None else 0) + (1 if post else 0))
    seg_out = ph.counter("segment_coefficients", 1)
    seg_inner = ph.counter("segment_steps", 2 * QUAD)
    seg_used = ph.counter("segments_added", QUAD)
    NA = NQ + (2 * QUAD if big else 0)
    NV = NQ + (0 if big else 1)
    proj_a = ph.counter("projection_a", NA)
    proj_a_out = ph.counter("projection_a_copied", NA)
    proj_v = ph.counter("projection_v", NV)
    proj_v_out = ph.counter("projection_v_copied", NV)
    k_made = ph.counter("keys_spread", QUAD)
    scored = ph.counter("scores", UN)
    shifted = ph.counter("scores_less_maximum", UN)
    inner = ph.counter("softmax_steps", UN * (2 if pos is not None else 1))
    exped = ph.counter("exponentials", UN)
    summed = ph.counter("sums_inverted", UN)
    probs = ph.counter("probabilities", UN)
    p_turned = ph.counter("probabilities_transposed", UN)
    p_copied = ph.counter("probabilities_copied", UN)
    headed = ph.counter("head_outputs", UN)
    h_copied = ph.counter("head_outputs_copied", UN)
    woed = ph.counter("output_products", UN)
    ffn1 = ph.counter("ff_hidden", FF)
    ffn1_out = ph.counter("ff_activated", FF)
    ffn2 = ph.counter("ff_out", 1)
    a_read = ph.counter("psA_read", 2 if post else 1)
    res_used = ph.counter("residual_added", 1)
    normed_y = ph.counter("y_normed", 1)
    summing = ph.counter("sums", UN)
    done = ph.counter("turn_done", 1)
    x_stored = ph.counter("x_stored", 16)

    loads = [(wq, w["wq"]), (wk, w["wk"]), (wv, w["wv"]), (wo, w["wo"])]
    for t, n in ((bq, "bq"), (bk, "bk"), (bv, "bv"), (bo, "bo"), (xs, "xs"), (xb, "xb"), (cs, "cs"), (cb, "cb"),
                 (own, "own")):
        if t is not None:
            loads.append((t, w[n]))
    if post:
        loads += [(w1, w["w1"]), (b1, w["b1"]), (w2, w["w2"])]
        loads += [(rows[:, i, :], w[n]) for i, n in enumerate(("g1", "be1", "b2", "g2", "be2"))]
    if segments:
        loads += [(seg_w, w["seg_w"]), (seg_c, w["seg_c"]), (seg_m8, w["seg_m"]), (neg_m, w["neg_m"])]
    CONSTS = 2 + (1 if big else 1)

    with nc.Block() as block:

        @block.sync
        def _(sp):
            for t, src in loads:
                sp.dma_start(t if isinstance(t, bass.AP) else t[:], src).then_inc(w_in, 16)

            def load(t, first=False):
                if not first:
                    sp.wait_ge(kept.sem, kept.at(t, 0))
                sp.dma_start(x_raw[:], x_in[bass.ds(t * QUAD, QUAD)].rearrange("b p d -> p b d")).then_inc(x_in_s.sem, 16)
                if ctx is not None:
                    if not first:
                        sp.wait_ge(turned.sem, turned.at(t - 1, 1))
                    sp.dma_start(c_raw[:], ctx[bass.ds(t * QUAD, QUAD)].rearrange("b p d -> p b d")).then_inc(c_in_s.sem, 16)
                elif ctxT is not None:
                    if not first:
                        sp.wait_ge(proj_a.sem, proj_a.at(t, 0))
                        sp.sem_inc(apart, 1)
                        sp.wait_ge(proj_v.sem, proj_v.at(t, 0))
                        sp.sem_inc(apart, 1)
                    sp.dma_start(kvT[:].rearrange("p (b k) -> p b k", b=QUAD),
                                 ctxT[bass.ds(t * QUAD, QUAD)].rearrange("b p k -> p b k")).then_inc(c_in_s.sem, 16)

            def load_pos(t, b):
                sp.wait_ge(shifted.sem, shifted.at(t, 4 * (b - 1)))
                sp.dma_start(p_sb[:, b % 2, 0:H * WIN - 1],
                             pos[bass.ds(t * QUAD + b, 1), :, ROW0:ROW0 + H * WIN - 1].rearrange("b p n -> p (b n)")
                             ).then_inc(pos_in[b % 2].sem, 16)

            def turn(t, last=False):
                if pos is not None:
                    load_pos(t, 0)
                    load_pos(t, 1)
                if not last:
                    load(t + 1)
                if pos is not None:
                    load_pos(t, 2)
                    load_pos(t, 3)
                sp.wait_ge(done.sem, done.at(t, 1))
                sp.dma_start(x_out[bass.ds(t * QUAD, QUAD)].rearrange("b p d -> p b d"), x_new[:]
                             ).then_inc(x_stored.sem, 16)

            load(0, first=True)
            with sp.Fori(0, turns - 1) as t:
                turn(t)
            turn(turns - 1, last=True)
            sp.wait_ge(x_stored.sem, 16 * turns)

        @block.gpsimd
        def _(pool):
            make_identity(nc, pool, ident, zeroed, consts)
            nc.gpsimd.memset(halfs[:], -0.5).then_inc(consts, 1)
            nc.gpsimd.memset(k_bd[:] if big else v_sb[:], 0.0).then_inc(consts, 1)
            pool.wait_ge(w_in, 16 * len(loads))
            if segments:
                pool.wait_ge(m_done, 2)
            with pool.Fori(0, turns) as t:
                n = 0

                def power(of, to):
                    nonlocal n
                    n += 1
                    nc.gpsimd.tensor_tensor(to, of, halfs[0:of.shape[0], :], ALU.pow).then_inc(powers.sem, 1)

                base = 0
                if ctx is not None:
                    pool.wait_ge(steps.sem, steps.at(t, 6))
                    power(stat[0:keys, 3, :], stat[0:keys, 4, :])
                    base = 7
                if pre:
                    pool.wait_ge(steps.sem, steps.at(t, base + (6 if pre == "ln" else 3)))
                    power(stat[:, 1, :], stat[:, 2, :])

                def spread(b):
                    pool.wait_ge(proj_v_out.sem, proj_v_out.at(t, 1))
                    if b >= 2:
                        pool.wait_ge(scored.sem, scored.at(t, 4 * (b - 1)))
                    else:
                        pool.wait_ge(scored.sem, scored.at(t, 0))
                    nc.gpsimd.tensor_tensor(k_bd[:, b % 2, :, :], over(kT[:, b, :], 1, H),
                                            over(own[:], 2, keys), ALU.mult).then_inc(k_made.sem, 1)

                def add_segments(b):
                    pool.wait_ge(pos_in[b % 2].sem, pos_in[b % 2].at(t, 16 * (b // 2 + 1)))
                    if b == 0:
                        pool.wait_ge(seg_out.sem, seg_out.at(t, 1))
                    pv = p_sb[:, b % 2, :].rearrange("p (n j) -> p n j", n=H)[:, :, 0:S2]
                    pool.wait_ge(seg_used.sem, seg_used.at(t, b))
                    nc.gpsimd.tensor_tensor(seg_t[:], over(seg_m[:], 1, H), over(seg_d[:, b, :], 2, S2), ALU.mult
                                            ).then_inc(seg_inner.sem, 1)
                    pool.wait_ge(seg_inner.sem, seg_inner.at(t, 2 * b + 1))
                    nc.gpsimd.tensor_tensor(seg_t[:], seg_t[:], over(neg_m[:], 1, H), ALU.add).then_inc(seg_inner.sem, 1)
                    pool.wait_ge(seg_inner.sem, seg_inner.at(t, 2 * b + 2))
                    nc.gpsimd.tensor_tensor(pv, pv, seg_t[:], ALU.add).then_inc(seg_used.sem, 1)

                if not big:
                    spread(0)
                    spread(1)
                if segments:
                    add_segments(0)
                for i in range(UN):
                    b = i // 4
                    if segments and i % 4 == 1 and b + 1 < QUAD:
                        add_segments(b + 1)
                    if not big and i % 4 == 1 and 1 <= b < QUAD - 1:
                        spread(b + 1)
                    pool.wait_ge(summed.sem, summed.at(t, i + 1))
                    pool.wait_ge(p_turned.sem, p_turned.at(t, i + 1 - NB))
                    nc.gpsimd.tensor_tensor(pr[:, i % NB, :].rearrange("p (h k) -> p h k", h=G),
                                            ex[:, i % NB, :].rearrange("p (h k) -> p h k", h=G),
                                            over(rc[:, i % NB, :], 2, keys), ALU.mult).then_inc(probs.sem, 1)
                if post:
                    pool.wait_ge(steps.sem, steps.at(t, NS + 7))
                    power(stat[:, 1, :], stat[:, 2, :])
                    pool.wait_ge(steps.sem, steps.at(t, NS + 18))
                    power(stat[:, 1, :], stat[:, 2, :])

        @block.scalar
        def _(act):
            act.wait_ge(w_in, 16 * len(loads))
            with act.Fori(0, turns) as t:
                act.wait_ge(x_in_s.sem, x_in_s.at(t, 16))
                act.wait_ge(res_used.sem, res_used.at(t, 0))
                nc.scalar.activation(x_res[:], x_raw[:], ACT.Copy).then_inc(kept.sem, 1)
                k = 0
                if ctx is not None:
                    k += 1
                    act.wait_ge(turned.sem, turned.at(t, k))
                    act.wait_ge(proj_a.sem, proj_a.at(t, 0))
                    act.wait_ge(proj_v.sem, proj_v.at(t, 0))
                    nc.scalar.activation(kvT[:], psM[:, 0:QUAD * keys], ACT.Identity, bias=cb[:, 0:1],
                                         scale=cs[:, 0:1]).then_inc(turned_out.sem, 1)
                k += 1
                act.wait_ge(turned.sem, turned.at(t, k))
                act.wait_ge(proj_a.sem, proj_a.at(t, 0))
                if self_kv:
                    act.wait_ge(proj_v.sem, proj_v.at(t, 0))
                nc.scalar.activation(xT[:], psM[:], ACT.Identity, bias=xb[:, 0:1] if xb is not None else 0.0,
                                     scale=xs[:, 0:1] if xs is not None else 1.0).then_inc(turned_out.sem, 1)
                for m in range(NQ):
                    act.wait_ge(proj_a.sem, proj_a.at(t, m + 1))
                    act.wait_ge(scored.sem, scored.at(t, 0))
                    nc.scalar.activation(qT[:, m, :], psO[m % 2][:], ACT.Identity,
                                         bias=bq[:, m:m + 1] if bq is not None else 0.0).then_inc(proj_a_out.sem, 1)
                if big:
                    for j in range(2 * QUAD):
                        act.wait_ge(proj_a.sem, proj_a.at(t, NQ + j + 1))
                        act.wait_ge(headed.sem, headed.at(t, 0))
                        nc.scalar.activation(v_sb[:, j // 2, (j % 2) * 512:(j % 2) * 512 + 512],
                                             psO[j % 2][0:keys, :], ACT.Identity).then_inc(proj_a_out.sem, 1)

                def copy_probs(i):
                    act.wait_ge(p_turned.sem, p_turned.at(t, i + 1))
                    act.wait_ge(headed.sem, headed.at(t, i - 1))
                    nc.scalar.activation(pT[:, i % 2, :], psT[i % 2][0:keys, :], ACT.Copy).then_inc(p_copied.sem, 1)

                def copy_heads(i):
                    act.wait_ge(headed.sem, headed.at(t, i + 1))
                    act.wait_ge(woed.sem, woed.at(t, i - 1))
                    nc.scalar.activation(oT[:, i % 2, :], psO[i % 2][:, 0:OC * P], ACT.Copy).then_inc(h_copied.sem, 1)

                for i in range(UN + 3):
                    if i < UN:
                        act.wait_ge(shifted.sem, shifted.at(t, i + 1))
                        act.wait_ge(probs.sem, probs.at(t, i + 1 - NB))
                        nc.scalar.activation(ex[:, i % NB, :], sc[:, i % NB, :], ACT.Exp, scale=scale).then_inc(exped.sem, 1)
                    if 2 <= i < UN + 2:
                        copy_probs(i - 2)
                    if i >= 3:
                        copy_heads(i - 3)
                if post:
                    act.wait_ge(turned.sem, turned.at(t, turned.per_turn))
                    nc.scalar.activation(yT[:], psM[:], ACT.Copy).then_inc(turned_out.sem, 1)
                    for f in range(FF):
                        act.wait_ge(ffn1.sem, ffn1.at(t, f + 1))
                        nc.scalar.activation(u[:, f, :], (psS + psT)[f][:], post, bias=b1[:, f:f + 1]
                                             ).then_inc(ffn1_out.sem, 1)

        @block.tensor
        def _(pe):
            pe.wait_ge(w_in, 16 * len(loads))
            pe.wait_ge(consts, CONSTS)
            with pe.Fori(0, turns) as t:
                k = 0
                if ctx is not None:
                    k += 1
                    pe.wait_ge(c_normed.sem, c_normed.at(t, 1))
                    pe.wait_ge(turned_out.sem, turned_out.at(t, 0))
                    for b in range(QUAD):
                        mm = pe.transpose(psM[:, b * keys:(b + 1) * keys], c_nrm[:, b, :], ident[0:keys, 0:keys])
                    mm.then_inc(turned.sem, 1)
                pe.wait_ge((normed if pre else kept).sem, kept.at(t, 1))
                pe.wait_ge(turned_out.sem, turned_out.at(t, k))
                if segments:
                    pe.wait_ge(seg_out.sem, seg_out.at(t, 0))
                for b in range(QUAD):
                    mm = pe.transpose(psM[:, b * P:(b + 1) * P], x_nrm[:, b, :], ident[:])
                mm.then_inc(turned.sem, 1)
                k += 1
                pe.wait_ge(turned_out.sem, turned_out.at(t, k))
                if ctxT is not None:
                    pe.wait_ge(c_in_s.sem, c_in_s.at(t, 16))

                if segments:
                    for b in range(QUAD):
                        mm = pe.matmul(psM[:, b * H:(b + 1) * H], xT[:, b * P:(b + 1) * P], seg_w[:], start=True, stop=True)
                    mm.then_inc(turned.sem, 1)

                def k_job(m):
                    pe.wait_ge(p_copied.sem, p_copied.at(t, 0))
                    if post:
                        pe.wait_ge(ffn1_out.sem, ffn1_out.at(t, 0))
                    pe.wait_ge(proj_v_out.sem, proj_v_out.at(t, m - 1))
                    pe.matmul(psT[m % 2][:, 0:QUAD * keys], wk[:, m * P:(m + 1) * P], kvT[:], start=True, stop=True
                              ).then_inc(proj_v.sem, 1)

                for m in range(NQ):
                    pe.wait_ge(h_copied.sem, h_copied.at(t, 0))
                    pe.wait_ge(proj_a_out.sem, proj_a_out.at(t, m - 1))
                    pe.matmul(psO[m % 2][:], wq[:, m * P:(m + 1) * P], xT[:], start=True, stop=True).then_inc(proj_a.sem, 1)
                    k_job(m)
                if big:
                    for j in range(2 * QUAD):
                        b = j // 2
                        pe.wait_ge(proj_a_out.sem, proj_a_out.at(t, NQ + j - 1))
                        pe.matmul(psO[j % 2][0:keys, :], kvT[:, b * keys:(b + 1) * keys],
                                  wv[:, (j % 2) * 512:(j % 2) * 512 + 512], start=True, stop=True).then_inc(proj_a.sem, 1)
                else:
                    for b in range(QUAD):
                        mm = pe.matmul(psT[1][0:keys, b * P:(b + 1) * P], kvT[:, b * keys:(b + 1) * keys], wv[:],
                                       start=True, stop=True)
                    mm.then_inc(proj_v.sem, 1)

                def scores(i):
                    b, g = i // 4, i % 4
                    if i == 0:
                        pe.wait_ge(proj_a_out.sem, proj_a_out.at(t, NA))
                        pe.wait_ge(proj_v_out.sem, proj_v_out.at(t, NV))
                    if not big and g == 0:
                        pe.wait_ge(k_made.sem, k_made.at(t, b + 1))
                    pe.wait_ge(shifted.sem, shifted.at(t, i - 1))
                    for j in range(2 if big else 1):
                        m = 2 * g + j if big else 0
                        mm = pe.matmul(psS[i % 2][:, j * W:(j + 1) * W], qT[:, m, b * P:(b + 1) * P],
                                       k_bd[:, m, b, :] if big else k_bd[:, b % 2, G * g:G * (g + 1), :],
                                       start=True, stop=True)
                    mm.then_inc(scored.sem, 1)

                def turn_probs(i):
                    pe.wait_ge(probs.sem, probs.at(t, i + 1))
                    pe.wait_ge(p_copied.sem, p_copied.at(t, i - 1))
                    for c in range(G):
                        mm = pe.transpose(psT[i % 2][0:keys, c * P:(c + 1) * P], pr[:, i % NB, c * keys:(c + 1) * keys], ident[:])
                    mm.then_inc(p_turned.sem, 1)

                def heads(i):
                    b, g = i // 4, i % 4
                    pe.wait_ge(p_copied.sem, p_copied.at(t, i + 1))
                    pe.wait_ge(h_copied.sem, h_copied.at(t, i - 1))
                    for c in range(G):
                        n = G * g + c
                        if big:
                            mm = pe.matmul(psO[i % 2][(c % 2) * 64:(c % 2) * 64 + 64, (c // 2) * P:(c // 2 + 1) * P],
                                           v_sb[:, b, n * 64:(n + 1) * 64], pT[:, i % 2, c * P:(c + 1) * P],
                                           start=True, stop=True)
                        else:
                            mm = pe.matmul(psO[i % 2][32 * c:32 * c + 32, 0:P], v_sb[:, b, n, :],
                                           pT[:, i % 2, c * P:(c + 1) * P], start=True, stop=True)
                    mm.then_inc(headed.sem, 1)

                def out_product(i):
                    b, g = i // 4, i % 4
                    pe.wait_ge(h_copied.sem, h_copied.at(t, i + 1))
                    if i == 0:
                        pe.wait_ge(a_read.sem, a_read.at(t, 0))
                    for j in range(OC):
                        m = OC * g + j
                        mm = pe.matmul(psA[:, b * P:(b + 1) * P], oT[:, i % 2, j * P:(j + 1) * P],
                                       wo[:, m * P:(m + 1) * P], start=(m == 0), stop=(m == OC * G - 1))
                    mm.then_inc(woed.sem, 1)

                for i in range(UN + 4):
                    if i < UN:
                        scores(i)
                    if 2 <= i < UN + 2:
                        turn_probs(i - 2)
                    if 3 <= i < UN + 3:
                        heads(i - 3)
                    if i >= 4:
                        out_product(i - 4)
                if post:
                    pe.wait_ge(normed_y.sem, normed_y.at(t, 1))
                    for b in range(QUAD):
                        mm = pe.transpose(psM[:, b * P:(b + 1) * P], y[:, b, :], ident[:])
                    mm.then_inc(turned.sem, 1)
                    pe.wait_ge(turned_out.sem, turned_out.at(t, turned_out.per_turn))
                    for f in range(FF):
                        if f == 0:
                            pe.wait_ge(shifted.sem, shifted.at(t, UN))
                            pe.wait_ge(p_copied.sem, p_copied.at(t, UN))
                        pe.matmul((psS + psT)[f][:], w1[:, f * P:(f + 1) * P], yT[:], start=True, stop=True
                                  ).then_inc(ffn1.sem, 1)
                    pe.wait_ge(ffn1_out.sem, ffn1_out.at(t, FF))
                    pe.wait_ge(a_read.sem, a_read.at(t, 1))
                    for b in range(QUAD):
                        for f in range(FF):
                            mm = pe.matmul(psA[:, b * P:(b + 1) * P], u[:, f, b * P:(b + 1) * P], w2[:, f, :],
                                           start=(f == 0), stop=(f == FF - 1))
                    mm.then_inc(ffn2.sem, 1)

        @block.vector
        def _(dve):
            v = nc.vector
            dve.wait_ge(w_in, 16 * len(loads))
            dve.wait_ge(consts, CONSTS)
            if segments:
                v.tensor_copy(seg_m[:], seg_m8[:]).then_inc(m_done, 1)
                v.tensor_scalar(neg_m[:], neg_m[:], -NEG / scale, None, ALU.mult).then_inc(m_done, 1)
            with dve.Fori(0, turns) as t:
                step = Steps(dve, steps, t)

                def stats(src, st, sq, eps, r, xc, mean=True, squares=None):
                    p = src.shape[0]
                    if mean:
                        step(v.reduce_sum(st[0:p, 0, :], src, AX_X))
                        step(v.tensor_scalar(st[0:p, 0, :], st[0:p, 0, :], 1.0 / P, None, ALU.mult))
                        step(v.tensor_tensor(xc, src, over(st[0:p, 0, :], 2, P), ALU.subtract))
                        src = xc
                    step(v.tensor_tensor(sq, src, src, ALU.mult))
                    step(v.reduce_sum(st[0:p, r, :], sq, AX_X))
                    step(v.tensor_scalar(st[0:p, r, :], st[0:p, r, :], 1.0 / P, eps, ALU.mult, ALU.add))

                pw = 0
                if ctx is not None:
                    dve.wait_ge(c_in_s.sem, c_in_s.at(t, 16))
                    dve.wait_ge(turned.sem, turned.at(t, 0))
                    stats(c_raw[:], stat, x_sq[0:keys], w["ceps"], 3, c_nrm[:])
                    pw += 1
                    dve.wait_ge(powers.sem, powers.at(t, pw))
                    step(v.tensor_tensor(c_nrm[:], c_nrm[:], over(stat[0:keys, 4, :], 2, P), ALU.mult))
                    dve.sem_inc(c_normed.sem, 1)
                if pre:
                    dve.wait_ge(kept.sem, kept.at(t, 1))
                    dve.wait_ge(turned.sem, turned.at(t, 1 if ctx is not None else 0))
                    stats(x_res[:], stat, x_sq[:], w["eps"], 1, x_nrm[:], mean=pre == "ln")
                    pw += 1
                    dve.wait_ge(powers.sem, powers.at(t, pw))
                    step(v.tensor_tensor(x_nrm[:], (x_nrm if pre == "ln" else x_res)[:], over(stat[:, 2, :], 2, P), ALU.mult))
                    dve.sem_inc(normed.sem, 1)
                if segments:
                    dve.wait_ge(turned.sem, turned.at(t, 2))
                    dve.wait_ge(seg_used.sem, seg_used.at(t, 0))
                    v.tensor_tensor(seg_d[:], psM[:, 0:QUAD * H].rearrange("p (b n) -> p b n", b=QUAD),
                                    over(seg_c[:], 1, QUAD), ALU.add).then_inc(seg_out.sem, 1)
                if big:
                    for m in range(NQ):
                        dve.wait_ge(proj_v.sem, proj_v.at(t, m + 1))
                        dve.wait_ge(scored.sem, scored.at(t, 0))
                        for hf in range(2):
                            lo = slice(hf * 64, hf * 64 + 64)
                            src = psT[m % 2][lo, 0:QUAD * keys].rearrange("p (b k) -> p b k", b=QUAD)
                            dst = k_bd[lo, m, :, hf * keys:(hf + 1) * keys]
                            ins = (v.tensor_scalar(dst, src, bk[lo, m:m + 1], None, ALU.add) if bk is not None
                                   else v.tensor_copy(dst, src))
                        ins.then_inc(proj_v_out.sem, 1)
                else:
                    dve.wait_ge(proj_v.sem, proj_v.at(t, 1))
                    dve.wait_ge(k_made.sem, k_made.at(t, 0))
                    src = psT[0][:, 0:QUAD * keys].rearrange("p (b k) -> p b k", b=QUAD)
                    (v.tensor_scalar(kT[:], src, bk[:, 0:1], None, ALU.add) if bk is not None
                     else v.tensor_copy(kT[:], src)).then_inc(proj_v_out.sem, 1)
                    dve.wait_ge(proj_v.sem, proj_v.at(t, 2))
                    dve.wait_ge(headed.sem, headed.at(t, 0))
                    src = psT[1][0:keys, :].rearrange("p (b h e) -> p b h e", b=QUAD, h=H)
                    dst = v_sb[:, :, :, 0:8]
                    (v.tensor_tensor(dst, src, over(bv[0:keys, :].rearrange("p (h e) -> p h e", h=H), 1, QUAD), ALU.add)
                     if bv is not None else v.tensor_copy(dst, src)).then_inc(proj_v_out.sem, 1)

                def soft(i):
                    b, g = i // 4, i % 4
                    s = i % NB
                    nin = 2 if pos is not None else 1
                    sv = sc[:, s, :].rearrange("p (h k) -> p h k", h=G)
                    src = psS[i % 2][:, 0:GK].rearrange("p (h k) -> p h k", h=G)
                    dve.wait_ge(scored.sem, scored.at(t, i + 1))
                    dve.wait_ge(exped.sem, exped.at(t, i + 1 - NB))
                    q = i * nin
                    if pos is not None:
                        if segments:
                            dve.wait_ge(seg_used.sem, seg_used.at(t, b + 1))
                        else:
                            dve.wait_ge(pos_in[b % 2].sem, pos_in[b % 2].at(t, 16 * (b // 2 + 1)))
                        v.tensor_tensor(sv, src, p_sb[:, b % 2, G * g * WIN:G * (g + 1) * WIN].rearrange(
                            "p (h k) -> p h k", h=G)[:, :, 0:S2], ALU.add).then_inc(inner.sem, 1)
                        q += 1
                        dve.wait_ge(inner.sem, inner.at(t, q))
                        src = sv
                    v.reduce_max(mx[:, s, :], src, AX_X).then_inc(inner.sem, 1)
                    q += 1
                    dve.wait_ge(inner.sem, inner.at(t, q))
                    v.tensor_tensor(sv, src, over(mx[:, s, :], 2, keys), ALU.subtract).then_inc(shifted.sem, 1)

                def sums(i):
                    s = i % NB
                    nin = 2 if pos is not None else 1
                    dve.wait_ge(exped.sem, exped.at(t, i + 1))
                    dve.wait_ge(probs.sem, probs.at(t, i + 1 - NB))
                    v.reduce_sum(sm[:, s, :], ex[:, s, :].rearrange("p (h k) -> p h k", h=G), AX_X).then_inc(summing.sem, 1)
                    dve.wait_ge(summing.sem, summing.at(t, i + 1))
                    v.reciprocal(rc[:, s, :], sm[:, s, :]).then_inc(summed.sem, 1)

                for i in range(UN + 1):
                    if i < UN:
                        soft(i)
                    if i >= 1:
                        sums(i - 1)

                dve.wait_ge(woed.sem, woed.at(t, UN))
                dve.wait_ge(x_stored.sem, x_stored.at(t, 0))
                pa = psA[:].rearrange("p (b d) -> p b d", b=QUAD)
                if not post:
                    if bo is None:
                        step(v.tensor_tensor(h[:], pa, x_res[:], ALU.add))
                    else:
                        step(v.tensor_tensor(h[:], pa, x_res[:], ALU.add))
                        step(v.tensor_tensor(h[:], h[:], over(bo[:], 1, QUAD), ALU.add))
                    dve.sem_inc(a_read.sem, 1)
                    dve.sem_inc(res_used.sem, 1)
                    dve.sem_inc(done.sem, 1)
                else:
                    step(v.tensor_tensor(h[:], pa, x_res[:], ALU.add))
                    dve.sem_inc(a_read.sem, 1)
                    dve.sem_inc(res_used.sem, 1)
                    stats(h[:], stat, x_sq[:], w["eps1"], 1, h[:])
                    pw += 1
                    dve.wait_ge(powers.sem, powers.at(t, pw))
                    step(v.tensor_tensor(y[:], h[:], over(stat[:, 2, :], 2, P), ALU.mult))
                    step(v.tensor_tensor(y[:], y[:], over(rows[:, 0, :], 1, QUAD), ALU.mult))
                    step(v.tensor_tensor(y[:], y[:], over(rows[:, 1, :], 1, QUAD), ALU.add))
                    dve.sem_inc(normed_y.sem, 1)
                    dve.wait_ge(turned.sem, turned.at(t, turned.per_turn))
                    step(v.tensor_tensor(y[:], y[:], over(rows[:, 2, :], 1, QUAD), ALU.add))
                    dve.wait_ge(ffn2.sem, ffn2.at(t, 1))
                    step(v.tensor_tensor(h[:], pa, y[:], ALU.add))
                    dve.sem_inc(a_read.sem, 1)
                    stats(h[:], stat, x_sq[:], w["eps2"], 1, h[:])
                    pw += 1
                    dve.wait_ge(powers.sem, powers.at(t, pw))
                    step(v.tensor_tensor(x_new[:], h[:], over(stat[:, 2, :], 2, P), ALU.mult))
                    step(v.tensor_tensor(x_new[:], x_new[:], over(rows[:, 3, :], 1, QUAD), ALU.mult))
                    step(v.tensor_tensor(x_new[:], x_new[:], over(rows[:, 4, :], 1, QUAD), ALU.add))
                    dve.sem_inc(done.sem, 1)
                step.end()
    ph.close()


def position_phase(nc, name, batches, x_in, pos_out, w, *, big, first, seg_out=None):
    R2 = 2 * batches
    pairs = P // 2
    NQ = 8 if big else 1
    NO = 2 if big else H
    SPLIT = [(0, 6), (6, 11), (11, 16)]
    ph = Phase(nc, name)
    sb = ph.sbuf
    ident = sb("ident", [P, P])
    wr = sb("wr", [P, NQ * P])
    wqT = sb("wqT", [P, NQ, P])
    peT = sb("peT", [P, RP])
    cols = sb("cols", [P, 5, NQ])
    own = sb("own", [P, NO])
    ones = sb("ones", [P, P])
    rT = sb("rT", [P, NQ, RP])
    r_own = sb("r_own", [P, 2, RP])
    b_rep = sb("b_rep", [P, 2, P])
    e_rep = sb("e_rep", [P, 2, P])
    s_own = sb("s_own", [P, 2, RP])
    win = sb("win", [P, H, RP])
    cst = sb("cst", [P, H, RP])
    if seg_out:
        dcols = sb("dcols", [P, 2, NQ])
        d_own = sb("d_own", [P, H])
        segs = sb("segs", [P, 2, H])
        s_rep = sb("s_rep", [P, NQ, P])
    xi = sb("xi", [P, 2, P])
    xiT = sb("xiT", [P, 2, P])
    stage = sb("stage", [P, 2, H, WIN])
    ps = [[ph.psum(f"ps{s}{c}") for c in range(3)] for s in range(2)]
    psX = [ph.psum(f"psX{s}") for s in range(2)]

    zeroed, made, w_in = ph.sem("zeroed"), ph.sem("identity_made"), ph.sem("weights_loaded")
    r_done, r_copied = ph.sem("r_projected"), ph.sem("r_copied")
    pre_v = ph.sem("constants_prepared")
    win_done, win_copied = ph.sem("windows_done"), ph.sem("windows_copied")
    cst_copied = ph.sem("constants_copied")
    seg_done, seg_copied, seg_stored = ph.sem("segments_done"), ph.sem("segments_copied"), ph.sem("segments_stored")
    apart_v, apart_p = ph.sem("apart_vector"), ph.sem("apart_tensor")
    x_loaded = [ph.counter(f"x_loaded{s}", 32) for s in range(2)]
    turned = ph.counter("x_transposed", 2)
    copied = ph.counter("x_copied", 2)
    multiplied = ph.counter("products", 2)
    staged = ph.counter("rows_staged", 2)
    stored = [ph.counter(f"rows_stored{s}", 32) for s in range(2)]

    loads = [(wr[:], w["wr"]), (wqT[:], w["wqT"]), (peT[:], w["peT"]), (own[:], w["own"])]
    loads += [(cols[:, i, :], w[n]) for i, n in enumerate(("pb", "sb", "cb", "se0", "se1")) if n in w]
    turns = pairs // 2
    extra = "sb" in w
    DC = 4 if extra else 1

    with nc.Block() as block:

        @block.gpsimd
        def _(pool):
            make_identity(nc, pool, ident, zeroed, made)
            nc.gpsimd.memset(ones[:], 1.0).then_inc(made, 1)

        @block.sync
        def _(sp):
            for t, src in loads:
                sp.dma_start(t, src).then_inc(w_in, 16)
            if seg_out:
                sp.wait_ge(seg_copied, 1)
                sp.dma_start(seg_out[0], segs[:, 0, :]).then_inc(seg_stored, 16)
                sp.dma_start(seg_out[1], segs[:, 1, :]).then_inc(seg_stored, 16)
                sp.wait_ge(seg_stored, 32)
            with sp.Fori(0, turns) as t:
                for s in range(2):
                    sp.wait_ge(staged.sem, staged.at(t, s + 1))
                    for i in range(2):
                        at = ROW0 - 1 + i
                        sp.dma_start(pos_out[:, bass.ds(t * 4 + 2 * s + i, 1), at:at + H * WIN].rearrange("b i n -> b (i n)"),
                                     stage[batches * i:batches * (i + 1), s, :, :].rearrange("p n j -> p (n j)")
                                     ).then_inc(stored[s].sem, 16)
            for s in range(2):
                sp.wait_ge(stored[s].sem, 32 * turns)

        @block.scalar
        def _(act):
            for m in range(NQ):
                act.wait_ge(r_done, m + 1)
                nc.scalar.activation(rT[:, m, :], psX[m % 2][:, 0:RP], ACT.Copy).then_inc(r_copied, 1)
            for n in range(H):
                act.wait_ge(win_done, n + 1)
                nc.scalar.activation(win[:, n, :], ps[n % 2][0][:, 0:RP], ACT.Copy).then_inc(win_copied, 1)
            if seg_out:
                act.wait_ge(seg_done, 1)
                nc.scalar.activation(segs[:].rearrange("p a n -> p (a n)"), psX[0][:, 0:2 * H], ACT.Copy).then_inc(seg_copied, 1)

            def load(t, s):
                for i in range(2):
                    act.dma_start(xi[batches * i:batches * (i + 1), s, :],
                                  x_in[:, bass.ds(t * 4 + 2 * s + i, 1), :].rearrange("b i d -> b (i d)")
                                  ).then_inc(x_loaded[s].sem, 16)

            def turn(t, last=False):
                for s in range(2):
                    act.wait_ge(turned.sem, turned.at(t, s + 1))
                    if not last:
                        load(t + 1, s)
                    act.wait_ge(multiplied.sem, multiplied.at(t, s - 1))
                    nc.scalar.activation(xiT[:, s, 0:R2], psX[s][:, 0:R2], ACT.Copy).then_inc(copied.sem, 1)

            load(0, 0)
            load(0, 1)
            with act.Fori(0, turns - 1) as t:
                turn(t)
            turn(turns - 1, last=True)

        @block.vector
        def _(dve):
            v = nc.vector
            dve.wait_ge(w_in, 16 * len(loads))
            dve.wait_ge(made, 2)
            done = 0
            if extra:
                v.tensor_tensor(cols[:, 2, :], cols[:, 1, :], cols[:, 2, :], ALU.subtract).then_inc(pre_v, 1)
                v.tensor_tensor(dcols[:, 0, :], cols[:, 4, :], cols[:, 3, :], ALU.subtract).then_inc(pre_v, 1)
                dve.wait_ge(pre_v, 2)
                v.tensor_tensor(s_rep[:], over(ones[:], 1, NQ), over(cols[:, 1, :], 2, P), ALU.mult).then_inc(pre_v, 1)
                done = 3
                for n in range(H):
                    m, o = n // NO, n % NO
                    v.tensor_tensor(d_own[:, n:n + 1], dcols[:, 0, m:m + 1], own[:, o:o + 1], ALU.mult).then_inc(pre_v, 1)
                    done += 1
            for n in range(H):
                m, o = n // NO, n % NO
                dve.wait_ge(r_copied, m + 1)
                if n >= 2:
                    dve.wait_ge(win_done, n - 1)
                v.tensor_scalar(r_own[:, n % 2, :], rT[:, m, :], own[:, o:o + 1], None, ALU.mult).then_inc(pre_v, 1)
                v.tensor_scalar(b_rep[:, n % 2, :], ones[:], cols[:, 0, m:m + 1], None, ALU.mult).then_inc(pre_v, 1)
                done += 2
                if extra:
                    v.tensor_scalar(e_rep[:, n % 2, :], ones[:], cols[:, 2, m:m + 1], None, ALU.mult).then_inc(pre_v, 1)
                    v.tensor_tensor(s_own[:, n % 2, :], over(cols[:, 3, m], 1, RP), over(own[:, o], 1, RP), ALU.mult
                                    ).then_inc(pre_v, 1)
                    done += 2
                if n >= 1:
                    dve.wait_ge(win_done, n)
                    v.tensor_copy(cst[:, n - 1, :], ps[(n - 1) % 2][1][:, 0:RP]).then_inc(cst_copied, 1)
            dve.wait_ge(win_done, H)
            v.tensor_copy(cst[:, H - 1, :], ps[(H - 1) % 2][1][:, 0:RP]).then_inc(cst_copied, 1)
            dve.wait_ge(cst_copied, H)
            with dve.Fori(0, turns) as t:
                for s in range(2):
                    dve.wait_ge(multiplied.sem, multiplied.at(t, s + 1))
                    dve.wait_ge(stored[s].sem, stored[s].at(t, 0))
                    dve.sem_inc(apart_v, 1)
                    for c, (a, b) in enumerate(SPLIT):
                        ins = v.tensor_tensor(
                            stage[0:R2, s, a:b, :], ps[s][c][0:R2, 0:(b - a) * WIN].rearrange("p (n j) -> p n j", n=b - a),
                            cst[0:R2, a:b, bass.ds(first - 2 * s - t * 4, WIN)], ALU.add)
                    ins.then_inc(staged.sem, 1)

        @block.tensor
        def _(pe):
            pe.wait_ge(w_in, 16 * len(loads))
            pe.wait_ge(made, 2)
            for m in range(NQ):
                if m >= 2:
                    pe.wait_ge(r_copied, m - 1)
                pe.matmul(psX[m % 2][:, 0:RP], wr[:, m * P:(m + 1) * P], peT[:], start=True, stop=True).then_inc(r_done, 1)
            pre = 3 + H if extra else 0
            for n in range(H):
                m = n // NO
                pe.wait_ge(pre_v, pre + (4 if extra else 2) * (n + 1))
                if n >= 2:
                    pe.wait_ge(win_copied, n - 1)
                    pe.wait_ge(cst_copied, n - 1)
                pe.matmul(ps[n % 2][0][:, 0:RP], wqT[:, m, :], r_own[:, n % 2, :], start=True, stop=True)
                mm = pe.matmul(ps[n % 2][1][:, 0:RP], b_rep[:, n % 2, :], r_own[:, n % 2, :], start=True, stop=not extra)
                if extra:
                    mm = pe.matmul(ps[n % 2][1][:, 0:RP], e_rep[:, n % 2, :], s_own[:, n % 2, :], start=False, stop=True)
                mm.then_inc(win_done, 1)
            if seg_out:
                pe.wait_ge(r_copied, NQ)
                for n in range(H):
                    m = n // NO
                    pe.matmul(psX[0][:, n:n + 1], wqT[:, m, :], d_own[:, n:n + 1], start=True, stop=True)
                    mm = pe.matmul(psX[0][:, H + n:H + n + 1], s_rep[:, m, :], d_own[:, n:n + 1], start=True, stop=True)
                mm.then_inc(seg_done, 1)
            pe.wait_ge(win_copied, H)
            pe.wait_ge(cst_copied, H)
            if seg_out:
                pe.wait_ge(seg_copied, 1)
            with pe.Fori(0, turns) as t:
                for s in range(2):
                    pe.wait_ge(x_loaded[s].sem, x_loaded[s].at(t, 32))
                    pe.wait_ge(copied.sem, copied.at(t, s - 1))
                    pe.transpose(psX[s][:, 0:R2], xi[0:R2, s, :], ident[0:R2, 0:R2]).then_inc(turned.sem, 1)
                for s in range(2):
                    pe.wait_ge(copied.sem, copied.at(t, s + 1))
                    pe.wait_ge(staged.sem, staged.at(t, s - 1))
                    pe.sem_inc(apart_p, 1)
                    for c, (a, b) in enumerate(SPLIT):
                        mm = pe.matmul(ps[s][c][0:R2, 0:(b - a) * WIN], xiT[:, s, 0:R2],
                                       win[:, a:b, bass.ds(first - 2 * s - t * 4, WIN)], start=True, stop=True)
                    mm.then_inc(multiplied.sem, 1)
    ph.close()


def experts_phase(nc, name, turns, x_in, x_out, w):
    ph = Phase(nc, name)
    sb = ph.sbuf
    ident = sb("ident", [P, P])
    halfs = sb("halfs", [P, QUAD])
    number = sb("number", [P, E])
    rw = sb("rw", [P, E])
    rb = sb("rb", [P, E])
    xs = sb("xs", [P, 1])
    xb = sb("xb", [P, 1])
    w1 = sb("w1", [P, E, FF * P])
    b1 = sb("b1", [P, E, FF])
    w2 = sb("w2", [P, E, FF * P])
    b2 = sb("b2", [P, E, P])
    x_raw = sb("x_raw", [P, 2, QUAD, P])
    xc = sb("xc", [P, QUAD, P])
    sq = sb("sq", [P, QUAD, P])
    stat = sb("stat", [P, 3, QUAD])
    hT = sb("hT", [P, QUAD * P])
    logit = sb("logit", [P, QUAD, E])
    best = sb("best", [P, QUAD, 8])
    at_u = sb("at_u", [P, QUAD, 8], U32)
    at_f = sb("at_f", [P, QUAD, 8])
    e2 = sb("e2", [P, 5, QUAD])
    pick = sb("pick", [P, 2, QUAD, E])
    gate = sb("gate", [P, QUAD, E])
    u = sb("u", [P, 2, FF, QUAD * P])
    t_sb = sb("t_sb", [P, 2, QUAD, P])
    acc = sb("acc", [P, QUAD, P])
    ps1 = [ph.psum(f"ps1{i}") for i in range(4)]
    ps2 = [ph.psum(f"ps2{i}") for i in range(2)]
    psM = ph.psum("psM")
    psL = ph.psum("psL")

    zeroed, made, w_in = ph.sem("zeroed"), ph.sem("constants_made"), ph.sem("weights_loaded")
    apart = ph.sem("apart")
    x_loaded = ph.counter("x_loaded", 16)
    STEPS = 20
    steps = ph.counter("vector_steps", STEPS)
    powers = ph.counter("inverse_roots", 1)
    turned = ph.counter("transposed", 1)
    copied = ph.counter("transposed_copied", 1)
    logits = ph.counter("logits", 1)
    gap = ph.counter("logit_gap", 1)
    gap_exp = ph.counter("logit_gap_exponential", 1)
    hidden = ph.counter("hidden", E * FF)
    active = ph.counter("activated", E * FF)
    outs = ph.counter("expert_outputs", E)
    taken = ph.counter("expert_outputs_taken", E)
    mixed = ph.counter("outputs_mixed", E)
    stored = ph.counter("x_stored", 16)
    loads = [(rw[:], w["rw"]), (rb[:], w["rb"]), (xs[:], w["xs"]), (xb[:], w["xb"]), (b1[:], w["b1"]),
             (w1[:], w["w1"]), (w2[:], w["w2"]), (b2[:], w["b2"])]

    with nc.Block() as block:

        @block.gpsimd
        def _(pool):
            make_identity(nc, pool, ident, zeroed, made)
            nc.gpsimd.memset(halfs[:], -0.5).then_inc(made, 1)
            for e in range(E):
                ins = nc.gpsimd.memset(number[:, e:e + 1], float(e))
            ins.then_inc(made, 1)
            with pool.Fori(0, turns) as t:
                pool.wait_ge(steps.sem, steps.at(t, 6))
                nc.gpsimd.tensor_tensor(stat[:, 2, :], stat[:, 1, :], halfs[:], ALU.pow).then_inc(powers.sem, 1)

        @block.sync
        def _(sp):
            for t, src in loads:
                sp.dma_start(t, src).then_inc(w_in, 16)
            with sp.Fori(0, turns) as t:
                sp.wait_ge(stored.sem, stored.at(t, 0))
                sp.dma_start(x_raw[:, 0], x_in[bass.ds(t * QUAD, QUAD)].rearrange("b p d -> p b d")).then_inc(x_loaded.sem, 16)
                sp.wait_ge(mixed.sem, mixed.at(t, E))
                sp.dma_start(x_out[bass.ds(t * QUAD, QUAD)].rearrange("b p d -> p b d"), acc[:]).then_inc(stored.sem, 16)
            sp.wait_ge(stored.sem, 16 * turns)

        @block.scalar
        def _(act):
            act.wait_ge(w_in, 16 * len(loads))
            with act.Fori(0, turns) as t:
                act.wait_ge(turned.sem, turned.at(t, 1))
                act.wait_ge(hidden.sem, hidden.at(t, 0))
                nc.scalar.activation(hT[:], psM[:], ACT.Identity, bias=xb[:, 0:1], scale=xs[:, 0:1]).then_inc(copied.sem, 1)
                act.wait_ge(gap.sem, gap.at(t, 1))
                nc.scalar.activation(e2[:, 1, :], e2[:, 0, :], ACT.Exp).then_inc(gap_exp.sem, 1)
                for e in range(E):
                    for f in range(FF):
                        act.wait_ge(hidden.sem, hidden.at(t, e * FF + f + 1))
                        act.wait_ge(outs.sem, outs.at(t, e - 1))
                        nc.scalar.activation(u[:, e % 2, f, :], ps1[f][:], ACT.Gelu, bias=b1[:, e, f:f + 1]
                                             ).then_inc(active.sem, 1)

        @block.tensor
        def _(pe):
            pe.wait_ge(w_in, 16 * len(loads))
            pe.wait_ge(made, 3)
            with pe.Fori(0, turns) as t:
                pe.wait_ge(steps.sem, steps.at(t, 7))
                pe.wait_ge(copied.sem, copied.at(t, 0))
                for b in range(QUAD):
                    mm = pe.transpose(psM[:, b * P:(b + 1) * P], xc[:, b, :], ident[:])
                mm.then_inc(turned.sem, 1)
                pe.wait_ge(copied.sem, copied.at(t, 1))
                for b in range(QUAD):
                    mm = pe.matmul(psL[:, b * E:(b + 1) * E], hT[:, b * P:(b + 1) * P], rw[:], start=True, stop=True)
                mm.then_inc(logits.sem, 1)

                def first_layer(e):
                    for f in range(FF):
                        pe.wait_ge(active.sem, active.at(t, (e - 1) * FF + f + 1))
                        pe.matmul(ps1[f][:], w1[:, e, f * P:(f + 1) * P], hT[:], start=True, stop=True
                                  ).then_inc(hidden.sem, 1)

                def second_layer(e):
                    pe.wait_ge(active.sem, active.at(t, (e + 1) * FF))
                    pe.wait_ge(taken.sem, taken.at(t, e - 1))
                    for b in range(QUAD):
                        for f in range(FF):
                            mm = pe.matmul(ps2[e % 2][:, b * P:(b + 1) * P], u[:, e % 2, f, b * P:(b + 1) * P],
                                           w2[:, e, f * P:(f + 1) * P], start=(f == 0), stop=(f == FF - 1))
                    mm.then_inc(outs.sem, 1)

                first_layer(0)
                for e in range(E):
                    if e + 1 < E:
                        first_layer(e + 1)
                    second_layer(e)

        @block.vector
        def _(dve):
            v = nc.vector
            dve.wait_ge(w_in, 16 * len(loads))
            dve.wait_ge(made, 3)
            with dve.Fori(0, turns) as t:
                step = Steps(dve, steps, t)
                dve.wait_ge(x_loaded.sem, x_loaded.at(t, 16))
                dve.wait_ge(turned.sem, turned.at(t, 0))
                x = x_raw[:, 0]
                step(v.reduce_sum(stat[:, 0, :], x, AX_X))
                step(v.tensor_scalar(stat[:, 0, :], stat[:, 0, :], 1.0 / P, None, ALU.mult))
                step(v.tensor_tensor(xc[:], x, over(stat[:, 0, :], 2, P), ALU.subtract))
                step(v.tensor_tensor(sq[:], xc[:], xc[:], ALU.mult))
                step(v.reduce_sum(stat[:, 1, :], sq[:], AX_X))
                step(v.tensor_scalar(stat[:, 1, :], stat[:, 1, :], 1.0 / P, w["eps"], ALU.mult, ALU.add))
                dve.wait_ge(powers.sem, powers.at(t, 1))
                step(v.tensor_tensor(xc[:], xc[:], over(stat[:, 2, :], 2, P), ALU.mult))
                dve.wait_ge(logits.sem, logits.at(t, 1))
                step(v.tensor_tensor(logit[:], psL[:, 0:QUAD * E].rearrange("p (b e) -> p b e", b=QUAD),
                                     over(rb[:], 1, QUAD), ALU.add))
                dve.sem_inc(apart, 1)
                for b in range(QUAD):
                    ins = v.max(best[:, b, :], logit[:, b, :])
                step(ins)
                dve.sem_inc(apart, 1)
                for b in range(QUAD):
                    ins = v.max_index(at_u[:, b, :], best[:, b, :], logit[:, b, :])
                step(ins)
                step(v.tensor_copy(at_f[:], at_u[:]))
                dve.wait_ge(gap_exp.sem, gap_exp.at(t, 0))
                v.tensor_tensor(e2[:, 0, :], best[:, :, 1], best[:, :, 0], ALU.subtract).then_inc(gap.sem, 1)
                dve.wait_ge(gap_exp.sem, gap_exp.at(t, 1))
                step(v.tensor_scalar(e2[:, 2, :], e2[:, 1, :], 1.0, None, ALU.add))
                step(v.reciprocal(e2[:, 3, :], e2[:, 2, :]))
                step(v.tensor_tensor(e2[:, 4, :], e2[:, 3, :], e2[:, 1, :], ALU.mult))
                for i in range(2):
                    step(v.tensor_tensor(pick[:, i], over(at_f[:, :, i], 2, E), over(number[:], 1, QUAD), ALU.is_equal))
                    step(v.tensor_tensor(pick[:, i], pick[:, i], over(e2[:, 3 + i, :], 2, E), ALU.mult))
                step(v.tensor_tensor(gate[:], pick[:, 0], pick[:, 1], ALU.add))
                dve.wait_ge(stored.sem, stored.at(t, 0))
                step(v.tensor_copy(acc[:], x))
                for e in range(E):
                    dve.wait_ge(outs.sem, outs.at(t, e + 1))
                    v.tensor_tensor(t_sb[:, e % 2], ps2[e % 2][:].rearrange("p (b d) -> p b d", b=QUAD),
                                    over(b2[:, e, :], 1, QUAD), ALU.add).then_inc(taken.sem, 1)
                    dve.wait_ge(taken.sem, taken.at(t, e + 1))
                    dve.wait_ge(mixed.sem, mixed.at(t, e))
                    for b in range(QUAD):
                        ins = v.scalar_tensor_tensor(out=acc[:, b, :], in0=t_sb[:, e % 2, b, :], scalar=gate[:, b, e:e + 1],
                                                     in1=acc[:, b, :], op0=ALU.mult, op1=ALU.add)
                    ins.then_inc(mixed.sem, 1)
                step.n = None
                assert step.k == STEPS, step.k
    ph.close()


def build(nc, a, out, turns=16, layers=9):
    B = turns * QUAD
    x = [nc.dram_tensor(f"x_{i}", [B, P, P], F32, kind="Internal").ap() for i in range(6)]
    pos = nc.dram_tensor("shifted_scores", [B, P, ROW], F32, kind="Internal").ap()
    seg = nc.dram_tensor("segment_terms", [2, P, H], F32, kind="Internal").ap()
    row = lambda name: a[name].rearrange("(o d) -> o d", o=1).broadcast_to([P, a[name].shape[0]])
    col = lambda name: a[name].rearrange("(d o) -> d o", o=1)
    ctxT = a["ctxT"]
    dst = lambda i: out if i == layers else x[i]

    position_phase(nc, "pos0", B, a["x"], pos, dict(
        wr=a["L0_Wr"], wqT=a["L0_WqT"], peT=a["L0_peT"], own=a["own64"], pb=a["L0_pb"], sb=a["L0_sb"],
        cb=a["L0_cb"], se0=a["L0_se0"], se1=a["L0_se1"]), big=True, first=P - 1, seg_out=seg)
    attention_phase(nc, "att0", turns, a["x"], out if layers == 0 else x[0], dict(
        wq=a["L0_Wq"], wk=a["L0_Wk"], wv=a["L0_Wv"], wo=a["L0_Wo"], bq=a["L0_cb"], bk=a["L0_se0"],
        w1=a["L0_W1"], b1=a["L0_b1"], w2=a["L0_W2"], g1=row("L0_g1"), be1=row("L0_be1"), b2=row("L0_b2"),
        g2=row("L0_g2"), be2=row("L0_be2"), eps1=1e-12, eps2=1e-12,
        seg_w=seg[0], seg_c=seg[1], seg_m=a["seg_mask"], neg_m=a["mask"]),
        dim=64, keys=S2, ctxT=ctxT, pos=pos, post=ACT.Relu, scale=0.125, segments=True)
    if layers == 0:
        return
    attention_phase(nc, "att1", turns, x[0], out if layers == 1 else x[1], dict(
        wq=a["L1_wq"], wk=a["L1_wk"], wv=a["L1_wv"], wo=a["L1_wo"], xs=col("L1_norm_w"), eps=1e-6),
        dim=64, keys=S2, ctxT=ctxT, pre="rms")
    if layers == 1:
        return
    position_phase(nc, "pos2", B, x[1], pos, dict(
        wr=a["L2_w_r"], wqT=a["L2_w_qT"], peT=a["L2_peT"], own=a["own8"], pb=a["L2_rr"]), big=False, first=P - 2)
    attention_phase(nc, "att2", turns, x[1], out if layers == 2 else x[2], dict(
        wq=a["L2_w_q"], wk=a["L2_w_k"], wv=a["L2_w_v"], wo=a["L2_w_o"], bq=a["L2_rw"], own=a["own8"],
        w1=a["L2_W1"], b1=a["L2_b1"], w2=a["L2_W2"], g1=row("L2_g1"), be1=row("L2_be1"), b2=row("L2_b2"),
        g2=row("L2_g2"), be2=row("L2_be2"), eps1=1e-9, eps2=1e-9),
        dim=8, keys=S2, ctxT=ctxT, pos=pos, post=ACT.Gelu_apprx_tanh, scale=8.0 ** -0.5)
    if layers == 2:
        return
    attention_phase(nc, "att3", turns, x[2], out if layers == 3 else x[3], dict(
        wq=a["sa_wq"], wk=a["sa_wk"], wv=a["sa_wv"], wo=a["sa_wo"], bq=a["sa_bq"], bk=a["sa_bk"], bv=row("sa_bv"),
        bo=row("sa_bo"), own=a["own8"], xs=col("sa_g"), xb=col("sa_b"), eps=1e-5),
        dim=8, keys=P, pre="ln", scale=8.0 ** -0.5)
    if layers == 3:
        return
    attention_phase(nc, "att4", turns, x[3], out if layers == 4 else x[4], dict(
        wq=a["ca_wq"], wk=a["ca_wk"], wv=a["ca_wv"], wo=a["ca_wo"], bq=a["ca_bq"], bk=a["ca_bk"], bv=row("ca_bv"),
        bo=row("ca_bo"), own=a["own8"], xs=col("ca_qg"), xb=col("ca_qb"), cs=col("ca_kg"), cb=col("ca_kb"),
        eps=1e-5, ceps=1e-5), dim=8, keys=S2, ctx=a["ctx"], pre="ln", scale=8.0 ** -0.5)
    if layers == 4:
        return
    experts_phase(nc, "moe", turns, x[4], out, dict(
        rw=a["rwT"], rb=row("rb"), xs=col("moe_g"), xb=col("moe_b"), w1=a["e_w1"], b1=a["e_b1"], w2=a["e_w2"],
        b2=a["e_b2"].rearrange("(o e) d -> o (e d)", o=1).broadcast_to([P, E * P]).rearrange("p (e d) -> p e d", e=E), eps=1e-5))


def lay_out(i):
    A = np.ascontiguousarray
    L0, L1, L2, L3 = (lambda n, k=k: np.asarray(i[f"L{k}_xattn_{n}"]) for k in range(4))
    o = {}
    o["x"] = np.asarray(i["x"])
    o["ctx"] = np.asarray(i["ctx_1024"])
    o["ctxT"] = o["ctx"].transpose(0, 2, 1)
    o["mask"] = np.asarray(i["mask_1x1xSxS2_ff0"])[0, 0]
    o["seg_mask"] = np.asarray(i["mask_1xSxS2_bk1"])[0]
    o["own64"] = np.repeat(np.eye(2, dtype=np.float32), 64, axis=0)
    o["own8"] = np.repeat(np.eye(H, dtype=np.float32), 8, axis=0)
    chunk = lambda m: m.reshape(-1, P, m.shape[-1]).transpose(1, 0, 2)
    heads = lambda m: m.reshape(-1, P).T
    for n in ("Wq", "Wk", "Wv", "Wr"):
        o["L0_" + n] = L0(n).reshape(P, -1)
    o["L0_WqT"] = chunk(o["L0_Wq"].T)
    o["L0_Wo"] = chunk(L0("Wo").reshape(P, -1).T).reshape(P, -1)
    o["L0_peT"] = L0("position_encoding")[0, :RP].T
    for n, s in (("pb", L0("position_bias")), ("sb", L0("segment_bias")), ("cb", L0("content_bias")),
                 ("se0", L0("segment_encoding")[0]), ("se1", L0("segment_encoding")[1])):
        o["L0_" + n] = heads(s)
    o["L0_W1"], o["L0_b1"], o["L0_W2"] = L0("W1"), heads(L0("b1")), chunk(L0("W2"))
    o["L0_b2"], o["L0_g1"], o["L0_be1"], o["L0_g2"], o["L0_be2"] = (
        L0("b2"), L0("ln1_gamma"), L0("ln1_beta"), L0("ln2_gamma"), L0("ln2_beta"))
    for n in ("wq", "wk", "wv"):
        o["L1_" + n] = L1(n)
    o["L1_wo"] = chunk(L1("wo")).reshape(P, -1)
    o["L1_norm_w"] = L1("norm_w")
    for n in ("w_q", "w_k", "w_v", "w_r"):
        o["L2_" + n] = L2(n).reshape(P, P)
    o["L2_w_qT"] = chunk(o["L2_w_q"].T)

    def spaced(m):
        s = np.zeros((G, 32, G, P), np.float32)
        s[:, :8] = m.reshape(G, G, 8, P).transpose(1, 2, 0, 3)
        return s.reshape(P, G * P)

    o["L2_w_o"] = spaced(L2("w_o").reshape(P, P))
    pe = L2("pos_emb")
    at = (np.arange(204) - 51) % pe.shape[0]
    o["L2_peT"] = np.concatenate([pe[at], pe[:1]]).T
    o["L2_rw"], o["L2_rr"] = heads(L2("r_w_bias")), heads(L2("r_r_bias"))
    o["L2_W1"], o["L2_b1"], o["L2_W2"] = L2("ffn_w1"), heads(L2("ffn_b1")), chunk(L2("ffn_w2"))
    o["L2_b2"], o["L2_g1"], o["L2_be1"], o["L2_g2"], o["L2_be2"] = (
        L2("ffn_b2"), L2("ln1_g"), L2("ln1_b"), L2("ln2_g"), L2("ln2_b"))
    for k in ("sa", "ca"):
        iw, ib = L3(f"{k}_in_w"), L3(f"{k}_in_b")
        o[f"{k}_wq"], o[f"{k}_wk"], o[f"{k}_wv"] = iw[:P].T, iw[P:2 * P].T, iw[2 * P:].T
        o[f"{k}_bq"], o[f"{k}_bk"], o[f"{k}_bv"] = ib[:P, None], ib[P:2 * P, None], ib[2 * P:]
        o[f"{k}_wo"] = spaced(L3(f"{k}_out_w").T)
        o[f"{k}_bo"] = L3(f"{k}_out_b")
    o["sa_g"], o["sa_b"] = L3("sa_ln_g"), L3("sa_ln_b")
    o["ca_qg"], o["ca_qb"], o["ca_kg"], o["ca_kb"] = L3("ca_q_ln_g"), L3("ca_q_ln_b"), L3("ca_kv_ln_g"), L3("ca_kv_ln_b")
    o["moe_g"], o["moe_b"], o["rwT"], o["rb"] = L3("moe_ln_g"), L3("moe_ln_b"), L3("router_w").T, L3("router_b")
    o["e_w1"] = L3("e_fc1_w").transpose(2, 0, 1)
    o["e_b1"] = L3("e_fc1_b").reshape(E, FF, P).transpose(2, 0, 1)
    o["e_w2"] = L3("e_fc2_w").reshape(E, P, FF, P).transpose(3, 0, 2, 1).reshape(P, E, FF * P)
    o["e_b2"] = L3("e_fc2_b")
    return {k: A(v) for k, v in o.items()}


def kernel(**inputs):
    import concourse.bacc as bacc
    from concourse.bass_utils import run_bass_kernel_spmd

    arrays = lay_out(inputs)
    nc = bacc.Bacc("TRN2", target_bir_lowering=False, num_devices=1)
    args = {n: nc.dram_tensor(f"in_{n}", v.shape, mybir.dt.from_np(v.dtype), kind="ExternalInput").ap()
            for n, v in arrays.items()}
    out = nc.dram_tensor("out_0", (64, P, P), F32, kind="ExternalOutput").ap()
    build(nc, args, out)
    r = run_bass_kernel_spmd(nc, [{f"in_{n}": v for n, v in arrays.items()}], core_ids=[0])
    return r.results[0]["out_0"]
```

```python
from contextlib import ExitStack

import concourse.bass as bass
import numpy as np
from concourse import mybir

ALU = mybir.AluOpType
ACT = mybir.ActivationFunctionType
F32 = mybir.dt.float32
U8 = mybir.dt.uint8
U32 = mybir.dt.uint32
AX_X = mybir.AxisListType.X

P = 128
S2 = 77
H = 16
G = 4
QUAD = 4
FF = 4
E = 8
ROW = 1280
ROW0 = 8
WIN = S2 + 1
RP = 205
NEG = 1e30
LAG = 3
NB = LAG + 2
CTX_NORM = (2, 4, 6)
X_NORM = (7, 9, 11)
CTX_TURN = 8
X_TURN = 13
X_TURN_RAW = 4
Y_NORM = (2, 3, 4, 5)
Y_TURN = 7
HIDDEN = 8
FF_OUT = 13
Z_NORM = (14, 15, 16)
HEAD = 2
AHEAD = 2


class Signal:

    def __init__(self, handle, per_turn):
        self.sem, self.per_turn, self.made = handle, per_turn, 0

    def at(self, turn, k):
        assert k <= self.per_turn
        return turn * self.per_turn + max(k, 0)


class Phase:

    def __init__(self, nc, name):
        self.nc, self.name, self.stack, self.sems = nc, name, ExitStack(), []

    def sbuf(self, name, shape, dtype=F32):
        return self.stack.enter_context(self.nc.sbuf_tensor(f"{self.name}_{name}", shape, dtype))

    def psum(self, name):
        return self.stack.enter_context(self.nc.psum_tensor(f"{self.name}_{name}", [P, 512], F32))

    def sem(self, name):
        s = self.nc.alloc_semaphore(f"{self.name}_{name}")
        self.sems.append(s)
        return s

    def counter(self, name, per_turn):
        return Signal(self.sem(name), per_turn)

    def close(self):
        self.stack.close()
        self.nc.clear_and_free_semaphores(self.sems)
        self.nc.all_engine_barrier()


def over(ap, axis, n):
    u = ap.unsqueeze(axis)
    shape = list(u.shape)
    shape[axis] = n
    return u.broadcast_to(shape)


def make_identity(nc, pool, ident, zeroed, made):
    nc.gpsimd.memset(ident[:], 0.0).then_inc(zeroed, 1)
    pool.wait_ge(zeroed, 1)
    nc.gpsimd.affine_select(out=ident[:], in_=ident[:], compare_op=ALU.not_equal, fill=1.0, base=0,
                            pattern=[[-1, P]], channel_multiplier=1).then_inc(made, 1)


class Steps:

    def __init__(self, eng, count, turn):
        self.eng, self.count, self.turn, self.k = eng, count, turn, 0

    def __call__(self, ins):
        self.k += 1
        ins.then_inc(self.count.sem, 1)
        self.eng.wait_ge(self.count.sem, self.count.at(self.turn, self.k))

    def end(self):
        assert self.k == self.count.per_turn, (self.k, self.count.per_turn)


def attention_phase(nc, name, turns, x_in, x_out, w, *, dim, keys, ctxT=None, ctx=None, pos=None,
                    pre=None, kv_bias=False, post=None, scale=1.0, segments=None):
    big = dim == 64
    NQ = 8 if big else 1
    W = 2 * keys if big else G * keys
    GK = G * keys
    self_kv = ctxT is None and ctx is None
    ph = Phase(nc, name)
    sb = ph.sbuf

    ident = sb("ident", [P, P])
    halfs = sb("halfs", [P, QUAD])
    wq = sb("wq", [P, NQ * P])
    wk = sb("wk", [P, NQ * P])
    wv = sb("wv", [P, NQ * P])
    wo = sb("wo", [P, (NQ if big else G) * P])
    bq = sb("bq", [P, NQ]) if "bq" in w else None
    bk = sb("bk", [P, NQ]) if "bk" in w else None
    bv = sb("bv", [P, P]) if "bv" in w else None
    bo = sb("bo", [P, P]) if "bo" in w else None
    xs = sb("xs", [P, 1]) if "xs" in w else None
    xb = sb("xb", [P, 1]) if "xb" in w else None
    cs = sb("cs", [P, 1]) if "cs" in w else None
    cb = sb("cb", [P, 1]) if "cb" in w else None
    own = None if big else sb("own", [P, H])
    if post:
        w1 = sb("w1", [P, FF * P])
        b1 = sb("b1", [P, FF])
        w2 = sb("w2", [P, FF, P])
        rows = sb("rows", [P, 5, P])
    if segments:
        seg_w = sb("seg_w", [P, H])
        seg_c = sb("seg_c", [P, H])
        seg_m8 = sb("seg_m8", [P, S2], U8)
        seg_m = sb("seg_m", [P, S2])
        neg_m = sb("neg_m", [P, S2])

    x_raw = sb("x_raw", [P, QUAD, P])
    x_res = sb("x_res", [P, QUAD, P])
    x_nrm = sb("x_nrm", [P, QUAD, P]) if pre else x_raw
    x_sq = sb("x_sq", [P, QUAD, P])
    stat = sb("stat", [P, 8, QUAD])
    xT = sb("xT", [P, QUAD * P])
    if ctx is not None:
        c_raw = sb("c_raw", [keys, QUAD, P])
        c_nrm = sb("c_nrm", [keys, QUAD, P])
        kvT = sb("kvT", [P, QUAD * keys])
    elif self_kv:
        kvT = xT
    else:
        kvT = sb("kvT", [P, QUAD * keys])
    qT = sb("qT", [P, NQ, QUAD * P])
    if big:
        k_bd = sb("k_bd", [P, NQ, QUAD, 2 * keys])
        v_sb = sb("v_sb", [keys, QUAD, NQ * P])
        VW = dim
    else:
        kT = sb("kT", [P, QUAD, keys])
        k_bd = sb("k_bd", [P, 2, H, keys])
        v_sb = sb("v_sb", [keys, QUAD, H, 32])
        VW = 32
    if pos is not None:
        p_sb = sb("p_sb", [P, 2, H * WIN])
    if segments:
        seg_d = sb("seg_d", [P, QUAD, H])
        seg_t = sb("seg_t", [P, G, S2])
    sc = sb("sc", [P, NB, GK])
    ex = sb("ex", [P, NB, GK])
    pr = sb("pr", [P, NB, GK])
    mx = sb("mx", [P, NB, G])
    sm = sb("sm", [P, NB, G])
    rc = sb("rc", [P, NB, G])
    pT = sb("pT", [keys, 2, G * P])
    oT = sb("oT", [P, 2, 2 * P if big else P])
    h = sb("h", [P, QUAD, P])
    y = sb("y", [P, QUAD, P]) if post else None
    x_new = sb("x_new", [P, QUAD, P]) if post else h
    if post:
        yT = sb("yT", [P, QUAD * P])
        u = sb("u", [P, FF, QUAD * P])
    OC = 2 if big else 1

    psS = [ph.psum("psS0"), ph.psum("psS1")]
    psT = [ph.psum("psT0"), ph.psum("psT1")]
    psO = [ph.psum("psO0"), ph.psum("psO1")]
    psA = ph.psum("psA")
    psM = ph.psum("psM")
    gelu = post not in (None, ACT.Relu)

    UN = 4 * QUAD
    zeroed = ph.sem("zeroed")
    consts = ph.sem("consts_made")
    w_in = ph.sem("weights_loaded")
    m_done = ph.sem("mask_terms_made")
    apart = ph.sem("apart")
    x_in_s = ph.counter("x_loaded", 16)
    c_in_s = ph.counter("ctx_loaded", 16)
    pos_in = [ph.counter(f"pos_loaded{i}", 16 * 2) for i in range(2)]
    kept = ph.counter("x_kept", 1)
    NS = {"ln": 7, "rms": 4, None: 0}[pre] + (7 if ctx is not None else 0)
    pre_steps = ph.counter("norm_steps", NS)
    pre_powers = ph.counter("norm_inverse_roots", (1 if pre else 0) + (1 if ctx is not None else 0))
    steps = ph.counter("vector_steps", 21 if post else 1 if bo is None else 2)
    powers = ph.counter("inverse_roots", 2 if post else 0)
    normed = ph.counter("x_normed", 1)
    c_normed = ph.counter("ctx_normed", 1)
    turned = ph.counter("transposed", 2 if ctx is not None else 1)
    turned_out = ph.counter("transposed_copied", 2 if ctx is not None else 1)
    y_turned = ph.counter("y_transposed", 1)
    y_copied = ph.counter("y_transposed_copied", 1)
    seg_made = ph.counter("segment_products", 1)
    seg_out = ph.counter("segment_coefficients", 1)
    seg_inner = ph.counter("segment_steps", 2 * UN)
    seg_used = ph.counter("segments_added", UN)
    NA = NQ + (QUAD if big else 0)
    NV = 2 if not big else NQ + QUAD
    proj_a = ph.counter("projection_a", NA)
    proj_a_out = ph.counter("projection_a_copied", NA)
    proj_v = ph.counter("projection_v", NV)
    proj_v_out = ph.counter("projection_v_copied", 2)
    v_out = ph.counter("values_copied", QUAD)
    k_half = ph.counter("keys_even_heads", NQ)
    k_copied = ph.counter("keys_odd_heads", NQ)
    k_made = ph.counter("keys_spread", 2 * QUAD)
    scored = ph.counter("scores", UN)
    shifted = ph.counter("scores_less_maximum", UN)
    inner = ph.counter("softmax_steps", UN * (2 if pos is not None else 1))
    exped = ph.counter("exponentials", UN)
    summed = ph.counter("sums_inverted", UN)
    probs = ph.counter("probabilities", UN)
    p_turned = ph.counter("probabilities_transposed", UN)
    p_copied = ph.counter("probabilities_copied", UN)
    headed = ph.counter("head_outputs", UN)
    h_copied = ph.counter("head_outputs_copied", UN)
    woed = ph.counter("output_products", UN)
    ffn1 = ph.counter("ff_hidden", FF)
    ffn1_out = ph.counter("ff_activated", FF)
    ffn_act = ph.counter("ff_gelu", 1)
    ffn2 = ph.counter("ff_out", 1)
    ffn2_read = ph.counter("ff_out_read", 1)
    a_read = ph.counter("psA_read", 1)
    res_used = ph.counter("residual_added", 1)
    normed_y = ph.counter("y_normed", 1)
    summing = ph.counter("sums", UN)
    done = ph.counter("turn_done", 1)
    x_stored = ph.counter("x_stored", 16)

    loads = [(wq, w["wq"]), (wk, w["wk"]), (wv, w["wv"]), (wo, w["wo"])]
    for t, n in ((bq, "bq"), (bk, "bk"), (bv, "bv"), (bo, "bo"), (xs, "xs"), (xb, "xb"), (cs, "cs"), (cb, "cb"),
                 (own, "own")):
        if t is not None:
            loads.append((t, w[n]))
    if post:
        loads += [(w1, w["w1"]), (b1, w["b1"]), (w2, w["w2"])]
        loads += [(rows[:, i, :], w[n]) for i, n in enumerate(("g1", "be1", "b2", "g2", "be2"))]
    if segments:
        loads += [(seg_w, w["seg_w"]), (seg_c, w["seg_c"]), (seg_m8, w["seg_m"]), (neg_m, w["neg_m"])]
    CONSTS = 3
    QB = lambda m: m % 2 if big else 1
    x_turn = X_TURN if pre else X_TURN_RAW

    with nc.Block() as block:

        @block.sync
        def _(sp):
            for t, src in loads:
                sp.dma_start(t if isinstance(t, bass.AP) else t[:], src).then_inc(w_in, 16)

            def load(t, first=False):
                if not first:
                    sp.wait_ge(kept.sem, kept.at(t, 0))
                sp.dma_start(x_raw[:], x_in[bass.ds(t * QUAD, QUAD)].rearrange("b p d -> p b d")).then_inc(x_in_s.sem, 16)
                if ctx is not None:
                    if not first:
                        sp.wait_ge(turned.sem, turned.at(t - 1, 1))
                    sp.dma_start(c_raw[:], ctx[bass.ds(t * QUAD, QUAD)].rearrange("b p d -> p b d")).then_inc(c_in_s.sem, 16)
                elif ctxT is not None:
                    if not first:
                        sp.wait_ge(proj_a.sem, proj_a.at(t, 0))
                        sp.sem_inc(apart, 1)
                        sp.wait_ge(proj_v.sem, proj_v.at(t, 0))
                        sp.sem_inc(apart, 1)
                    sp.dma_start(kvT[:].rearrange("p (b k) -> p b k", b=QUAD),
                                 ctxT[bass.ds(t * QUAD, QUAD)].rearrange("b p k -> p b k")).then_inc(c_in_s.sem, 16)

            def load_pos(t, b, first=False):
                if pos is None:
                    return
                if not first:
                    sp.wait_ge(shifted.sem, shifted.at(t, 0) + 4 * (b - 1))
                sp.dma_start(p_sb[:, b % 2, 0:H * WIN - 1],
                             pos[bass.ds(t * QUAD + b, 1), :, ROW0:ROW0 + H * WIN - 1].rearrange("b p n -> p (b n)")
                             ).then_inc(pos_in[b % 2].sem, 16)

            def turn(t, first=False, last=False):
                if not last:
                    load(t + 1)
                load_pos(t, 2)
                load_pos(t, 3)
                if not last:
                    load_pos(t + 1, 0)
                    load_pos(t + 1, 1)
                if not post:
                    store(t)
                elif not first:
                    store(t - 1)

            def store(t):
                sp.wait_ge(done.sem, done.at(t, 1))
                sp.dma_start(x_out[bass.ds(t * QUAD, QUAD)].rearrange("b p d -> p b d"), x_new[:]
                             ).then_inc(x_stored.sem, 16)

            load(0, first=True)
            load_pos(0, 0, first=True)
            load_pos(0, 1, first=True)
            turn(0, first=True)
            with sp.Fori(1, turns - 1) as t:
                turn(t)
            turn(turns - 1, last=True)
            if post:
                store(turns - 1)
            sp.wait_ge(x_stored.sem, 16 * turns)

        @block.gpsimd
        def _(pool):
            make_identity(nc, pool, ident, zeroed, consts)
            nc.gpsimd.memset(halfs[:], -0.5).then_inc(consts, 1)
            nc.gpsimd.memset(k_bd[:] if big else v_sb[:], 0.0).then_inc(consts, 1)
            pool.wait_ge(w_in, 16 * len(loads))
            if segments:
                pool.wait_ge(m_done, 2)

            def power(t, k, of, to, after=steps, made=powers):
                pool.wait_ge(after.sem, after.at(t, k))
                nc.gpsimd.tensor_tensor(to, of, halfs[0:of.shape[0], :], ALU.pow).then_inc(made.sem, 1)

            def ready(t, i):
                if ctx is not None and i == CTX_NORM[1]:
                    power(t, 6, stat[0:keys, 3, :], stat[0:keys, 4, :], pre_steps, pre_powers)
                if pre and i == X_NORM[1]:
                    power(t, (7 if ctx is not None else 0) + (6 if pre == "ln" else 3), stat[:, 5, :], stat[:, 6, :], pre_steps, pre_powers)

            def spread(t, b, half):
                hs = slice(half * H // 2, (half + 1) * H // 2)
                pool.wait_ge(proj_v_out.sem, proj_v_out.at(t, 1))
                if half == 0:
                    pool.wait_ge(scored.sem, scored.at(t, 4 * (b - 1)) if b else scored.at(t, 0))
                nc.gpsimd.tensor_tensor(k_bd[:, b % 2, hs, :], over(kT[:, b, :], 1, H // 2),
                                        over(own[:, hs], 2, keys), ALU.mult).then_inc(k_made.sem, 1)

            def add_segments(t, i):
                b, hs = i // 4, slice(G * (i % 4), G * (i % 4) + G)
                if i % 4 == 0:
                    pool.wait_ge(pos_in[b % 2].sem, pos_in[b % 2].at(t, 16 * (b // 2 + 1)))
                if i == 0:
                    pool.wait_ge(seg_out.sem, seg_out.at(t, 1))
                pv = p_sb[:, b % 2, :].rearrange("p (n j) -> p n j", n=H)[:, hs, 0:S2]
                pool.wait_ge(seg_used.sem, seg_used.at(t, i))
                nc.gpsimd.tensor_tensor(seg_t[:], over(seg_m[:], 1, G), over(seg_d[:, b, hs], 2, S2), ALU.mult
                                        ).then_inc(seg_inner.sem, 1)
                pool.wait_ge(seg_inner.sem, seg_inner.at(t, 2 * i + 1))
                nc.gpsimd.tensor_tensor(seg_t[:], seg_t[:], over(neg_m[:], 1, G), ALU.add).then_inc(seg_inner.sem, 1)
                pool.wait_ge(seg_inner.sem, seg_inner.at(t, 2 * i + 2))
                nc.gpsimd.tensor_tensor(pv, pv, seg_t[:], ALU.add).then_inc(seg_used.sem, 1)

            def finish(t, i):
                if i == Y_NORM[1]:
                    power(t, 7, stat[:, 1, :], stat[:, 2, :])
                if i == Z_NORM[1]:
                    power(t, 18, stat[:, 1, :], stat[:, 2, :])

            def start(t):
                if not big:
                    for b in range(2):
                        for half in range(2):
                            spread(t, b, half)
                if segments:
                    for i in range(HEAD + AHEAD):
                        add_segments(t, i)

            def turn(t, first=False, last=False):
                for i in range(UN):
                    if segments and HEAD <= i and i + AHEAD < UN:
                        add_segments(t, i + AHEAD)
                    pool.wait_ge(summed.sem, summed.at(t, i + 1))
                    pool.wait_ge(p_turned.sem, p_turned.at(t, i + 1 - NB))
                    nc.gpsimd.tensor_tensor(pr[:, i % NB, :].rearrange("p (h k) -> p h k", h=G),
                                            ex[:, i % NB, :].rearrange("p (h k) -> p h k", h=G),
                                            over(rc[:, i % NB, :], 2, keys), ALU.mult).then_inc(probs.sem, 1)
                    if not big and i in (2, 3, 6, 7):
                        spread(t, 2 + i // 4, i % 2)
                    if post and not first:
                        finish(t - 1, i + 1)
                    if not last:
                        ready(t + 1, i + 1)
                if not last:
                    start(t + 1)

            for i in range(UN):
                ready(0, i)
            start(0)
            turn(0, first=True)
            with pool.Fori(1, turns - 1) as t:
                turn(t)
            turn(turns - 1, last=True)
            if post:
                for i in range(UN):
                    finish(turns - 1, i)

        @block.scalar
        def _(act):
            act.wait_ge(w_in, 16 * len(loads))

            def ready(t, i):
                if ctx is not None and i == CTX_TURN:
                    act.wait_ge(turned.sem, turned.at(t, 1))
                    nc.scalar.activation(kvT[:], psM[:, 0:QUAD * keys], ACT.Identity, bias=cb[:, 0:1],
                                         scale=cs[:, 0:1]).then_inc(turned_out.sem, 1)
                if i == x_turn:
                    act.wait_ge(turned.sem, turned.at(t, 2 if ctx is not None else 1))
                    nc.scalar.activation(xT[:], psM[:], ACT.Identity, bias=xb[:, 0:1] if xb is not None else 0.0,
                                         scale=xs[:, 0:1] if xs is not None else 1.0).then_inc(turned_out.sem, 1)

            def copy_q(t, m):
                act.wait_ge(proj_a.sem, proj_a.at(t, m + 1))
                act.wait_ge(scored.sem, scored.at(t, 0))
                nc.scalar.activation(qT[:, m, :], psS[QB(m)][:], ACT.Identity,
                                     bias=bq[:, m:m + 1] if bq is not None else 0.0).then_inc(proj_a_out.sem, 1)

            def copy_k(t, m):
                act.wait_ge(proj_v.sem, proj_v.at(t, m + 1))
                act.wait_ge(k_half.sem, k_half.at(t, m + 1))
                src = (psT + psO)[m % 4][64:P, 0:QUAD * keys].rearrange("p (b k) -> p b k", b=QUAD)
                nc.scalar.activation(k_bd[64:P, m, :, keys:2 * keys], src, ACT.Identity,
                                     bias=bk[64:P, m:m + 1] if bk is not None else 0.0).then_inc(k_copied.sem, 1)

            def project_first(t, d):
                for m in range(2 * d - 2, 2 * d) if big else range(d - 1, d):
                    if 0 <= m < NQ:
                        copy_q(t, m)

            def project(t):
                for m in range(NQ if big else 0):
                    copy_k(t, m)
                for i in range(HEAD):
                    exponential(t, i)
                if big:
                    for b in range(QUAD):
                        act.wait_ge(proj_a.sem, proj_a.at(t, NQ + b + 1))
                        act.wait_ge(headed.sem, headed.at(t, 0))
                        nc.scalar.activation(v_sb[:, b, 0:512], psO[b % 2][0:keys, :], ACT.Copy).then_inc(proj_a_out.sem, 1)
                act.wait_ge(x_in_s.sem, x_in_s.at(t, 16))
                act.wait_ge(res_used.sem, res_used.at(t, 0))
                nc.scalar.activation(x_res[:], x_raw[:], ACT.Copy).then_inc(kept.sem, 1)

            def exponential(t, i):
                act.wait_ge(shifted.sem, shifted.at(t, i + 1))
                act.wait_ge(probs.sem, probs.at(t, i + 1 - NB))
                nc.scalar.activation(ex[:, i % NB, :], sc[:, i % NB, :], ACT.Exp, scale=scale).then_inc(exped.sem, 1)

            def copy_probs(t, i):
                act.wait_ge(p_turned.sem, p_turned.at(t, i + 1))
                act.wait_ge(headed.sem, headed.at(t, i - 1))
                nc.scalar.activation(pT[:, i % 2, :], psT[i % 2][0:keys, :], ACT.Copy).then_inc(p_copied.sem, 1)

            def copy_heads(t, i):
                act.wait_ge(headed.sem, headed.at(t, i + 1))
                act.wait_ge(woed.sem, woed.at(t, i - 1))
                nc.scalar.activation(oT[:, i % 2, :], psO[i % 2][:, 0:OC * P], ACT.Copy).then_inc(h_copied.sem, 1)

            def finish(t, i):
                if i == Y_TURN:
                    act.wait_ge(y_turned.sem, y_turned.at(t, 1))
                    nc.scalar.activation(yT[:], psM[:], ACT.Copy).then_inc(y_copied.sem, 1)
                if HIDDEN <= i < HIDDEN + FF:
                    f = i - HIDDEN
                    act.wait_ge(ffn1.sem, ffn1.at(t, f + 1))
                    act.wait_ge(ffn2.sem, ffn2.at(t, 0))
                    nc.scalar.activation(u[:, f, :], psM[:], ACT.Identity if gelu else post, bias=b1[:, f:f + 1]
                                         ).then_inc(ffn1_out.sem, 1)
                if i == HIDDEN + FF - 1 and gelu:
                    act.wait_ge(ffn1_out.sem, ffn1_out.at(t, FF))
                    nc.scalar.activation(u[:], u[:], post).then_inc(ffn_act.sem, 1)

            def turn(t, first=False, last=False):
                for i in range(HEAD, UN + LAG + 2):
                    if LAG <= i < UN + LAG:
                        copy_probs(t, i - LAG)
                    if LAG < i < UN + LAG + 1:
                        copy_heads(t, i - LAG - 1)
                    if i < UN:
                        exponential(t, i)
                    if post and not first:
                        finish(t - 1, i)
                    if not last:
                        ready(t + 1, i)
                        project_first(t + 1, i - UN)
                if not last:
                    project(t + 1)

            for i in range(UN):
                ready(0, i)
            for d in range(LAG + 2):
                project_first(0, d)
            project(0)
            turn(0, first=True)
            with act.Fori(1, turns - 1) as t:
                turn(t)
            turn(turns - 1, last=True)
            if post:
                for i in range(UN):
                    finish(turns - 1, i)

        @block.tensor
        def _(pe):
            pe.wait_ge(w_in, 16 * len(loads))
            pe.wait_ge(consts, CONSTS)

            def ready(t, i):
                if ctx is not None and i == CTX_TURN:
                    pe.wait_ge(c_normed.sem, c_normed.at(t, 1))
                    pe.wait_ge(turned_out.sem, turned_out.at(t, 0))
                    for b in range(QUAD):
                        mm = pe.transpose(psM[:, b * keys:(b + 1) * keys], c_nrm[:, b, :], ident[0:keys, 0:keys])
                    mm.then_inc(turned.sem, 1)
                if i == x_turn:
                    if segments:
                        pe.wait_ge(seg_out.sem, seg_out.at(t, 0))
                    if pre:
                        pe.wait_ge(normed.sem, normed.at(t, 1))
                    else:
                        pe.wait_ge(x_in_s.sem, x_in_s.at(t, 16))
                    pe.wait_ge(turned_out.sem, turned_out.at(t, 1 if ctx is not None else 0))
                    for b in range(QUAD):
                        mm = pe.transpose(psM[:, b * P:(b + 1) * P], x_nrm[:, b, :], ident[:])
                    mm.then_inc(turned.sem, 1)

            def project_first(t, d):
                if d == (0 if self_kv else 1):
                    pe.wait_ge(turned_out.sem, turned_out.at(t, turned_out.per_turn))
                if d == 0:
                    if ctx is not None:
                        pe.wait_ge(turned_out.sem, turned_out.at(t, 1))
                    if ctxT is not None:
                        pe.wait_ge(c_in_s.sem, c_in_s.at(t, 16))
                    pe.wait_ge(shifted.sem, shifted.at(t, 0))
                    if not big:
                        pe.matmul(psS[0][:, 0:QUAD * keys], wk[:], kvT[:], start=True, stop=True).then_inc(proj_v.sem, 1)
                for m in range(2 * d - 2, 2 * d) if big else range(d - 1, d):
                    if 0 <= m < NQ:
                        pe.wait_ge(proj_a_out.sem, proj_a_out.at(t, m - 1))
                        pe.matmul(psS[QB(m)][:], wq[:, m * P:(m + 1) * P], xT[:], start=True, stop=True
                                  ).then_inc(proj_a.sem, 1)

            def project(t, first=False):
                if segments:
                    if not first:
                        pe.wait_ge(ffn2_read.sem, ffn2_read.at(t - 1, 0))
                    for b in range(QUAD):
                        mm = pe.matmul(psM[:, b * H:(b + 1) * H], xT[:, b * P:(b + 1) * P], seg_w[:], start=True, stop=True)
                    mm.then_inc(seg_made.sem, 1)

                for m in range(NQ if big else 0):
                    pe.wait_ge(p_copied.sem, p_copied.at(t, 0))
                    pe.wait_ge(h_copied.sem, h_copied.at(t, 0))
                    pe.wait_ge(k_copied.sem, k_copied.at(t, m - 3))
                    pe.matmul((psT + psO)[m % 4][:, 0:QUAD * keys], wk[:, m * P:(m + 1) * P], kvT[:], start=True, stop=True
                              ).then_inc(proj_v.sem, 1)
                if not big:
                    pe.wait_ge(p_copied.sem, p_copied.at(t, 0))
                    for b in range(QUAD):
                        mm = pe.matmul(psT[1][0:keys, b * P:(b + 1) * P], kvT[:, b * keys:(b + 1) * keys], wv[:],
                                       start=True, stop=True)
                    mm.then_inc(proj_v.sem, 1)
                for i in range(HEAD):
                    scores(t, i)
                if big:
                    for b in range(QUAD):
                        pe.wait_ge(k_copied.sem, k_copied.at(t, NQ))
                        pe.wait_ge(proj_a_out.sem, proj_a_out.at(t, NQ + b - 1))
                        pe.matmul(psO[b % 2][0:keys, :], kvT[:, b * keys:(b + 1) * keys], wv[:, 0:512],
                                  start=True, stop=True).then_inc(proj_a.sem, 1)
                        pe.wait_ge(v_out.sem, v_out.at(t, b - 1))
                        pe.matmul(psT[b % 2][0:keys, :], kvT[:, b * keys:(b + 1) * keys], wv[:, 512:1024],
                                  start=True, stop=True).then_inc(proj_v.sem, 1)

            def scores(t, i):
                b, g = i // 4, i % 4
                if i == 0:
                    pe.wait_ge(proj_a_out.sem, proj_a_out.at(t, NQ))
                    if big:
                        pe.wait_ge(k_half.sem, k_half.at(t, NQ))
                        pe.wait_ge(k_copied.sem, k_copied.at(t, NQ))
                if not big and g % 2 == 0:
                    pe.wait_ge(k_made.sem, k_made.at(t, 2 * b + g // 2 + 1))
                pe.wait_ge(shifted.sem, shifted.at(t, i - 1))
                for j in range(2 if big else 1):
                    m = 2 * g + j if big else 0
                    mm = pe.matmul(psS[i % 2][:, j * W:(j + 1) * W], qT[:, m, b * P:(b + 1) * P],
                                   k_bd[:, m, b, :] if big else k_bd[:, b % 2, G * g:G * (g + 1), :],
                                   start=True, stop=True)
                mm.then_inc(scored.sem, 1)

            def turn_probs(t, i):
                pe.wait_ge(probs.sem, probs.at(t, i + 1))
                pe.wait_ge(p_copied.sem, p_copied.at(t, i - 1))
                if i == 0 and big:
                    pe.wait_ge(v_out.sem, v_out.at(t, QUAD))
                for c in range(G):
                    mm = pe.transpose(psT[i % 2][0:keys, c * P:(c + 1) * P], pr[:, i % NB, c * keys:(c + 1) * keys], ident[:])
                mm.then_inc(p_turned.sem, 1)

            def heads(t, i):
                b, g = i // 4, i % 4
                if i == 0:
                    if big:
                        pe.wait_ge(proj_a_out.sem, proj_a_out.at(t, NA))
                        pe.wait_ge(v_out.sem, v_out.at(t, QUAD))
                    else:
                        pe.wait_ge(proj_v_out.sem, proj_v_out.at(t, 2))
                pe.wait_ge(p_copied.sem, p_copied.at(t, i + 1))
                pe.wait_ge(h_copied.sem, h_copied.at(t, i - 1))
                for c in range(G):
                    n = G * g + c
                    if big:
                        mm = pe.matmul(psO[i % 2][(c % 2) * 64:(c % 2) * 64 + 64, (c // 2) * P:(c // 2 + 1) * P],
                                       v_sb[:, b, n * 64:(n + 1) * 64], pT[:, i % 2, c * P:(c + 1) * P],
                                       start=True, stop=True)
                    else:
                        mm = pe.matmul(psO[i % 2][32 * c:32 * c + 32, 0:P], v_sb[:, b, n, :],
                                       pT[:, i % 2, c * P:(c + 1) * P], start=True, stop=True)
                mm.then_inc(headed.sem, 1)

            def out_product(t, i):
                b, g = i // 4, i % 4
                pe.wait_ge(h_copied.sem, h_copied.at(t, i + 1))
                if i == 0:
                    pe.wait_ge(a_read.sem, a_read.at(t, 0))
                for j in range(OC):
                    m = OC * g + j
                    mm = pe.matmul(psA[:, b * P:(b + 1) * P], oT[:, i % 2, j * P:(j + 1) * P],
                                   wo[:, m * P:(m + 1) * P], start=(m == 0), stop=(m == OC * G - 1))
                mm.then_inc(woed.sem, 1)

            def finish(t, i, last=False):
                if i == Y_TURN:
                    pe.wait_ge(normed_y.sem, normed_y.at(t, 1))
                    if not last:
                        pe.wait_ge(turned_out.sem, turned_out.at(t + 2, 1))
                    for b in range(QUAD):
                        mm = pe.transpose(psM[:, b * P:(b + 1) * P], y[:, b, :], ident[:])
                    mm.then_inc(y_turned.sem, 1)
                if HIDDEN <= i < HIDDEN + FF:
                    f = i - HIDDEN
                    pe.wait_ge(y_copied.sem, y_copied.at(t, 1))
                    pe.wait_ge(ffn1_out.sem, ffn1_out.at(t, f))
                    pe.matmul(psM[:], w1[:, f * P:(f + 1) * P], yT[:], start=True, stop=True).then_inc(ffn1.sem, 1)
                if i == FF_OUT:
                    pe.wait_ge(ffn1_out.sem, ffn1_out.at(t, FF))
                    if gelu:
                        pe.wait_ge(ffn_act.sem, ffn_act.at(t, 1))
                    for b in range(QUAD):
                        for f in range(FF):
                            mm = pe.matmul(psM[:, b * P:(b + 1) * P], u[:, f, b * P:(b + 1) * P], w2[:, f, :],
                                           start=(f == 0), stop=(f == FF - 1))
                    mm.then_inc(ffn2.sem, 1)

            def turn(t, first=False, last=False):
                for i in range(HEAD, UN + LAG + 2):
                    if i < UN:
                        scores(t, i)
                    if LAG <= i < UN + LAG:
                        turn_probs(t, i - LAG)
                    if LAG < i < UN + LAG + 1:
                        heads(t, i - LAG - 1)
                    if i > LAG + 1:
                        out_product(t, i - LAG - 2)
                    if post and not first:
                        finish(t - 1, i, last)
                    if not last:
                        ready(t + 1, i)
                        project_first(t + 1, i - UN)
                if not last:
                    project(t + 1)

            for i in range(UN):
                ready(0, i)
            for d in range(LAG + 2):
                project_first(0, d)
            project(0, first=True)
            turn(0, first=True)
            with pe.Fori(1, turns - 1) as t:
                turn(t)
            turn(turns - 1, last=True)
            if post:
                for i in range(UN):
                    finish(turns - 1, i, last=True)

        @block.vector
        def _(dve):
            v = nc.vector
            dve.wait_ge(w_in, 16 * len(loads))
            dve.wait_ge(consts, CONSTS)
            if segments:
                v.tensor_copy(seg_m[:], seg_m8[:]).then_inc(m_done, 1)
                v.tensor_scalar(neg_m[:], neg_m[:], -NEG / scale, None, ALU.mult).then_inc(m_done, 1)

            def mean_off(step, src, st, xc):
                p = src.shape[0]
                step(v.reduce_sum(st[0:p, 0, :], src, AX_X))
                step(v.tensor_scalar(st[0:p, 0, :], st[0:p, 0, :], 1.0 / P, None, ALU.mult))
                step(v.tensor_tensor(xc, src, over(st[0:p, 0, :], 2, P), ALU.subtract))

            def mean_square(step, src, st, sq, eps):
                step(v.tensor_tensor(sq, src, src, ALU.mult))
                step(v.reduce_sum(st, sq, AX_X))
                step(v.tensor_scalar(st, st, 1.0 / P, eps, ALU.mult, ALU.add))

            def ready(t, i):
                if ctx is not None:
                    step = Steps(dve, pre_steps, t)
                    if i == CTX_NORM[0]:
                        dve.wait_ge(c_in_s.sem, c_in_s.at(t, 16))
                        mean_off(step, c_raw[:], stat, c_nrm[:])
                    if i == CTX_NORM[1]:
                        step.k = 3
                        mean_square(step, c_nrm[:], stat[0:keys, 3, :], x_sq[0:keys], w["ceps"])
                    if i == CTX_NORM[2]:
                        step.k = 6
                        dve.wait_ge(pre_powers.sem, pre_powers.at(t, 1))
                        step(v.tensor_tensor(c_nrm[:], c_nrm[:], over(stat[0:keys, 4, :], 2, P), ALU.mult))
                        dve.sem_inc(c_normed.sem, 1)
                if pre:
                    base = 7 if ctx is not None else 0
                    step = Steps(dve, pre_steps, t)
                    if i == X_NORM[0]:
                        dve.wait_ge(x_in_s.sem, x_in_s.at(t, 16))
                        if pre == "ln":
                            step.k = base
                            mean_off(step, x_raw[:], stat, x_nrm[:])
                    if i == X_NORM[1]:
                        step.k = base + (3 if pre == "ln" else 0)
                        mean_square(step, (x_nrm if pre == "ln" else x_raw)[:], stat[:, 5, :], x_sq[:], w["eps"])
                    if i == X_NORM[2]:
                        step.k = base + (6 if pre == "ln" else 3)
                        dve.wait_ge(pre_powers.sem, pre_powers.at(t, 2 if ctx is not None else 1))
                        step(v.tensor_tensor(x_nrm[:], (x_nrm if pre == "ln" else x_raw)[:], over(stat[:, 6, :], 2, P), ALU.mult))
                        dve.sem_inc(normed.sem, 1)

            def project_segments(t):
                dve.wait_ge(seg_made.sem, seg_made.at(t, 1))
                dve.wait_ge(seg_used.sem, seg_used.at(t, 0))
                v.tensor_tensor(seg_d[:], psM[:, 0:QUAD * H].rearrange("p (b n) -> p b n", b=QUAD),
                                over(seg_c[:], 1, QUAD), ALU.add).then_inc(seg_out.sem, 1)

            def narrow_keys(t):
                dve.wait_ge(proj_v.sem, proj_v.at(t, 1))
                dve.wait_ge(k_made.sem, k_made.at(t, 0))
                src = psS[0][:, 0:QUAD * keys].rearrange("p (b k) -> p b k", b=QUAD)
                (v.tensor_scalar(kT[:], src, bk[:, 0:1], None, ALU.add) if bk is not None
                 else v.tensor_copy(kT[:], src)).then_inc(proj_v_out.sem, 1)

            def project(t):
                if big:
                    for m in range(NQ):
                        dve.wait_ge(proj_v.sem, proj_v.at(t, m + 1))
                        dve.wait_ge(scored.sem, scored.at(t, 0))
                        src = (psT + psO)[m % 4][0:64, 0:QUAD * keys].rearrange("p (b k) -> p b k", b=QUAD)
                        dst = k_bd[0:64, m, :, 0:keys]
                        (v.tensor_scalar(dst, src, bk[0:64, m:m + 1], None, ALU.add) if bk is not None
                         else v.tensor_copy(dst, src)).then_inc(k_half.sem, 1)
                else:
                    dve.wait_ge(proj_v.sem, proj_v.at(t, 2))
                    dve.wait_ge(headed.sem, headed.at(t, 0))
                    src = psT[1][0:keys, :].rearrange("p (b h e) -> p b h e", b=QUAD, h=H)
                    dst = v_sb[:, :, :, 0:8]
                    (v.tensor_tensor(dst, src, over(bv[0:keys, :].rearrange("p (h e) -> p h e", h=H), 1, QUAD), ALU.add)
                     if bv is not None else v.tensor_copy(dst, src)).then_inc(proj_v_out.sem, 1)
                for i in range(HEAD):
                    soft(t, i)
                if big:
                    for b in range(QUAD):
                        dve.wait_ge(proj_v.sem, proj_v.at(t, NQ + b + 1))
                        dve.wait_ge(headed.sem, headed.at(t, 0))
                        v.tensor_copy(v_sb[:, b, 512:1024], psT[b % 2][0:keys, :]).then_inc(v_out.sem, 1)

            def soft(t, i):
                b, g = i // 4, i % 4
                s = i % NB
                nin = 2 if pos is not None else 1
                sv = sc[:, s, :].rearrange("p (h k) -> p h k", h=G)
                src = psS[i % 2][:, 0:GK].rearrange("p (h k) -> p h k", h=G)
                dve.wait_ge(scored.sem, scored.at(t, i + 1))
                dve.wait_ge(exped.sem, exped.at(t, i + 1 - NB))
                q = i * nin
                if pos is not None:
                    if segments:
                        dve.wait_ge(seg_used.sem, seg_used.at(t, i + 1))
                    else:
                        dve.wait_ge(pos_in[b % 2].sem, pos_in[b % 2].at(t, 16 * (b // 2 + 1)))
                    v.tensor_tensor(sv, src, p_sb[:, b % 2, G * g * WIN:G * (g + 1) * WIN].rearrange(
                        "p (h k) -> p h k", h=G)[:, :, 0:S2], ALU.add).then_inc(inner.sem, 1)
                    q += 1
                    dve.wait_ge(inner.sem, inner.at(t, q))
                    src = sv
                v.reduce_max(mx[:, s, :], src, AX_X).then_inc(inner.sem, 1)
                q += 1
                dve.wait_ge(inner.sem, inner.at(t, q))
                v.tensor_tensor(sv, src, over(mx[:, s, :], 2, keys), ALU.subtract).then_inc(shifted.sem, 1)

            def sums(t, i):
                s = i % NB
                dve.wait_ge(exped.sem, exped.at(t, i + 1))
                dve.wait_ge(probs.sem, probs.at(t, i + 1 - NB))
                v.reduce_sum(sm[:, s, :], ex[:, s, :].rearrange("p (h k) -> p h k", h=G), AX_X).then_inc(summing.sem, 1)
                dve.wait_ge(summing.sem, summing.at(t, i + 1))
                v.reciprocal(rc[:, s, :], sm[:, s, :]).then_inc(summed.sem, 1)

            def finish(t, i):
                step = Steps(dve, steps, t)
                if i == Y_NORM[0]:
                    step.k = 1
                    mean_off(step, h[:], stat, h[:])
                if i == Y_NORM[1]:
                    step.k = 4
                    mean_square(step, h[:], stat[:, 1, :], x_sq[:], w["eps1"])
                if i == Y_NORM[2]:
                    step.k = 7
                    dve.wait_ge(powers.sem, powers.at(t, 1))
                    step(v.tensor_tensor(y[:], h[:], over(stat[:, 2, :], 2, P), ALU.mult))
                if i == Y_NORM[3]:
                    step.k = 8
                    step(v.tensor_tensor(y[:], y[:], over(rows[:, 0, :], 1, QUAD), ALU.mult))
                    step(v.tensor_tensor(y[:], y[:], over(rows[:, 1, :], 1, QUAD), ALU.add))
                    dve.sem_inc(normed_y.sem, 1)
                if i == HIDDEN:
                    step.k = 10
                    dve.wait_ge(y_turned.sem, y_turned.at(t, 1))
                    step(v.tensor_tensor(y[:], y[:], over(rows[:, 2, :], 1, QUAD), ALU.add))
                if i == Z_NORM[0]:
                    step.k = 11
                    dve.wait_ge(ffn2.sem, ffn2.at(t, 1))
                    step(v.tensor_tensor(h[:], psM[:].rearrange("p (b d) -> p b d", b=QUAD), y[:], ALU.add))
                    dve.sem_inc(ffn2_read.sem, 1)
                    mean_off(step, h[:], stat, h[:])
                if i == Z_NORM[1]:
                    step.k = 15
                    mean_square(step, h[:], stat[:, 1, :], x_sq[:], w["eps2"])
                if i == Z_NORM[2]:
                    step.k = 18
                    dve.wait_ge(powers.sem, powers.at(t, 2))
                    dve.wait_ge(x_stored.sem, x_stored.at(t, 0))
                    step(v.tensor_tensor(x_new[:], h[:], over(stat[:, 2, :], 2, P), ALU.mult))
                    step(v.tensor_tensor(x_new[:], x_new[:], over(rows[:, 3, :], 1, QUAD), ALU.mult))
                    step(v.tensor_tensor(x_new[:], x_new[:], over(rows[:, 4, :], 1, QUAD), ALU.add))
                    dve.sem_inc(done.sem, 1)
                    step.end()

            def turn(t, first=False, last=False):
                for i in range(HEAD - 1):
                    sums(t, i)
                for i in range(HEAD, UN + 1):
                    if i < UN:
                        soft(t, i)
                    sums(t, i - 1)
                    if i == UN and not big and not last:
                        narrow_keys(t + 1)
                    if post and not first:
                        finish(t - 1, i)
                    if not last:
                        ready(t + 1, i)

                step = Steps(dve, steps, t)
                dve.wait_ge(kept.sem, kept.at(t, 1))
                dve.wait_ge(woed.sem, woed.at(t, UN))
                if not post:
                    dve.wait_ge(x_stored.sem, x_stored.at(t, 0))
                step(v.tensor_tensor(h[:], psA[:].rearrange("p (b d) -> p b d", b=QUAD), x_res[:], ALU.add))
                dve.sem_inc(a_read.sem, 1)
                dve.sem_inc(res_used.sem, 1)
                if bo is not None:
                    step(v.tensor_tensor(h[:], h[:], over(bo[:], 1, QUAD), ALU.add))
                if not post:
                    dve.sem_inc(done.sem, 1)
                    step.end()
                if not last:
                    if segments:
                        project_segments(t + 1)
                    project(t + 1)

            for i in range(UN):
                ready(0, i)
            if segments:
                project_segments(0)
            if not big:
                narrow_keys(0)
            project(0)
            turn(0, first=True)
            with dve.Fori(1, turns - 1) as t:
                turn(t)
            turn(turns - 1, last=True)
            if post:
                for i in range(UN + 1):
                    finish(turns - 1, i)
    ph.close()


def position_phase(nc, name, batches, x_in, pos_out, w, *, big, first, seg_out=None):
    R2 = 2 * batches
    pairs = P // 2
    NQ = 8 if big else 1
    NO = 2 if big else H
    SPLIT = [(0, 6), (6, 11), (11, 16)]
    ph = Phase(nc, name)
    sb = ph.sbuf
    ident = sb("ident", [P, P])
    wr = sb("wr", [P, NQ * P])
    wqT = sb("wqT", [P, NQ, P])
    peT = sb("peT", [P, RP])
    cols = sb("cols", [P, 5, NQ])
    own = sb("own", [P, NO])
    ones = sb("ones", [P, P])
    rT = sb("rT", [P, NQ, RP])
    r_own = sb("r_own", [P, 2, RP])
    b_rep = sb("b_rep", [P, 2, P])
    e_rep = sb("e_rep", [P, 2, P])
    s_own = sb("s_own", [P, 2, RP])
    win = sb("win", [P, H, RP])
    cst = sb("cst", [P, H, RP])
    if seg_out:
        dcols = sb("dcols", [P, 2, NQ])
        d_own = sb("d_own", [P, H])
        segs = sb("segs", [P, 2, H])
        s_rep = sb("s_rep", [P, NQ, P])
    xi = sb("xi", [P, 2, P])
    xiT = sb("xiT", [P, 2, P])
    stage = sb("stage", [P, 2, H, WIN])
    ps = [[ph.psum(f"ps{s}{c}") for c in range(3)] for s in range(2)]
    psX = [ph.psum(f"psX{s}") for s in range(2)]

    zeroed, made, w_in = ph.sem("zeroed"), ph.sem("identity_made"), ph.sem("weights_loaded")
    r_done, r_copied = ph.sem("r_projected"), ph.sem("r_copied")
    pre_v = ph.sem("constants_prepared")
    win_done, win_copied = ph.sem("windows_done"), ph.sem("windows_copied")
    cst_copied = ph.sem("constants_copied")
    seg_done, seg_copied, seg_stored = ph.sem("segments_done"), ph.sem("segments_copied"), ph.sem("segments_stored")
    apart_v, apart_p = ph.sem("apart_vector"), ph.sem("apart_tensor")
    x_loaded = [ph.counter(f"x_loaded{s}", 32) for s in range(2)]
    turned = ph.counter("x_transposed", 2)
    copied = ph.counter("x_copied", 2)
    multiplied = ph.counter("products", 2)
    staged = ph.counter("rows_staged", 2)
    stored = [ph.counter(f"rows_stored{s}", 32) for s in range(2)]

    loads = [(wr[:], w["wr"]), (wqT[:], w["wqT"]), (peT[:], w["peT"]), (own[:], w["own"])]
    loads += [(cols[:, i, :], w[n]) for i, n in enumerate(("pb", "sb", "cb", "se0", "se1")) if n in w]
    turns = pairs // 2
    extra = "sb" in w
    DC = 4 if extra else 1

    with nc.Block() as block:

        @block.gpsimd
        def _(pool):
            make_identity(nc, pool, ident, zeroed, made)
            nc.gpsimd.memset(ones[:], 1.0).then_inc(made, 1)

        @block.sync
        def _(sp):
            for t, src in loads:
                sp.dma_start(t, src).then_inc(w_in, 16)
            if seg_out:
                sp.wait_ge(seg_copied, 1)
                sp.dma_start(seg_out[0], segs[:, 0, :]).then_inc(seg_stored, 16)
                sp.dma_start(seg_out[1], segs[:, 1, :]).then_inc(seg_stored, 16)
                sp.wait_ge(seg_stored, 32)
            with sp.Fori(0, turns) as t:
                for s in range(2):
                    sp.wait_ge(staged.sem, staged.at(t, s + 1))
                    for i in range(2):
                        at = ROW0 - 1 + i
                        sp.dma_start(pos_out[:, bass.ds(t * 4 + 2 * s + i, 1), at:at + H * WIN].rearrange("b i n -> b (i n)"),
                                     stage[batches * i:batches * (i + 1), s, :, :].rearrange("p n j -> p (n j)")
                                     ).then_inc(stored[s].sem, 16)
            for s in range(2):
                sp.wait_ge(stored[s].sem, 32 * turns)

        @block.scalar
        def _(act):
            for m in range(NQ):
                act.wait_ge(r_done, m + 1)
                nc.scalar.activation(rT[:, m, :], psX[m % 2][:, 0:RP], ACT.Copy).then_inc(r_copied, 1)
            for n in range(H):
                act.wait_ge(win_done, n + 1)
                nc.scalar.activation(win[:, n, :], ps[n % 2][0][:, 0:RP], ACT.Copy).then_inc(win_copied, 1)
            if seg_out:
                act.wait_ge(seg_done, 1)
                nc.scalar.activation(segs[:].rearrange("p a n -> p (a n)"), psX[0][:, 0:2 * H], ACT.Copy).then_inc(seg_copied, 1)

            def load(t, s):
                for i in range(2):
                    act.dma_start(xi[batches * i:batches * (i + 1), s, :],
                                  x_in[:, bass.ds(t * 4 + 2 * s + i, 1), :].rearrange("b i d -> b (i d)")
                                  ).then_inc(x_loaded[s].sem, 16)

            def turn(t, last=False):
                for s in range(2):
                    act.wait_ge(turned.sem, turned.at(t, s + 1))
                    if not last:
                        load(t + 1, s)
                    act.wait_ge(multiplied.sem, multiplied.at(t, s - 1))
                    nc.scalar.activation(xiT[:, s, 0:R2], psX[s][:, 0:R2], ACT.Copy).then_inc(copied.sem, 1)

            load(0, 0)
            load(0, 1)
            with act.Fori(0, turns - 1) as t:
                turn(t)
            turn(turns - 1, last=True)

        @block.vector
        def _(dve):
            v = nc.vector
            dve.wait_ge(w_in, 16 * len(loads))
            dve.wait_ge(made, 2)
            done = 0
            if extra:
                v.tensor_tensor(cols[:, 2, :], cols[:, 1, :], cols[:, 2, :], ALU.subtract).then_inc(pre_v, 1)
                v.tensor_tensor(dcols[:, 0, :], cols[:, 4, :], cols[:, 3, :], ALU.subtract).then_inc(pre_v, 1)
                dve.wait_ge(pre_v, 2)
                v.tensor_tensor(s_rep[:], over(ones[:], 1, NQ), over(cols[:, 1, :], 2, P), ALU.mult).then_inc(pre_v, 1)
                done = 3
                for n in range(H):
                    m, o = n // NO, n % NO
                    v.tensor_tensor(d_own[:, n:n + 1], dcols[:, 0, m:m + 1], own[:, o:o + 1], ALU.mult).then_inc(pre_v, 1)
                    done += 1
            for n in range(H):
                m, o = n // NO, n % NO
                dve.wait_ge(r_copied, m + 1)
                if n >= 2:
                    dve.wait_ge(win_done, n - 1)
                v.tensor_scalar(r_own[:, n % 2, :], rT[:, m, :], own[:, o:o + 1], None, ALU.mult).then_inc(pre_v, 1)
                v.tensor_scalar(b_rep[:, n % 2, :], ones[:], cols[:, 0, m:m + 1], None, ALU.mult).then_inc(pre_v, 1)
                done += 2
                if extra:
                    v.tensor_scalar(e_rep[:, n % 2, :], ones[:], cols[:, 2, m:m + 1], None, ALU.mult).then_inc(pre_v, 1)
                    v.tensor_tensor(s_own[:, n % 2, :], over(cols[:, 3, m], 1, RP), over(own[:, o], 1, RP), ALU.mult
                                    ).then_inc(pre_v, 1)
                    done += 2
                if n >= 1:
                    dve.wait_ge(win_done, n)
                    v.tensor_copy(cst[:, n - 1, :], ps[(n - 1) % 2][1][:, 0:RP]).then_inc(cst_copied, 1)
            dve.wait_ge(win_done, H)
            v.tensor_copy(cst[:, H - 1, :], ps[(H - 1) % 2][1][:, 0:RP]).then_inc(cst_copied, 1)
            dve.wait_ge(cst_copied, H)
            with dve.Fori(0, turns) as t:
                for s in range(2):
                    dve.wait_ge(multiplied.sem, multiplied.at(t, s + 1))
                    dve.wait_ge(stored[s].sem, stored[s].at(t, 0))
                    dve.sem_inc(apart_v, 1)
                    for c, (a, b) in enumerate(SPLIT):
                        ins = v.tensor_tensor(
                            stage[0:R2, s, a:b, :], ps[s][c][0:R2, 0:(b - a) * WIN].rearrange("p (n j) -> p n j", n=b - a),
                            cst[0:R2, a:b, bass.ds(first - 2 * s - t * 4, WIN)], ALU.add)
                    ins.then_inc(staged.sem, 1)

        @block.tensor
        def _(pe):
            pe.wait_ge(w_in, 16 * len(loads))
            pe.wait_ge(made, 2)
            for m in range(NQ):
                if m >= 2:
                    pe.wait_ge(r_copied, m - 1)
                pe.matmul(psX[m % 2][:, 0:RP], wr[:, m * P:(m + 1) * P], peT[:], start=True, stop=True).then_inc(r_done, 1)
            pre = 3 + H if extra else 0
            for n in range(H):
                m = n // NO
                pe.wait_ge(pre_v, pre + (4 if extra else 2) * (n + 1))
                if n >= 2:
                    pe.wait_ge(win_copied, n - 1)
                    pe.wait_ge(cst_copied, n - 1)
                pe.matmul(ps[n % 2][0][:, 0:RP], wqT[:, m, :], r_own[:, n % 2, :], start=True, stop=True)
                mm = pe.matmul(ps[n % 2][1][:, 0:RP], b_rep[:, n % 2, :], r_own[:, n % 2, :], start=True, stop=not extra)
                if extra:
                    mm = pe.matmul(ps[n % 2][1][:, 0:RP], e_rep[:, n % 2, :], s_own[:, n % 2, :], start=False, stop=True)
                mm.then_inc(win_done, 1)
            if seg_out:
                pe.wait_ge(r_copied, NQ)
                for n in range(H):
                    m = n // NO
                    pe.matmul(psX[0][:, n:n + 1], wqT[:, m, :], d_own[:, n:n + 1], start=True, stop=True)
                    mm = pe.matmul(psX[0][:, H + n:H + n + 1], s_rep[:, m, :], d_own[:, n:n + 1], start=True, stop=True)
                mm.then_inc(seg_done, 1)
            pe.wait_ge(win_copied, H)
            pe.wait_ge(cst_copied, H)
            if seg_out:
                pe.wait_ge(seg_copied, 1)
            with pe.Fori(0, turns) as t:
                for s in range(2):
                    pe.wait_ge(x_loaded[s].sem, x_loaded[s].at(t, 32))
                    pe.wait_ge(copied.sem, copied.at(t, s - 1))
                    pe.transpose(psX[s][:, 0:R2], xi[0:R2, s, :], ident[0:R2, 0:R2]).then_inc(turned.sem, 1)
                for s in range(2):
                    pe.wait_ge(copied.sem, copied.at(t, s + 1))
                    pe.wait_ge(staged.sem, staged.at(t, s - 1))
                    pe.sem_inc(apart_p, 1)
                    for c, (a, b) in enumerate(SPLIT):
                        mm = pe.matmul(ps[s][c][0:R2, 0:(b - a) * WIN], xiT[:, s, 0:R2],
                                       win[:, a:b, bass.ds(first - 2 * s - t * 4, WIN)], start=True, stop=True)
                    mm.then_inc(multiplied.sem, 1)
    ph.close()


def experts_phase(nc, name, turns, x_in, x_out, w):
    ph = Phase(nc, name)
    sb = ph.sbuf
    ident = sb("ident", [P, P])
    halfs = sb("halfs", [P, QUAD])
    number = sb("number", [P, E])
    rw = sb("rw", [P, E])
    rb = sb("rb", [P, E])
    xs = sb("xs", [P, 1])
    xb = sb("xb", [P, 1])
    w1 = sb("w1", [P, E, FF * P])
    b1 = sb("b1", [P, E, FF])
    w2 = sb("w2", [P, E, FF * P])
    b2 = sb("b2", [P, E, P])
    x_raw = sb("x_raw", [P, QUAD, P])
    xc = sb("xc", [P, QUAD, P])
    sq = sb("sq", [P, QUAD, P])
    stat = sb("stat", [P, 3, QUAD])
    hT = sb("hT", [P, QUAD * P])
    logit = sb("logit", [P, QUAD, E])
    best = sb("best", [P, QUAD, 8])
    at_u = sb("at_u", [P, QUAD, 8], U32)
    at_f = sb("at_f", [P, QUAD, 8])
    e2 = sb("e2", [P, 5, QUAD])
    pick = sb("pick", [P, 2, QUAD, E])
    gate = sb("gate", [P, QUAD, E])
    u = sb("u", [P, 2, FF, QUAD * P])
    t_sb = sb("t_sb", [P, 2, QUAD, P])
    acc = sb("acc", [P, QUAD, P])
    ps1 = [ph.psum(f"ps1{i}") for i in range(4)]
    ps2 = [ph.psum(f"ps2{i}") for i in range(2)]
    psM = ph.psum("psM")
    psL = ph.psum("psL")

    zeroed, made, w_in = ph.sem("zeroed"), ph.sem("constants_made"), ph.sem("weights_loaded")
    apart = ph.sem("apart")
    x_loaded = ph.counter("x_loaded", 16)
    steps = ph.counter("norm_steps", 7)
    gate_steps = ph.counter("gate_steps", 12)
    powers = ph.counter("inverse_roots", 1)
    turned = ph.counter("transposed", 1)
    copied = ph.counter("transposed_copied", 1)
    logits = ph.counter("logits", 1)
    gap = ph.counter("logit_gap", 1)
    gap_exp = ph.counter("logit_gap_exponential", 1)
    hidden = ph.counter("hidden", E * FF)
    active = ph.counter("activated", E * FF)
    outs = ph.counter("expert_outputs", E)
    taken = ph.counter("expert_outputs_taken", E)
    mixed = ph.counter("outputs_mixed", E)
    stored = ph.counter("x_stored", 16)
    loads = [(rw[:], w["rw"]), (rb[:], w["rb"]), (xs[:], w["xs"]), (xb[:], w["xb"]), (b1[:], w["b1"]),
             (w1[:], w["w1"]), (w2[:], w["w2"]), (b2[:], w["b2"])]

    with nc.Block() as block:

        @block.gpsimd
        def _(pool):
            make_identity(nc, pool, ident, zeroed, made)
            nc.gpsimd.memset(halfs[:], -0.5).then_inc(made, 1)
            for e in range(E):
                ins = nc.gpsimd.memset(number[:, e:e + 1], float(e))
            ins.then_inc(made, 1)
            with pool.Fori(0, turns) as t:
                pool.wait_ge(steps.sem, steps.at(t, 6))
                nc.gpsimd.tensor_tensor(stat[:, 2, :], stat[:, 1, :], halfs[:], ALU.pow).then_inc(powers.sem, 1)

        @block.sync
        def _(sp):
            for t, src in loads:
                sp.dma_start(t, src).then_inc(w_in, 16)

            def load(t):
                sp.dma_start(x_raw[:], x_in[bass.ds(t * QUAD, QUAD)].rearrange("b p d -> p b d")).then_inc(x_loaded.sem, 16)

            def store(t):
                sp.wait_ge(mixed.sem, mixed.at(t, E))
                sp.dma_start(x_out[bass.ds(t * QUAD, QUAD)].rearrange("b p d -> p b d"), acc[:]).then_inc(stored.sem, 16)

            load(0)
            with sp.Fori(0, turns - 1) as t:
                sp.wait_ge(mixed.sem, mixed.at(t, 1))
                load(t + 1)
                store(t)
            store(turns - 1)
            sp.wait_ge(stored.sem, 16 * turns)

        @block.scalar
        def _(act):
            act.wait_ge(w_in, 16 * len(loads))

            def router(t):
                act.wait_ge(turned.sem, turned.at(t, 1))
                act.wait_ge(hidden.sem, hidden.at(t, 0))
                nc.scalar.activation(hT[:], psM[:], ACT.Identity, bias=xb[:, 0:1], scale=xs[:, 0:1]).then_inc(copied.sem, 1)
                act.wait_ge(gap.sem, gap.at(t, 1))
                nc.scalar.activation(e2[:, 1, :], e2[:, 0, :], ACT.Exp).then_inc(gap_exp.sem, 1)

            def turn(t, first=False, last=False):
                for e in range(E):
                    for f in range(FF):
                        act.wait_ge(hidden.sem, hidden.at(t, e * FF + f + 1))
                        if e >= 2 or not first:
                            act.wait_ge(outs.sem, outs.at(t, 0) + e - 1)
                        nc.scalar.activation(u[:, e % 2, f, :], ps1[f][:], ACT.Gelu, bias=b1[:, e, f:f + 1]
                                             ).then_inc(active.sem, 1)
                if not last:
                    router(t + 1)

            router(0)
            turn(0, first=True)
            with act.Fori(1, turns - 1) as t:
                turn(t)
            turn(turns - 1, last=True)

        @block.tensor
        def _(pe):
            pe.wait_ge(w_in, 16 * len(loads))
            pe.wait_ge(made, 3)

            def transposes(t):
                pe.wait_ge(steps.sem, steps.at(t, 7))
                pe.wait_ge(copied.sem, copied.at(t, 0))
                for b in range(QUAD):
                    mm = pe.transpose(psM[:, b * P:(b + 1) * P], xc[:, b, :], ident[:])
                mm.then_inc(turned.sem, 1)

            def router(t):
                pe.wait_ge(copied.sem, copied.at(t, 1))
                pe.wait_ge(gate_steps.sem, gate_steps.at(t, 0))
                for b in range(QUAD):
                    mm = pe.matmul(psL[:, b * E:(b + 1) * E], hT[:, b * P:(b + 1) * P], rw[:], start=True, stop=True)
                mm.then_inc(logits.sem, 1)

            def first_layer(t, e):
                for f in range(FF):
                    pe.wait_ge(active.sem, active.at(t, (e - 1) * FF + f + 1))
                    pe.matmul(ps1[f][:], w1[:, e, f * P:(f + 1) * P], hT[:], start=True, stop=True
                              ).then_inc(hidden.sem, 1)

            def second_layer(t, e):
                pe.wait_ge(active.sem, active.at(t, (e + 1) * FF))
                pe.wait_ge(taken.sem, taken.at(t, e - 1))
                for b in range(QUAD):
                    for f in range(FF):
                        mm = pe.matmul(ps2[e % 2][:, b * P:(b + 1) * P], u[:, e % 2, f, b * P:(b + 1) * P],
                                       w2[:, e, f * P:(f + 1) * P], start=(f == 0), stop=(f == FF - 1))
                mm.then_inc(outs.sem, 1)

            def turn(t, last=False):
                for e in range(E):
                    if e + 1 < E:
                        first_layer(t, e + 1)
                    elif not last:
                        router(t + 1)
                        first_layer(t + 1, 0)
                    second_layer(t, e)
                    if e == E - 3 and not last:
                        transposes(t + 1)

            transposes(0)
            router(0)
            first_layer(0, 0)
            with pe.Fori(0, turns - 1) as t:
                turn(t)
            turn(turns - 1, last=True)

        @block.vector
        def _(dve):
            v = nc.vector
            dve.wait_ge(w_in, 16 * len(loads))
            dve.wait_ge(made, 3)

            def norm(t, part):
                step = Steps(dve, steps, t)
                if part == 0:
                    dve.wait_ge(x_loaded.sem, x_loaded.at(t, 16))
                    step(v.reduce_sum(stat[:, 0, :], x_raw[:], AX_X))
                    step(v.tensor_scalar(stat[:, 0, :], stat[:, 0, :], 1.0 / P, None, ALU.mult))
                    dve.wait_ge(turned.sem, turned.at(t, 0))
                    step(v.tensor_tensor(xc[:], x_raw[:], over(stat[:, 0, :], 2, P), ALU.subtract))
                if part == 1:
                    step.k = 3
                    step(v.tensor_tensor(sq[:], xc[:], xc[:], ALU.mult))
                    step(v.reduce_sum(stat[:, 1, :], sq[:], AX_X))
                    step(v.tensor_scalar(stat[:, 1, :], stat[:, 1, :], 1.0 / P, w["eps"], ALU.mult, ALU.add))
                if part == 2:
                    step.k = 6
                    dve.wait_ge(powers.sem, powers.at(t, 1))
                    step(v.tensor_tensor(xc[:], xc[:], over(stat[:, 2, :], 2, P), ALU.mult))
                    step.end()

            def choose(t):
                step = Steps(dve, gate_steps, t)
                dve.wait_ge(logits.sem, logits.at(t, 1))
                step(v.tensor_tensor(logit[:], psL[:, 0:QUAD * E].rearrange("p (b e) -> p b e", b=QUAD),
                                     over(rb[:], 1, QUAD), ALU.add))
                dve.sem_inc(apart, 1)
                for b in range(QUAD):
                    ins = v.max(best[:, b, :], logit[:, b, :])
                step(ins)
                dve.sem_inc(apart, 1)
                for b in range(QUAD):
                    ins = v.max_index(at_u[:, b, :], best[:, b, :], logit[:, b, :])
                step(ins)
                dve.wait_ge(gap_exp.sem, gap_exp.at(t, 0))
                v.tensor_tensor(e2[:, 0, :], best[:, :, 1], best[:, :, 0], ALU.subtract).then_inc(gap.sem, 1)
                step(v.tensor_copy(at_f[:], at_u[:]))
                dve.wait_ge(gap_exp.sem, gap_exp.at(t, 1))
                step(v.tensor_scalar(e2[:, 2, :], e2[:, 1, :], 1.0, None, ALU.add))
                step(v.reciprocal(e2[:, 3, :], e2[:, 2, :]))
                step(v.tensor_tensor(e2[:, 4, :], e2[:, 3, :], e2[:, 1, :], ALU.mult))

            def gates(t):
                step = Steps(dve, gate_steps, t)
                step.k = 7
                for i in range(2):
                    step(v.tensor_tensor(pick[:, i], over(at_f[:, :, i], 2, E), over(number[:], 1, QUAD), ALU.is_equal))
                    step(v.tensor_tensor(pick[:, i], pick[:, i], over(e2[:, 3 + i, :], 2, E), ALU.mult))
                dve.wait_ge(mixed.sem, mixed.at(t, 0))
                step(v.tensor_tensor(gate[:], pick[:, 0], pick[:, 1], ALU.add))
                step.end()

            def mix(t, e):
                dve.wait_ge(outs.sem, outs.at(t, e + 1))
                v.tensor_tensor(t_sb[:, e % 2], ps2[e % 2][:].rearrange("p (b d) -> p b d", b=QUAD),
                                over(b2[:, e, :], 1, QUAD), ALU.add).then_inc(taken.sem, 1)
                dve.wait_ge(taken.sem, taken.at(t, e + 1))
                dve.wait_ge(mixed.sem, mixed.at(t, e))
                if e == 0:
                    dve.wait_ge(stored.sem, stored.at(t, 0))
                for b in range(QUAD):
                    ins = v.scalar_tensor_tensor(out=acc[:, b, :], in0=t_sb[:, e % 2, b, :], scalar=gate[:, b, e:e + 1],
                                                 in1=(acc if e else x_raw)[:, b, :], op0=ALU.mult, op1=ALU.add)
                ins.then_inc(mixed.sem, 1)

            def turn(t, last=False):
                for e in range(E):
                    if e == E - 1 and not last:
                        choose(t + 1)
                    mix(t, e)
                    if not last and 2 <= e < 5:
                        norm(t + 1, e - 2)
                if not last:
                    gates(t + 1)

            for part in range(3):
                norm(0, part)
            choose(0)
            gates(0)
            with dve.Fori(0, turns - 1) as t:
                turn(t)
            turn(turns - 1, last=True)
    ph.close()


def build(nc, a, out, turns=16, layers=9):
    B = turns * QUAD
    x = [nc.dram_tensor(f"x_{i}", [B, P, P], F32, kind="Internal").ap() for i in range(6)]
    pos = nc.dram_tensor("shifted_scores", [B, P, ROW], F32, kind="Internal").ap()
    seg = nc.dram_tensor("segment_terms", [2, P, H], F32, kind="Internal").ap()
    row = lambda name: a[name].rearrange("(o d) -> o d", o=1).broadcast_to([P, a[name].shape[0]])
    col = lambda name: a[name].rearrange("(d o) -> d o", o=1)
    ctxT = a["ctxT"]
    dst = lambda i: out if i == layers else x[i]

    position_phase(nc, "pos0", B, a["x"], pos, dict(
        wr=a["L0_Wr"], wqT=a["L0_WqT"], peT=a["L0_peT"], own=a["own64"], pb=a["L0_pb"], sb=a["L0_sb"],
        cb=a["L0_cb"], se0=a["L0_se0"], se1=a["L0_se1"]), big=True, first=P - 1, seg_out=seg)
    attention_phase(nc, "att0", turns, a["x"], out if layers == 0 else x[0], dict(
        wq=a["L0_Wq"], wk=a["L0_Wk"], wv=a["L0_Wv"], wo=a["L0_Wo"], bq=a["L0_cb"], bk=a["L0_se0"],
        w1=a["L0_W1"], b1=a["L0_b1"], w2=a["L0_W2"], g1=row("L0_g1"), be1=row("L0_be1"), b2=row("L0_b2"),
        g2=row("L0_g2"), be2=row("L0_be2"), eps1=1e-12, eps2=1e-12,
        seg_w=seg[0], seg_c=seg[1], seg_m=a["seg_mask"], neg_m=a["mask"]),
        dim=64, keys=S2, ctxT=ctxT, pos=pos, post=ACT.Relu, scale=0.125, segments=True)
    if layers == 0:
        return
    attention_phase(nc, "att1", turns, x[0], out if layers == 1 else x[1], dict(
        wq=a["L1_wq"], wk=a["L1_wk"], wv=a["L1_wv"], wo=a["L1_wo"], xs=col("L1_norm_w"), eps=1e-6),
        dim=64, keys=S2, ctxT=ctxT, pre="rms")
    if layers == 1:
        return
    position_phase(nc, "pos2", B, x[1], pos, dict(
        wr=a["L2_w_r"], wqT=a["L2_w_qT"], peT=a["L2_peT"], own=a["own8"], pb=a["L2_rr"]), big=False, first=P - 2)
    attention_phase(nc, "att2", turns, x[1], out if layers == 2 else x[2], dict(
        wq=a["L2_w_q"], wk=a["L2_w_k"], wv=a["L2_w_v"], wo=a["L2_w_o"], bq=a["L2_rw"], own=a["own8"],
        w1=a["L2_W1"], b1=a["L2_b1"], w2=a["L2_W2"], g1=row("L2_g1"), be1=row("L2_be1"), b2=row("L2_b2"),
        g2=row("L2_g2"), be2=row("L2_be2"), eps1=1e-9, eps2=1e-9),
        dim=8, keys=S2, ctxT=ctxT, pos=pos, post=ACT.Gelu_apprx_tanh, scale=8.0 ** -0.5)
    if layers == 2:
        return
    attention_phase(nc, "att3", turns, x[2], out if layers == 3 else x[3], dict(
        wq=a["sa_wq"], wk=a["sa_wk"], wv=a["sa_wv"], wo=a["sa_wo"], bq=a["sa_bq"], bk=a["sa_bk"], bv=row("sa_bv"),
        bo=row("sa_bo"), own=a["own8"], xs=col("sa_g"), xb=col("sa_b"), eps=1e-5),
        dim=8, keys=P, pre="ln", scale=8.0 ** -0.5)
    if layers == 3:
        return
    attention_phase(nc, "att4", turns, x[3], out if layers == 4 else x[4], dict(
        wq=a["ca_wq"], wk=a["ca_wk"], wv=a["ca_wv"], wo=a["ca_wo"], bq=a["ca_bq"], bk=a["ca_bk"], bv=row("ca_bv"),
        bo=row("ca_bo"), own=a["own8"], xs=col("ca_qg"), xb=col("ca_qb"), cs=col("ca_kg"), cb=col("ca_kb"),
        eps=1e-5, ceps=1e-5), dim=8, keys=S2, ctx=a["ctx"], pre="ln", scale=8.0 ** -0.5)
    if layers == 4:
        return
    experts_phase(nc, "moe", turns, x[4], out, dict(
        rw=a["rwT"], rb=row("rb"), xs=col("moe_g"), xb=col("moe_b"), w1=a["e_w1"], b1=a["e_b1"], w2=a["e_w2"],
        b2=a["e_b2"].rearrange("(o e) d -> o (e d)", o=1).broadcast_to([P, E * P]).rearrange("p (e d) -> p e d", e=E), eps=1e-5))


def lay_out(i):
    A = np.ascontiguousarray
    L0, L1, L2, L3 = (lambda n, k=k: np.asarray(i[f"L{k}_xattn_{n}"]) for k in range(4))
    o = {}
    o["x"] = np.asarray(i["x"])
    o["ctx"] = np.asarray(i["ctx_1024"])
    o["ctxT"] = o["ctx"].transpose(0, 2, 1)
    o["mask"] = np.asarray(i["mask_1x1xSxS2_ff0"])[0, 0]
    o["seg_mask"] = np.asarray(i["mask_1xSxS2_bk1"])[0]
    o["own64"] = np.repeat(np.eye(2, dtype=np.float32), 64, axis=0)
    o["own8"] = np.repeat(np.eye(H, dtype=np.float32), 8, axis=0)
    chunk = lambda m: m.reshape(-1, P, m.shape[-1]).transpose(1, 0, 2)
    heads = lambda m: m.reshape(-1, P).T
    for n in ("Wq", "Wk", "Wv", "Wr"):
        o["L0_" + n] = L0(n).reshape(P, -1)
    o["L0_WqT"] = chunk(o["L0_Wq"].T)
    o["L0_Wo"] = chunk(L0("Wo").reshape(P, -1).T).reshape(P, -1)
    o["L0_peT"] = L0("position_encoding")[0, :RP].T
    for n, s in (("pb", L0("position_bias")), ("sb", L0("segment_bias")), ("cb", L0("content_bias")),
                 ("se0", L0("segment_encoding")[0]), ("se1", L0("segment_encoding")[1])):
        o["L0_" + n] = heads(s)
    o["L0_W1"], o["L0_b1"], o["L0_W2"] = L0("W1"), heads(L0("b1")), chunk(L0("W2"))
    o["L0_b2"], o["L0_g1"], o["L0_be1"], o["L0_g2"], o["L0_be2"] = (
        L0("b2"), L0("ln1_gamma"), L0("ln1_beta"), L0("ln2_gamma"), L0("ln2_beta"))
    for n in ("wq", "wk", "wv"):
        o["L1_" + n] = L1(n)
    o["L1_wo"] = chunk(L1("wo")).reshape(P, -1)
    o["L1_norm_w"] = L1("norm_w")
    for n in ("w_q", "w_k", "w_v", "w_r"):
        o["L2_" + n] = L2(n).reshape(P, P)
    o["L2_w_qT"] = chunk(o["L2_w_q"].T)

    def spaced(m):
        s = np.zeros((G, 32, G, P), np.float32)
        s[:, :8] = m.reshape(G, G, 8, P).transpose(1, 2, 0, 3)
        return s.reshape(P, G * P)

    o["L2_w_o"] = spaced(L2("w_o").reshape(P, P))
    pe = L2("pos_emb")
    at = (np.arange(204) - 51) % pe.shape[0]
    o["L2_peT"] = np.concatenate([pe[at], pe[:1]]).T
    o["L2_rw"], o["L2_rr"] = heads(L2("r_w_bias")), heads(L2("r_r_bias"))
    o["L2_W1"], o["L2_b1"], o["L2_W2"] = L2("ffn_w1"), heads(L2("ffn_b1")), chunk(L2("ffn_w2"))
    o["L2_b2"], o["L2_g1"], o["L2_be1"], o["L2_g2"], o["L2_be2"] = (
        L2("ffn_b2"), L2("ln1_g"), L2("ln1_b"), L2("ln2_g"), L2("ln2_b"))
    for k in ("sa", "ca"):
        iw, ib = L3(f"{k}_in_w"), L3(f"{k}_in_b")
        o[f"{k}_wq"], o[f"{k}_wk"], o[f"{k}_wv"] = iw[:P].T, iw[P:2 * P].T, iw[2 * P:].T
        o[f"{k}_bq"], o[f"{k}_bk"], o[f"{k}_bv"] = ib[:P, None], ib[P:2 * P, None], ib[2 * P:]
        o[f"{k}_wo"] = spaced(L3(f"{k}_out_w").T)
        o[f"{k}_bo"] = L3(f"{k}_out_b")
    o["sa_g"], o["sa_b"] = L3("sa_ln_g"), L3("sa_ln_b")
    o["ca_qg"], o["ca_qb"], o["ca_kg"], o["ca_kb"] = L3("ca_q_ln_g"), L3("ca_q_ln_b"), L3("ca_kv_ln_g"), L3("ca_kv_ln_b")
    o["moe_g"], o["moe_b"], o["rwT"], o["rb"] = L3("moe_ln_g"), L3("moe_ln_b"), L3("router_w").T, L3("router_b")
    o["e_w1"] = L3("e_fc1_w").transpose(2, 0, 1)
    o["e_b1"] = L3("e_fc1_b").reshape(E, FF, P).transpose(2, 0, 1)
    o["e_w2"] = L3("e_fc2_w").reshape(E, P, FF, P).transpose(3, 0, 2, 1).reshape(P, E, FF * P)
    o["e_b2"] = L3("e_fc2_b")
    return {k: A(v) for k, v in o.items()}


def kernel(**inputs):
    import concourse.bacc as bacc
    from concourse.bass_utils import run_bass_kernel_spmd

    arrays = lay_out(inputs)
    nc = bacc.Bacc("TRN2", target_bir_lowering=False, num_devices=1)
    args = {n: nc.dram_tensor(f"in_{n}", v.shape, mybir.dt.from_np(v.dtype), kind="ExternalInput").ap()
            for n, v in arrays.items()}
    out = nc.dram_tensor("out_0", (64, P, P), F32, kind="ExternalOutput").ap()
    build(nc, args, out)
    r = run_bass_kernel_spmd(nc, [{f"in_{n}": v for n, v in arrays.items()}], core_ids=[0])
    return r.results[0]["out_0"]
```

```python
from contextlib import ExitStack

import concourse.bass as bass
import numpy as np
from concourse import mybir

ALU = mybir.AluOpType
ACT = mybir.ActivationFunctionType
F32 = mybir.dt.float32
U8 = mybir.dt.uint8
U32 = mybir.dt.uint32
AX_X = mybir.AxisListType.X

P = 128
S2 = 77
H = 16
G = 4
QUAD = 4
FF = 4
E = 8
ROW = 1280
ROW0 = 8
AT_ONCE = 4
WIN = S2 + 1
RP = 205
NEG = 1e30
LAG = 3
NB = LAG + 2
CTX_NORM = (3, 5, 7)
X_NORM = (7, 9, 11)
CTX_TURN = 8
X_TURN = 13
X_TURN_RAW = 4
Y_NORM = (3, 4, 5, 5)
Y_TURN = 7
HIDDEN = 8
FF_OUT = 13
Z_NORM = (14, 15, 16)
KEYS_TURN = 14
KEYS_TURN_POST = 12
QUERY_TURN = 15
VALUE_TURN = 19
HEAD = 2
HEAD_POST = 3
HEAD_NARROW = 3
AHEAD = 2


class Signal:

    def __init__(self, handle, per_turn):
        self.sem, self.per_turn, self.made = handle, per_turn, 0

    def at(self, turn, k):
        assert k <= self.per_turn
        return turn * self.per_turn + max(k, 0)


class Phase:

    def __init__(self, nc, name):
        self.nc, self.name, self.stack, self.sems = nc, name, ExitStack(), []

    def sbuf(self, name, shape, dtype=F32):
        return self.stack.enter_context(self.nc.sbuf_tensor(f"{self.name}_{name}", shape, dtype))

    def psum(self, name):
        return self.stack.enter_context(self.nc.psum_tensor(f"{self.name}_{name}", [P, 512], F32))

    def sem(self, name):
        s = self.nc.alloc_semaphore(f"{self.name}_{name}")
        self.sems.append(s)
        return s

    def counter(self, name, per_turn):
        return Signal(self.sem(name), per_turn)

    def close(self):
        self.stack.close()
        self.nc.clear_and_free_semaphores(self.sems)
        self.nc.all_engine_barrier()


def over(ap, axis, n):
    u = ap.unsqueeze(axis)
    shape = list(u.shape)
    shape[axis] = n
    return u.broadcast_to(shape)


def make_identity(nc, pool, ident, zeroed, made):
    nc.gpsimd.memset(ident[:], 0.0).then_inc(zeroed, 1)
    pool.wait_ge(zeroed, 1)
    nc.gpsimd.affine_select(out=ident[:], in_=ident[:], compare_op=ALU.not_equal, fill=1.0, base=0,
                            pattern=[[-1, P]], channel_multiplier=1).then_inc(made, 1)


class Steps:

    def __init__(self, eng, count, turn):
        self.eng, self.count, self.turn, self.k = eng, count, turn, 0

    def __call__(self, ins):
        self.k += 1
        ins.then_inc(self.count.sem, 1)
        self.eng.wait_ge(self.count.sem, self.count.at(self.turn, self.k))

    def end(self):
        assert self.k == self.count.per_turn, (self.k, self.count.per_turn)


def attention_phase(nc, name, turns, x_in, x_out, w, *, dim, keys, ctxT=None, ctx=None, pos=None,
                    pre=None, kv_bias=False, post=None, scale=1.0, segments=None):
    big = dim == 64
    NQ = 8 if big else 1
    W = 2 * keys if big else G * keys
    GK = G * keys
    self_kv = ctxT is None and ctx is None
    ph = Phase(nc, name)
    sb = ph.sbuf

    ident = sb("ident", [P, P])
    halfs = sb("halfs", [P, QUAD])
    wq = sb("wq", [P, NQ * P])
    wk = sb("wk", [P, NQ * P])
    wv = sb("wv", [P, NQ * P])
    wo = sb("wo", [P, (NQ if big else G) * P])
    bq = sb("bq", [P, NQ]) if "bq" in w else None
    bk = sb("bk", [P, NQ]) if "bk" in w else None
    bv = sb("bv", [P, P]) if "bv" in w else None
    bo = sb("bo", [P, P]) if "bo" in w else None
    xs = sb("xs", [P, 1]) if "xs" in w else None
    xb = sb("xb", [P, 1]) if "xb" in w else None
    cs = sb("cs", [P, 1]) if "cs" in w else None
    cb = sb("cb", [P, 1]) if "cb" in w else None
    own = None if big else sb("own", [P, H])
    if post:
        w1 = sb("w1", [P, FF * P])
        b1 = sb("b1", [P, FF])
        w2 = sb("w2", [P, FF, P])
        rows = sb("rows", [P, 5, P])
    if segments:
        seg_w = sb("seg_w", [P, H])
        seg_c = sb("seg_c", [P, H])
        seg_m8 = sb("seg_m8", [P, S2], U8)
        seg_m = sb("seg_m", [P, S2])
        neg_m = sb("neg_m", [P, S2])

    x_raw = sb("x_raw", [P, QUAD, P])
    x_res = sb("x_res", [P, QUAD, P])
    x_nrm = sb("x_nrm", [P, QUAD, P]) if pre else x_raw
    x_sq = sb("x_sq", [P, QUAD, P])
    stat = sb("stat", [P, 8, QUAD])
    xT = sb("xT", [P, QUAD * P])
    if ctx is not None:
        c_raw = sb("c_raw", [keys, QUAD, P])
        c_nrm = sb("c_nrm", [keys, QUAD, P])
        kvT = sb("kvT", [P, QUAD * keys])
    elif self_kv:
        kvT = xT
    else:
        kvT = sb("kvT", [P, QUAD * keys])
    qT = sb("qT", [P, NQ, QUAD * P])
    if big:
        k_bd = sb("k_bd", [P, NQ, QUAD, 2 * keys])
        v_sb = sb("v_sb", [keys, QUAD, NQ * P])
        VW = dim
    else:
        kT = sb("kT", [P, QUAD, keys])
        k_bd = sb("k_bd", [P, 2, H, keys])
        v_sb = sb("v_sb", [keys, QUAD, H, 32])
        VW = 32
    if pos is not None:
        p_sb = sb("p_sb", [P, 2, H * WIN])
    if segments:
        seg_d = sb("seg_d", [P, QUAD, H])
        seg_t = sb("seg_t", [P, G, S2])
    sc = sb("sc", [P, NB, GK]) if pos is not None else None
    ex = sb("ex", [P, NB, GK])
    pr = sb("pr", [P, NB, GK])
    mx = sb("mx", [P, NB, G])
    sm = sb("sm", [P, NB, G])
    rc = sb("rc", [P, NB, G])
    pT = sb("pT", [keys, 2, G * P])
    oT = sb("oT", [P, 2, 2 * P if big else P])
    h = sb("h", [P, QUAD, P])
    y = sb("y", [P, QUAD, P]) if post else None
    x_new = sb("x_new", [P, QUAD, P]) if post else h
    if post:
        yT = sb("yT", [P, QUAD * P])
        u = sb("u", [P, FF, QUAD * P])
    OC = 2 if big else 1

    psS = [ph.psum("psS0"), ph.psum("psS1")]
    psT = [ph.psum("psT0"), ph.psum("psT1")]
    psO = [ph.psum("psO0"), ph.psum("psO1")]
    psA = ph.psum("psA")
    psM = ph.psum("psM")
    gelu = post not in (None, ACT.Relu)

    UN = 4 * QUAD
    zeroed = ph.sem("zeroed")
    consts = ph.sem("consts_made")
    w_in = ph.sem("weights_loaded")
    late_in = ph.sem("late_weights_loaded")
    m_done = ph.sem("mask_terms_made")
    apart = ph.sem("apart")
    x_in_s = ph.counter("x_loaded", 16)
    c_in_s = ph.counter("ctx_loaded", 16)
    pos_in = [ph.counter(f"pos_loaded{i}", 16 * 2) for i in range(2)]
    res_in = ph.counter("residual_loaded", 16)
    NS = {"ln": 7, "rms": 4, None: 0}[pre] + (7 if ctx is not None else 0)
    pre_steps = ph.counter("norm_steps", NS)
    pre_powers = ph.counter("norm_inverse_roots", (1 if pre else 0) + (1 if ctx is not None else 0))
    steps = ph.counter("vector_steps", 21 if post else 1 if bo is None else 2)
    powers = ph.counter("inverse_roots", 2 if post else 0)
    normed = ph.counter("x_normed", 1)
    c_normed = ph.counter("ctx_normed", 1)
    turned = ph.counter("transposed", 2 if ctx is not None else 1)
    turned_out = ph.counter("transposed_copied", 2 if ctx is not None else 1)
    y_turned = ph.counter("y_transposed", 1)
    y_copied = ph.counter("y_transposed_copied", 1)
    seg_made = ph.counter("segment_products", 1)
    seg_out = ph.counter("segment_coefficients", 1)
    seg_inner = ph.counter("segment_steps", 2 * UN)
    seg_used = ph.counter("segments_added", UN)
    NA = NQ + (QUAD if big else 0)
    NV = 2 if not big else NQ + QUAD
    proj_a = ph.counter("projection_a", NA)
    proj_a_out = ph.counter("projection_a_copied", NA)
    proj_v = ph.counter("projection_v", NV)
    keys_out = ph.counter("keys_projection_copied", 1)
    v_out = ph.counter("values_copied", QUAD if big else 1)
    k_half = ph.counter("keys_even_heads", NQ)
    k_copied = ph.counter("keys_odd_heads", NQ)
    k_made = ph.counter("keys_spread", 2 * QUAD)
    scored = ph.counter("scores", UN)
    added = ph.counter("position_scores_added", UN)
    found = ph.counter("maxima_found", UN)
    maxed = ph.counter("maxima", UN)
    exped = ph.counter("exponentials", UN)
    left = added if pos is not None else exped
    summed = ph.counter("sums_inverted", UN)
    probs = ph.counter("probabilities", UN)
    p_turned = ph.counter("probabilities_transposed", UN)
    p_copied = ph.counter("probabilities_copied", UN)
    headed = ph.counter("head_outputs", UN)
    h_copied = ph.counter("head_outputs_copied", UN)
    woed = ph.counter("output_products", UN)
    ffn1 = ph.counter("ff_hidden", FF)
    ffn1_out = ph.counter("ff_activated", FF)
    ffn_act = ph.counter("ff_gelu", 1)
    ffn2 = ph.counter("ff_out", 1)
    ffn2_read = ph.counter("ff_out_read", 1)
    a_read = ph.counter("psA_read", 1)
    res_used = ph.counter("residual_added", 1)
    normed_y = ph.counter("y_normed", 1)
    done = ph.counter("turn_done", 1)
    x_stored = ph.counter("x_stored", 16)

    loads = [(wq, w["wq"]), (wk, w["wk"]), (wv, w["wv"])]
    for t, n in ((bq, "bq"), (bk, "bk"), (bv, "bv"), (bo, "bo"), (xs, "xs"), (xb, "xb"), (cs, "cs"), (cb, "cb"),
                 (own, "own")):
        if t is not None:
            loads.append((t, w[n]))
    late = [(wo, w["wo"])]
    if post:
        late += [(w1, w["w1"]), (b1, w["b1"]), (w2, w["w2"])]
        late += [(rows[:, i, :], w[n]) for i, n in enumerate(("g1", "be1", "b2", "g2", "be2"))]
    if segments:
        loads += [(seg_w, w["seg_w"]), (seg_c, w["seg_c"]), (seg_m8, w["seg_m"]), (neg_m, w["neg_m"])]
    CONSTS = 3
    heads_first = HEAD_NARROW if not big else HEAD_POST if post else HEAD
    x_turn = X_TURN if pre else X_TURN_RAW
    k_turn = KEYS_TURN_POST if post else KEYS_TURN
    UNITS = UN + LAG + 2

    with nc.Block() as block:

        @block.sync
        def _(sp):
            def load(t, first=False):
                if not first:
                    sp.wait_ge(turned.sem, turned.at(t, 0))
                sp.dma_start(x_raw[:], x_in[bass.ds(t * QUAD, QUAD)].rearrange("b p d -> p b d")).then_inc(x_in_s.sem, 16)
                if ctx is not None:
                    if not first:
                        sp.wait_ge(turned.sem, turned.at(t - 1, 1))
                    sp.dma_start(c_raw[:], ctx[bass.ds(t * QUAD, QUAD)].rearrange("b p d -> p b d")).then_inc(c_in_s.sem, 16)
                elif ctxT is not None:
                    if not first:
                        sp.wait_ge(proj_a.sem, proj_a.at(t, 0))
                        sp.sem_inc(apart, 1)
                        sp.wait_ge(proj_v.sem, proj_v.at(t, 0))
                        sp.sem_inc(apart, 1)
                    sp.dma_start(kvT[:].rearrange("p (b k) -> p b k", b=QUAD),
                                 ctxT[bass.ds(t * QUAD, QUAD)].rearrange("b p k -> p b k")).then_inc(c_in_s.sem, 16)

            def load_res(t, first=False):
                if not first:
                    sp.wait_ge(res_used.sem, res_used.at(t, 0))
                sp.dma_start(x_res[:], x_in[bass.ds(t * QUAD, QUAD)].rearrange("b p d -> p b d")).then_inc(res_in.sem, 16)

            def load_pos(t, b, first=False):
                if pos is None:
                    return
                if not first:
                    sp.wait_ge(added.sem, added.at(t, 0) + 4 * (b - 1))
                sp.dma_start(p_sb[:, b % 2, 0:H * WIN - 1],
                             pos[bass.ds(t * QUAD + b, 1), :, ROW0:ROW0 + H * WIN - 1].rearrange("b p n -> p (b n)")
                             ).then_inc(pos_in[b % 2].sem, 16)

            def turn(t, first=False, last=False):
                if not last:
                    load(t + 1)
                load_res(t, first)
                load_pos(t, 2)
                load_pos(t, 3)
                if not last:
                    load_pos(t + 1, 0)
                    load_pos(t + 1, 1)
                if not first:
                    store(t - 1)

            def store(t):
                sp.wait_ge(done.sem, done.at(t, 1))
                sp.dma_start(x_out[bass.ds(t * QUAD, QUAD)].rearrange("b p d -> p b d"), x_new[:]
                             ).then_inc(x_stored.sem, 16)

            load(0, first=True)
            for t, src in loads:
                sp.dma_start(t[:], src).then_inc(w_in, 16)
            load_pos(0, 0, first=True)
            for t, src in late:
                sp.dma_start(t if isinstance(t, bass.AP) else t[:], src).then_inc(late_in, 16)
            load_pos(0, 1, first=True)
            turn(0, first=True)
            with sp.Fori(1, turns - 1) as t:
                turn(t)
            turn(turns - 1, last=True)
            store(turns - 1)
            sp.wait_ge(x_stored.sem, 16 * turns)

        @block.gpsimd
        def _(pool):
            make_identity(nc, pool, ident, zeroed, consts)
            nc.gpsimd.memset(halfs[:], -0.5).then_inc(consts, 1)
            nc.gpsimd.memset(k_bd[:] if big else v_sb[:], 0.0).then_inc(consts, 1)
            pool.wait_ge(w_in, 16 * len(loads))
            if segments:
                pool.wait_ge(m_done, 2)

            def power(t, k, of, to, after=steps, made=powers):
                pool.wait_ge(after.sem, after.at(t, k))
                nc.gpsimd.tensor_tensor(to, of, halfs[0:of.shape[0], :], ALU.pow).then_inc(made.sem, 1)

            def ready(t, i):
                if ctx is not None and i == CTX_NORM[1]:
                    power(t, 6, stat[0:keys, 3, :], stat[0:keys, 4, :], pre_steps, pre_powers)
                if pre and i == X_NORM[1]:
                    power(t, (7 if ctx is not None else 0) + (6 if pre == "ln" else 3), stat[:, 5, :], stat[:, 6, :], pre_steps, pre_powers)

            def spread(t, b, half, first=False):
                hs = slice(half * H // 2, (half + 1) * H // 2)
                pool.wait_ge(keys_out.sem, keys_out.at(t, 1))
                if half == 0 and not first:
                    pool.wait_ge(scored.sem, scored.at(t, 0) + 4 * (b - 1))
                nc.gpsimd.tensor_tensor(k_bd[:, b % 2, hs, :], over(kT[:, b, :], 1, H // 2),
                                        over(own[:, hs], 2, keys), ALU.mult).then_inc(k_made.sem, 1)

            def add_segments(t, i):
                b, hs = i // 4, slice(G * (i % 4), G * (i % 4) + G)
                if i % 4 == 0:
                    pool.wait_ge(pos_in[b % 2].sem, pos_in[b % 2].at(t, 16 * (b // 2 + 1)))
                if i == 0:
                    pool.wait_ge(seg_out.sem, seg_out.at(t, 1))
                pv = p_sb[:, b % 2, :].rearrange("p (n j) -> p n j", n=H)[:, hs, 0:S2]
                pool.wait_ge(seg_used.sem, seg_used.at(t, i))
                nc.gpsimd.tensor_tensor(seg_t[:], over(seg_m[:], 1, G), over(seg_d[:, b, hs], 2, S2), ALU.mult
                                        ).then_inc(seg_inner.sem, 1)
                pool.wait_ge(seg_inner.sem, seg_inner.at(t, 2 * i + 1))
                nc.gpsimd.tensor_tensor(seg_t[:], seg_t[:], over(neg_m[:], 1, G), ALU.add).then_inc(seg_inner.sem, 1)
                pool.wait_ge(seg_inner.sem, seg_inner.at(t, 2 * i + 2))
                nc.gpsimd.tensor_tensor(pv, pv, seg_t[:], ALU.add).then_inc(seg_used.sem, 1)

            def finish(t, i):
                if i == Y_NORM[1]:
                    power(t, 7, stat[:, 1, :], stat[:, 2, :])
                if i == Z_NORM[1]:
                    power(t, 18, stat[:, 1, :], stat[:, 2, :])

            def start(t):
                for i in range(heads_first + AHEAD if segments else 0):
                    add_segments(t, i)

            def turn(t, first=False, last=False):
                for i in range(UN):
                    if segments and i >= heads_first and i + AHEAD < UN:
                        add_segments(t, i + AHEAD)
                    pool.wait_ge(summed.sem, summed.at(t, i + 1))
                    pool.wait_ge(p_turned.sem, p_turned.at(t, i + 1 - NB))
                    nc.gpsimd.tensor_tensor(pr[:, i % NB, :].rearrange("p (h k) -> p h k", h=G),
                                            ex[:, i % NB, :].rearrange("p (h k) -> p h k", h=G),
                                            over(rc[:, i % NB, :], 2, keys), ALU.mult).then_inc(probs.sem, 1)
                    if not big and i in (2, 3, 6, 7):
                        spread(t, 2 + i // 4, i % 2)
                    if post and not first:
                        finish(t - 1, i + 1)
                    if not last:
                        ready(t + 1, i + 1)
                    if not big and not last and i >= UN - 2:
                        spread(t + 1, 0, i - UN + 2)
                if not big and not last:
                    spread(t + 1, 1, 0)
                    spread(t + 1, 1, 1)
                if not last:
                    start(t + 1)

            for i in range(UN):
                ready(0, i)
            if not big:
                for b in range(2):
                    for half in range(2):
                        spread(0, b, half, first=True)
            start(0)
            turn(0, first=True)
            with pool.Fori(1, turns - 1) as t:
                turn(t)
            turn(turns - 1, last=True)
            if post:
                for i in range(UN):
                    finish(turns - 1, i)

        @block.scalar
        def _(act):
            act.wait_ge(w_in, 16 * len(loads))

            def ready(t, i):
                if ctx is not None and i == CTX_TURN:
                    act.wait_ge(turned.sem, turned.at(t, 1))
                    nc.scalar.activation(kvT[:], psM[:, 0:QUAD * keys], ACT.Identity, bias=cb[:, 0:1],
                                         scale=cs[:, 0:1]).then_inc(turned_out.sem, 1)
                if i == x_turn:
                    act.wait_ge(turned.sem, turned.at(t, 2 if ctx is not None else 1))
                    nc.scalar.activation(xT[:], psM[:], ACT.Identity, bias=xb[:, 0:1] if xb is not None else 0.0,
                                         scale=xs[:, 0:1] if xs is not None else 1.0).then_inc(turned_out.sem, 1)

            def copy_q(t, m):
                act.wait_ge(proj_a.sem, proj_a.at(t, m + 1))
                act.wait_ge(scored.sem, scored.at(t, 0))
                nc.scalar.activation(qT[:, m, :], psS[m % 2][:], ACT.Identity,
                                     bias=bq[:, m:m + 1] if bq is not None else 0.0).then_inc(proj_a_out.sem, 1)

            def copy_k(t, m):
                act.wait_ge(proj_v.sem, proj_v.at(t, m + 1))
                act.wait_ge(k_half.sem, k_half.at(t, m + 1))
                src = (psT + psO)[m % 4][64:P, 0:QUAD * keys].rearrange("p (b k) -> p b k", b=QUAD)
                nc.scalar.activation(k_bd[64:P, m, :, keys:2 * keys], src, ACT.Identity,
                                     bias=bk[64:P, m:m + 1] if bk is not None else 0.0).then_inc(k_copied.sem, 1)

            def ahead(t, i):
                if big:
                    d = i - UN
                    for m in range(2 * d - 2, 2 * d):
                        if 0 <= m < NQ:
                            copy_q(t, m)
                    return
                if i == k_turn:
                    act.wait_ge(proj_v.sem, proj_v.at(t, 1))
                    act.wait_ge(k_made.sem, k_made.at(t, 0))
                    nc.scalar.activation(kT[:], psM[:, 0:QUAD * keys].rearrange("p (b k) -> p b k", b=QUAD), ACT.Identity,
                                         bias=bk[:, 0:1] if bk is not None else 0.0).then_inc(keys_out.sem, 1)
                if i == QUERY_TURN + 1:
                    act.wait_ge(proj_a.sem, proj_a.at(t, 1))
                    act.wait_ge(scored.sem, scored.at(t, 0))
                    nc.scalar.activation(qT[:, 0, :], psM[:], ACT.Identity,
                                         bias=bq[:, 0:1] if bq is not None else 0.0).then_inc(proj_a_out.sem, 1)
                if 0 <= i - UN - 1 < heads_first:
                    exponential(t, i - UN - 1)

            def project(t):
                for m in range(NQ if big else 0):
                    copy_k(t, m)
                for i in range(heads_first if big else 0):
                    exponential(t, i)
                if big:
                    for b in range(QUAD):
                        act.wait_ge(proj_a.sem, proj_a.at(t, NQ + b + 1))
                        act.wait_ge(headed.sem, headed.at(t, 0))
                        nc.scalar.activation(v_sb[:, b, 0:512], psO[b % 2][0:keys, :], ACT.Copy).then_inc(proj_a_out.sem, 1)

            def exponential(t, i):
                act.wait_ge(maxed.sem, maxed.at(t, i + 1))
                act.wait_ge(probs.sem, probs.at(t, i + 1 - NB))
                for c in range(G):
                    hs = slice(c * keys, (c + 1) * keys)
                    ins = nc.scalar.activation(ex[:, i % NB, hs], psS[i % 2][:, hs] if pos is None else sc[:, i % NB, hs],
                                               ACT.Exp, bias=mx[:, i % NB, c:c + 1], scale=scale,
                                               accum_out=sm[:, i % NB, c:c + 1])
                ins.then_inc(exped.sem, 1)

            def copy_probs(t, i):
                act.wait_ge(p_turned.sem, p_turned.at(t, i + 1))
                act.wait_ge(headed.sem, headed.at(t, i - 1))
                nc.scalar.activation(pT[:, i % 2, :], psT[i % 2][0:keys, :], ACT.Copy).then_inc(p_copied.sem, 1)

            def copy_heads(t, i):
                act.wait_ge(headed.sem, headed.at(t, i + 1))
                act.wait_ge(woed.sem, woed.at(t, i - 1))
                nc.scalar.activation(oT[:, i % 2, :], psO[i % 2][:, 0:OC * P], ACT.Copy).then_inc(h_copied.sem, 1)

            def finish(t, i):
                if i == Y_TURN:
                    act.wait_ge(y_turned.sem, y_turned.at(t, 1))
                    nc.scalar.activation(yT[:], psM[:], ACT.Copy).then_inc(y_copied.sem, 1)
                if HIDDEN <= i < HIDDEN + FF:
                    f = i - HIDDEN
                    act.wait_ge(ffn1.sem, ffn1.at(t, f + 1))
                    act.wait_ge(ffn2.sem, ffn2.at(t, 0))
                    nc.scalar.activation(u[:, f, :], psM[:], ACT.Identity if gelu else post, bias=b1[:, f:f + 1]
                                         ).then_inc(ffn1_out.sem, 1)
                if i == HIDDEN + FF - 1 and gelu:
                    act.wait_ge(ffn1_out.sem, ffn1_out.at(t, FF))
                    nc.scalar.activation(u[:], u[:], post).then_inc(ffn_act.sem, 1)

            def turn(t, first=False, last=False):
                for i in range(heads_first, UNITS):
                    if LAG <= i < UN + LAG:
                        copy_probs(t, i - LAG)
                    if LAG < i < UN + LAG + 1:
                        copy_heads(t, i - LAG - 1)
                    if i < UN:
                        exponential(t, i)
                    if post and not first:
                        finish(t - 1, i)
                    if not last:
                        ready(t + 1, i)
                        ahead(t + 1, i)
                if not last:
                    project(t + 1)

            for i in range(UNITS):
                ready(0, i)
                ahead(0, i)
            project(0)
            act.wait_ge(late_in, 16 * len(late))
            turn(0, first=True)
            with act.Fori(1, turns - 1) as t:
                turn(t)
            turn(turns - 1, last=True)
            if post:
                for i in range(UN):
                    finish(turns - 1, i)

        @block.tensor
        def _(pe):
            pe.wait_ge(w_in, 16 * len(loads))
            pe.wait_ge(consts, CONSTS)

            def ready(t, i):
                if ctx is not None and i == CTX_TURN:
                    pe.wait_ge(c_normed.sem, c_normed.at(t, 1))
                    pe.wait_ge(turned_out.sem, turned_out.at(t, 0))
                    if not big:
                        pe.wait_ge(v_out.sem, v_out.at(t, 0))
                    for b in range(QUAD):
                        mm = pe.transpose(psM[:, b * keys:(b + 1) * keys], c_nrm[:, b, :], ident[0:keys, 0:keys])
                    mm.then_inc(turned.sem, 1)
                if i == x_turn:
                    if not big:
                        pe.wait_ge(v_out.sem, v_out.at(t, 0))
                    if segments:
                        pe.wait_ge(seg_out.sem, seg_out.at(t, 0))
                    if pre:
                        pe.wait_ge(normed.sem, normed.at(t, 1))
                    else:
                        pe.wait_ge(x_in_s.sem, x_in_s.at(t, 16))
                    pe.wait_ge(turned_out.sem, turned_out.at(t, 1 if ctx is not None else 0))
                    for b in range(QUAD):
                        mm = pe.transpose(psM[:, b * P:(b + 1) * P], x_nrm[:, b, :], ident[:])
                    mm.then_inc(turned.sem, 1)

            def ahead(t, i, first=False):
                if ctxT is not None and i == (UN if big else k_turn):
                    pe.wait_ge(c_in_s.sem, c_in_s.at(t, 16))
                if big:
                    d = i - UN
                    if d == 1:
                        pe.wait_ge(turned_out.sem, turned_out.at(t, turned_out.per_turn))
                        pe.wait_ge(left.sem, left.at(t, 0))
                    for m in range(2 * d - 2, 2 * d):
                        if 0 <= m < NQ:
                            pe.wait_ge(proj_a_out.sem, proj_a_out.at(t, m - 1))
                            pe.matmul(psS[m % 2][:], wq[:, m * P:(m + 1) * P], xT[:], start=True, stop=True
                                      ).then_inc(proj_a.sem, 1)
                    return
                if i == k_turn:
                    pe.wait_ge(turned_out.sem, turned_out.at(t, turned_out.per_turn))
                    if post and not first:
                        pe.wait_ge(ffn1_out.sem, ffn1_out.at(t - 1, 0))
                    pe.matmul(psM[:, 0:QUAD * keys], wk[:], kvT[:], start=True, stop=True).then_inc(proj_v.sem, 1)
                if i == QUERY_TURN:
                    pe.wait_ge(keys_out.sem, keys_out.at(t, 1))
                    if post and not first:
                        pe.wait_ge(ffn2_read.sem, ffn2_read.at(t - 1, 0))
                    pe.matmul(psM[:], wq[:], xT[:], start=True, stop=True).then_inc(proj_a.sem, 1)
                if 0 <= i - UN - 1 < heads_first:
                    scores(t, i - UN - 1)
                if i == VALUE_TURN:
                    pe.wait_ge(proj_a_out.sem, proj_a_out.at(t, 1))
                    for b in range(QUAD):
                        mm = pe.matmul(psM[0:keys, b * P:(b + 1) * P], kvT[:, b * keys:(b + 1) * keys], wv[:],
                                       start=True, stop=True)
                    mm.then_inc(proj_v.sem, 1)

            def project(t, first=False):
                if segments:
                    if not first:
                        pe.wait_ge(ffn2_read.sem, ffn2_read.at(t - 1, 0))
                    for b in range(QUAD):
                        mm = pe.matmul(psM[:, b * H:(b + 1) * H], xT[:, b * P:(b + 1) * P], seg_w[:], start=True, stop=True)
                    mm.then_inc(seg_made.sem, 1)

                for m in range(NQ if big else 0):
                    pe.wait_ge(p_copied.sem, p_copied.at(t, 0))
                    pe.wait_ge(h_copied.sem, h_copied.at(t, 0))
                    pe.wait_ge(k_copied.sem, k_copied.at(t, m - 3))
                    pe.matmul((psT + psO)[m % 4][:, 0:QUAD * keys], wk[:, m * P:(m + 1) * P], kvT[:], start=True, stop=True
                              ).then_inc(proj_v.sem, 1)
                for i in range(heads_first if big else 0):
                    scores(t, i)
                if big:
                    for b in range(QUAD):
                        pe.wait_ge(k_copied.sem, k_copied.at(t, NQ))
                        pe.wait_ge(proj_a_out.sem, proj_a_out.at(t, NQ + b - 1))
                        pe.matmul(psO[b % 2][0:keys, :], kvT[:, b * keys:(b + 1) * keys], wv[:, 0:512],
                                  start=True, stop=True).then_inc(proj_a.sem, 1)
                        pe.wait_ge(v_out.sem, v_out.at(t, b - 1))
                        pe.matmul(psT[b % 2][0:keys, :], kvT[:, b * keys:(b + 1) * keys], wv[:, 512:1024],
                                  start=True, stop=True).then_inc(proj_v.sem, 1)

            def scores(t, i):
                b, g = i // 4, i % 4
                if i == 0:
                    pe.wait_ge(proj_a_out.sem, proj_a_out.at(t, NQ))
                    if big:
                        pe.wait_ge(k_half.sem, k_half.at(t, NQ))
                        pe.wait_ge(k_copied.sem, k_copied.at(t, NQ))
                if not big and g % 2 == 0:
                    pe.wait_ge(k_made.sem, k_made.at(t, 2 * b + g // 2 + 1))
                pe.wait_ge(left.sem, left.at(t, i - 1))
                for j in range(2 if big else 1):
                    m = 2 * g + j if big else 0
                    mm = pe.matmul(psS[i % 2][:, j * W:(j + 1) * W], qT[:, m, b * P:(b + 1) * P],
                                   k_bd[:, m, b, :] if big else k_bd[:, b % 2, G * g:G * (g + 1), :],
                                   start=True, stop=True)
                mm.then_inc(scored.sem, 1)

            def turn_probs(t, i):
                pe.wait_ge(probs.sem, probs.at(t, i + 1))
                pe.wait_ge(p_copied.sem, p_copied.at(t, i - 1))
                if i == 0 and big:
                    pe.wait_ge(v_out.sem, v_out.at(t, QUAD))
                for c in range(G):
                    mm = pe.transpose(psT[i % 2][0:keys, c * P:(c + 1) * P], pr[:, i % NB, c * keys:(c + 1) * keys], ident[:])
                mm.then_inc(p_turned.sem, 1)

            def heads(t, i):
                b, g = i // 4, i % 4
                if i == 0:
                    if big:
                        pe.wait_ge(proj_a_out.sem, proj_a_out.at(t, NA))
                        pe.wait_ge(v_out.sem, v_out.at(t, QUAD))
                    else:
                        pe.wait_ge(v_out.sem, v_out.at(t, 1))
                pe.wait_ge(p_copied.sem, p_copied.at(t, i + 1))
                pe.wait_ge(h_copied.sem, h_copied.at(t, i - 1))
                for c in range(G):
                    n = G * g + c
                    if big:
                        mm = pe.matmul(psO[i % 2][(c % 2) * 64:(c % 2) * 64 + 64, (c // 2) * P:(c // 2 + 1) * P],
                                       v_sb[:, b, n * 64:(n + 1) * 64], pT[:, i % 2, c * P:(c + 1) * P],
                                       start=True, stop=True)
                    else:
                        mm = pe.matmul(psO[i % 2][32 * c:32 * c + 32, 0:P], v_sb[:, b, n, :],
                                       pT[:, i % 2, c * P:(c + 1) * P], start=True, stop=True)
                mm.then_inc(headed.sem, 1)

            def out_product(t, i):
                b, g = i // 4, i % 4
                pe.wait_ge(h_copied.sem, h_copied.at(t, i + 1))
                if i == 0:
                    pe.wait_ge(a_read.sem, a_read.at(t, 0))
                for j in range(OC):
                    m = OC * g + j
                    mm = pe.matmul(psA[:, b * P:(b + 1) * P], oT[:, i % 2, j * P:(j + 1) * P],
                                   wo[:, m * P:(m + 1) * P], start=(m == 0), stop=(m == OC * G - 1))
                mm.then_inc(woed.sem, 1)

            def finish(t, i, last=False):
                if i == Y_TURN:
                    pe.wait_ge(normed_y.sem, normed_y.at(t, 1))
                    if not last:
                        pe.wait_ge(turned_out.sem, turned_out.at(t + 2, 1))
                    for b in range(QUAD):
                        mm = pe.transpose(psM[:, b * P:(b + 1) * P], y[:, b, :], ident[:])
                    mm.then_inc(y_turned.sem, 1)
                if HIDDEN <= i < HIDDEN + FF:
                    f = i - HIDDEN
                    pe.wait_ge(y_copied.sem, y_copied.at(t, 1))
                    pe.wait_ge(ffn1_out.sem, ffn1_out.at(t, f))
                    pe.matmul(psM[:], w1[:, f * P:(f + 1) * P], yT[:], start=True, stop=True).then_inc(ffn1.sem, 1)
                if i == FF_OUT:
                    pe.wait_ge(ffn1_out.sem, ffn1_out.at(t, FF))
                    if not big and not last:
                        pe.wait_ge(keys_out.sem, keys_out.at(t + 2, 1))
                    if gelu:
                        pe.wait_ge(ffn_act.sem, ffn_act.at(t, 1))
                    for b in range(QUAD):
                        for f in range(FF):
                            mm = pe.matmul(psM[:, b * P:(b + 1) * P], u[:, f, b * P:(b + 1) * P], w2[:, f, :],
                                           start=(f == 0), stop=(f == FF - 1))
                    mm.then_inc(ffn2.sem, 1)

            def turn(t, first=False, last=False):
                for i in range(heads_first, UNITS):
                    if i < UN:
                        scores(t, i)
                    if LAG <= i < UN + LAG:
                        turn_probs(t, i - LAG)
                    if LAG < i < UN + LAG + 1:
                        heads(t, i - LAG - 1)
                    if i > LAG + 1:
                        out_product(t, i - LAG - 2)
                    if post and not first:
                        finish(t - 1, i, last)
                    if not last:
                        ready(t + 1, i)
                        ahead(t + 1, i)
                if not last:
                    project(t + 1)

            for i in range(UNITS):
                ready(0, i)
                ahead(0, i, first=True)
            project(0, first=True)
            pe.wait_ge(late_in, 16 * len(late))
            turn(0, first=True)
            with pe.Fori(1, turns - 1) as t:
                turn(t)
            turn(turns - 1, last=True)
            if post:
                for i in range(UN):
                    finish(turns - 1, i, last=True)

        @block.vector
        def _(dve):
            v = nc.vector
            dve.wait_ge(w_in, 16 * len(loads))
            dve.wait_ge(consts, CONSTS)
            if segments:
                v.tensor_copy(seg_m[:], seg_m8[:]).then_inc(m_done, 1)
                v.tensor_scalar(neg_m[:], neg_m[:], -NEG / scale, None, ALU.mult).then_inc(m_done, 1)

            def mean_off(step, src, st, xc):
                p = src.shape[0]
                step(v.reduce_sum(st[0:p, 0, :], src, AX_X))
                step(v.tensor_scalar(st[0:p, 0, :], st[0:p, 0, :], 1.0 / P, None, ALU.mult))
                step(v.tensor_tensor(xc, src, over(st[0:p, 0, :], 2, P), ALU.subtract))

            def mean_square(step, src, st, sq, eps):
                step(v.tensor_tensor(sq, src, src, ALU.mult))
                step(v.reduce_sum(st, sq, AX_X))
                step(v.tensor_scalar(st, st, 1.0 / P, eps, ALU.mult, ALU.add))

            def ready(t, i):
                if ctx is not None:
                    step = Steps(dve, pre_steps, t)
                    if i == CTX_NORM[0]:
                        dve.wait_ge(c_in_s.sem, c_in_s.at(t, 16))
                        mean_off(step, c_raw[:], stat, c_nrm[:])
                    if i == CTX_NORM[1]:
                        step.k = 3
                        mean_square(step, c_nrm[:], stat[0:keys, 3, :], x_sq[0:keys], w["ceps"])
                    if i == CTX_NORM[2]:
                        step.k = 6
                        dve.wait_ge(pre_powers.sem, pre_powers.at(t, 1))
                        step(v.tensor_tensor(c_nrm[:], c_nrm[:], over(stat[0:keys, 4, :], 2, P), ALU.mult))
                        dve.sem_inc(c_normed.sem, 1)
                if pre:
                    base = 7 if ctx is not None else 0
                    step = Steps(dve, pre_steps, t)
                    if i == X_NORM[0]:
                        dve.wait_ge(x_in_s.sem, x_in_s.at(t, 16))
                        if pre == "ln":
                            step.k = base
                            mean_off(step, x_raw[:], stat, x_nrm[:])
                    if i == X_NORM[1]:
                        step.k = base + (3 if pre == "ln" else 0)
                        mean_square(step, (x_nrm if pre == "ln" else x_raw)[:], stat[:, 5, :], x_sq[:], w["eps"])
                    if i == X_NORM[2]:
                        step.k = base + (6 if pre == "ln" else 3)
                        dve.wait_ge(pre_powers.sem, pre_powers.at(t, 2 if ctx is not None else 1))
                        step(v.tensor_tensor(x_nrm[:], (x_nrm if pre == "ln" else x_raw)[:], over(stat[:, 6, :], 2, P), ALU.mult))
                        dve.sem_inc(normed.sem, 1)

            def project_segments(t):
                dve.wait_ge(seg_made.sem, seg_made.at(t, 1))
                dve.wait_ge(seg_used.sem, seg_used.at(t, 0))
                v.tensor_tensor(seg_d[:], psM[:, 0:QUAD * H].rearrange("p (b n) -> p b n", b=QUAD),
                                over(seg_c[:], 1, QUAD), ALU.add).then_inc(seg_out.sem, 1)

            def ahead(t):
                for i in range(heads_first):
                    soft(t, i)
                    if i >= 1:
                        sums(t, i - 1)

            def project(t):
                if big:
                    for m in range(NQ):
                        dve.wait_ge(proj_v.sem, proj_v.at(t, m + 1))
                        dve.wait_ge(scored.sem, scored.at(t, 0))
                        src = (psT + psO)[m % 4][0:64, 0:QUAD * keys].rearrange("p (b k) -> p b k", b=QUAD)
                        dst = k_bd[0:64, m, :, 0:keys]
                        (v.tensor_scalar(dst, src, bk[0:64, m:m + 1], None, ALU.add) if bk is not None
                         else v.tensor_copy(dst, src)).then_inc(k_half.sem, 1)
                    for i in range(heads_first):
                        soft(t, i)
                    for b in range(QUAD):
                        dve.wait_ge(proj_v.sem, proj_v.at(t, NQ + b + 1))
                        dve.wait_ge(headed.sem, headed.at(t, 0))
                        v.tensor_copy(v_sb[:, b, 512:1024], psT[b % 2][0:keys, :]).then_inc(v_out.sem, 1)
                else:
                    dve.wait_ge(proj_v.sem, proj_v.at(t, 2))
                    dve.wait_ge(headed.sem, headed.at(t, 0))
                    src = psM[0:keys, :].rearrange("p (b h e) -> p b h e", b=QUAD, h=H)
                    dst = v_sb[:, :, :, 0:8]
                    (v.tensor_tensor(dst, src, over(bv[0:keys, :].rearrange("p (h e) -> p h e", h=H), 1, QUAD), ALU.add)
                     if bv is not None else v.tensor_copy(dst, src)).then_inc(v_out.sem, 1)

            def soft(t, i):
                b, g = i // 4, i % 4
                s = i % NB
                src = psS[i % 2][:, 0:GK].rearrange("p (h k) -> p h k", h=G)
                dve.wait_ge(scored.sem, scored.at(t, i + 1))
                dve.wait_ge(exped.sem, exped.at(t, i + 1 - NB))
                if pos is not None:
                    if segments:
                        dve.wait_ge(seg_used.sem, seg_used.at(t, i + 1))
                    else:
                        dve.wait_ge(pos_in[b % 2].sem, pos_in[b % 2].at(t, 16 * (b // 2 + 1)))
                    sv = sc[:, s, :].rearrange("p (h k) -> p h k", h=G)
                    v.tensor_tensor(sv, src, p_sb[:, b % 2, G * g * WIN:G * (g + 1) * WIN].rearrange(
                        "p (h k) -> p h k", h=G)[:, :, 0:S2], ALU.add).then_inc(added.sem, 1)
                    dve.wait_ge(added.sem, added.at(t, i + 1))
                    src = sv
                v.reduce_max(mx[:, s, :], src, AX_X).then_inc(found.sem, 1)
                dve.wait_ge(found.sem, found.at(t, i + 1))
                v.tensor_scalar(mx[:, s, :], mx[:, s, :], -scale, None, ALU.mult).then_inc(maxed.sem, 1)

            def sums(t, i):
                s = i % NB
                dve.wait_ge(exped.sem, exped.at(t, i + 1))
                dve.wait_ge(probs.sem, probs.at(t, i + 1 - NB))
                v.reciprocal(rc[:, s, :], sm[:, s, :]).then_inc(summed.sem, 1)

            def finish(t, i):
                step = Steps(dve, steps, t)
                if i == Y_NORM[0]:
                    step.k = 1
                    mean_off(step, h[:], stat, h[:])
                if i == Y_NORM[1]:
                    step.k = 4
                    mean_square(step, h[:], stat[:, 1, :], x_sq[:], w["eps1"])
                if i == Y_NORM[2]:
                    step.k = 7
                    dve.wait_ge(powers.sem, powers.at(t, 1))
                    step(v.tensor_tensor(y[:], h[:], over(stat[:, 2, :], 2, P), ALU.mult))
                if i == Y_NORM[3]:
                    step.k = 8
                    step(v.tensor_tensor(y[:], y[:], over(rows[:, 0, :], 1, QUAD), ALU.mult))
                    step(v.tensor_tensor(y[:], y[:], over(rows[:, 1, :], 1, QUAD), ALU.add))
                    dve.sem_inc(normed_y.sem, 1)
                if i == HIDDEN:
                    step.k = 10
                    dve.wait_ge(y_turned.sem, y_turned.at(t, 1))
                    step(v.tensor_tensor(y[:], y[:], over(rows[:, 2, :], 1, QUAD), ALU.add))
                if i == Z_NORM[0]:
                    step.k = 11
                    dve.wait_ge(ffn2.sem, ffn2.at(t, 1))
                    step(v.tensor_tensor(h[:], psM[:].rearrange("p (b d) -> p b d", b=QUAD), y[:], ALU.add))
                    dve.sem_inc(ffn2_read.sem, 1)
                    mean_off(step, h[:], stat, h[:])
                if i == Z_NORM[1]:
                    step.k = 15
                    mean_square(step, h[:], stat[:, 1, :], x_sq[:], w["eps2"])
                if i == Z_NORM[2]:
                    step.k = 18
                    dve.wait_ge(powers.sem, powers.at(t, 2))
                    dve.wait_ge(x_stored.sem, x_stored.at(t, 0))
                    step(v.tensor_tensor(x_new[:], h[:], over(stat[:, 2, :], 2, P), ALU.mult))
                    step(v.tensor_tensor(x_new[:], x_new[:], over(rows[:, 3, :], 1, QUAD), ALU.mult))
                    step(v.tensor_tensor(x_new[:], x_new[:], over(rows[:, 4, :], 1, QUAD), ALU.add))
                    dve.sem_inc(done.sem, 1)
                    step.end()

            def residual(t):
                step = Steps(dve, steps, t)
                dve.wait_ge(res_in.sem, res_in.at(t, 16))
                dve.wait_ge(woed.sem, woed.at(t, UN))
                if not post:
                    dve.wait_ge(x_stored.sem, x_stored.at(t, 0))
                step(v.tensor_tensor(h[:], psA[:].rearrange("p (b d) -> p b d", b=QUAD), x_res[:], ALU.add))
                dve.sem_inc(a_read.sem, 1)
                dve.sem_inc(res_used.sem, 1)
                if bo is not None:
                    step(v.tensor_tensor(h[:], h[:], over(bo[:], 1, QUAD), ALU.add))
                if not post:
                    dve.sem_inc(done.sem, 1)
                    step.end()

            def turn(t, first=False, last=False):
                for i in range(heads_first - 1 if big else 0):
                    sums(t, i)
                for i in range(heads_first, UN + 1):
                    if i < UN:
                        soft(t, i)
                    sums(t, i - 1)
                    if i == heads_first and not first:
                        residual(t - 1)
                    if post and not first:
                        finish(t - 1, i)
                    if not last:
                        ready(t + 1, i)

                if not big and not last:
                    ahead(t + 1)

                if not last:
                    if segments:
                        project_segments(t + 1)
                    project(t + 1)

            for i in range(UN):
                ready(0, i)
            if segments:
                project_segments(0)
            if not big:
                ahead(0)
            project(0)
            dve.wait_ge(late_in, 16 * len(late))
            turn(0, first=True)
            with dve.Fori(1, turns - 1) as t:
                turn(t)
            turn(turns - 1, last=True)
            residual(turns - 1)
            if post:
                for i in range(UN + 1):
                    finish(turns - 1, i)
    ph.close()


def position_phase(nc, name, batches, x_in, pos_out, w, *, big, first_at, seg_out=None):
    R2 = 2 * batches
    pairs = P // 2
    NQ = 8 if big else 1
    NO = 2 if big else H
    SPLIT = [(0, 6), (6, 11), (11, 16)]
    ph = Phase(nc, name)
    sb = ph.sbuf
    ident = sb("ident", [P, P])
    wr = sb("wr", [P, NQ * P])
    wqT = sb("wqT", [P, NQ, P])
    peT = sb("peT", [P, RP])
    cols = sb("cols", [P, 5, NQ])
    own = sb("own", [P, NO])
    ones = sb("ones", [P, P])
    rT = sb("rT", [P, NQ, RP])
    r_own = sb("r_own", [P, 2, RP])
    b_rep = sb("b_rep", [P, 2, P])
    e_rep = sb("e_rep", [P, 2, P])
    s_own = sb("s_own", [P, 2, RP])
    win = sb("win", [P, H, RP])
    cst = sb("cst", [P, H, RP])
    if seg_out:
        dcols = sb("dcols", [P, 2, NQ])
        d_own = sb("d_own", [P, H])
        segs = sb("segs", [P, 2, H])
        s_rep = sb("s_rep", [P, NQ, P])
    xi = sb("xi", [P, AT_ONCE, P])
    xiT = sb("xiT", [P, AT_ONCE, P])
    stage = sb("stage", [P, AT_ONCE, H, WIN])
    ps = [[ph.psum(f"ps{s}{c}") for c in range(3)] for s in range(2)]
    psX = [ph.psum(f"psX{s}") for s in range(2)]

    zeroed, made, w_in = ph.sem("zeroed"), ph.sem("identity_made"), ph.sem("weights_loaded")
    r_done, r_copied = ph.sem("r_projected"), ph.sem("r_copied")
    pre_v = ph.sem("constants_prepared")
    win_done, win_copied = ph.sem("windows_done"), ph.sem("windows_copied")
    cst_copied = ph.sem("constants_copied")
    seg_done, seg_copied, seg_stored = ph.sem("segments_done"), ph.sem("segments_copied"), ph.sem("segments_stored")
    apart_v, apart_p = ph.sem("apart_vector"), ph.sem("apart_tensor")
    x_loaded = [ph.counter(f"x_loaded{s}", 32) for s in range(AT_ONCE)]
    turned = ph.counter("x_transposed", AT_ONCE)
    copied = ph.counter("x_copied", AT_ONCE)
    multiplied = ph.counter("products", AT_ONCE)
    staged = ph.counter("rows_staged", AT_ONCE)
    stored = [ph.counter(f"rows_stored{s}", 32) for s in range(AT_ONCE)]

    loads = [(wr[:], w["wr"]), (wqT[:], w["wqT"]), (peT[:], w["peT"]), (own[:], w["own"])]
    loads += [(cols[:, i, :], w[n]) for i, n in enumerate(("pb", "sb", "cb", "se0", "se1")) if n in w]
    turns = pairs // AT_ONCE
    extra = "sb" in w

    with nc.Block() as block:

        @block.gpsimd
        def _(pool):
            make_identity(nc, pool, ident, zeroed, made)
            nc.gpsimd.memset(ones[:], 1.0).then_inc(made, 1)

        @block.sync
        def _(sp):
            for t, src in loads:
                sp.dma_start(t, src).then_inc(w_in, 16)
            if seg_out:
                sp.wait_ge(seg_copied, 1)
                sp.dma_start(seg_out[0], segs[:, 0, :]).then_inc(seg_stored, 16)
                sp.dma_start(seg_out[1], segs[:, 1, :]).then_inc(seg_stored, 16)
                sp.wait_ge(seg_stored, 32)
            with sp.Fori(0, turns) as t:
                for s in range(AT_ONCE):
                    sp.wait_ge(staged.sem, staged.at(t, s + 1))
                    for i in range(2):
                        at = ROW0 - 1 + i
                        sp.dma_start(pos_out[:, bass.ds(t * 2 * AT_ONCE + 2 * s + i, 1), at:at + H * WIN].rearrange("b i n -> b (i n)"),
                                     stage[batches * i:batches * (i + 1), s, :, :].rearrange("p n j -> p (n j)")
                                     ).then_inc(stored[s].sem, 16)
            for s in range(AT_ONCE):
                sp.wait_ge(stored[s].sem, 32 * turns)

        @block.scalar
        def _(act):
            def load(t, s):
                for i in range(2):
                    act.dma_start(xi[batches * i:batches * (i + 1), s, :],
                                  x_in[:, bass.ds(t * 2 * AT_ONCE + 2 * s + i, 1), :].rearrange("b i d -> b (i d)")
                                  ).then_inc(x_loaded[s].sem, 16)

            for s in range(AT_ONCE):
                load(0, s)
            for m in range(NQ):
                act.wait_ge(r_done, m + 1)
                nc.scalar.activation(rT[:, m, :], psX[m % 2][:, 0:RP], ACT.Copy).then_inc(r_copied, 1)
            for n in range(H):
                act.wait_ge(win_done, n + 1)
                nc.scalar.activation(win[:, n, :], ps[n % 2][0][:, 0:RP], ACT.Copy).then_inc(win_copied, 1)
            if seg_out:
                act.wait_ge(seg_done, 1)
                nc.scalar.activation(segs[:].rearrange("p a n -> p (a n)"), psX[0][:, 0:2 * H], ACT.Copy).then_inc(seg_copied, 1)

            def turn(t, first=False, last=False):
                for s in range(AT_ONCE):
                    act.wait_ge(turned.sem, turned.at(t, s + 1))
                    if not last:
                        load(t + 1, s)
                    if not first:
                        act.wait_ge(multiplied.sem, multiplied.at(t - 1, s + 1))
                    nc.scalar.activation(xiT[:, s, 0:R2], psX[s % 2][:, 0:R2], ACT.Copy).then_inc(copied.sem, 1)

            turn(0, first=True)
            with act.Fori(1, turns - 1) as t:
                turn(t)
            turn(turns - 1, last=True)

        @block.vector
        def _(dve):
            v = nc.vector
            dve.wait_ge(w_in, 16 * len(loads))
            dve.wait_ge(made, 2)
            done = 0
            if extra:
                v.tensor_tensor(cols[:, 2, :], cols[:, 1, :], cols[:, 2, :], ALU.subtract).then_inc(pre_v, 1)
                v.tensor_tensor(dcols[:, 0, :], cols[:, 4, :], cols[:, 3, :], ALU.subtract).then_inc(pre_v, 1)
                dve.wait_ge(pre_v, 2)
                v.tensor_tensor(s_rep[:], over(ones[:], 1, NQ), over(cols[:, 1, :], 2, P), ALU.mult).then_inc(pre_v, 1)
                done = 3
                for n in range(H):
                    m, o = n // NO, n % NO
                    v.tensor_tensor(d_own[:, n:n + 1], dcols[:, 0, m:m + 1], own[:, o:o + 1], ALU.mult).then_inc(pre_v, 1)
                    done += 1
            for n in range(H):
                m, o = n // NO, n % NO
                dve.wait_ge(r_copied, m + 1)
                if n >= 2:
                    dve.wait_ge(win_done, n - 1)
                v.tensor_scalar(r_own[:, n % 2, :], rT[:, m, :], own[:, o:o + 1], None, ALU.mult).then_inc(pre_v, 1)
                v.tensor_scalar(b_rep[:, n % 2, :], ones[:], cols[:, 0, m:m + 1], None, ALU.mult).then_inc(pre_v, 1)
                done += 2
                if extra:
                    v.tensor_scalar(e_rep[:, n % 2, :], ones[:], cols[:, 2, m:m + 1], None, ALU.mult).then_inc(pre_v, 1)
                    v.tensor_tensor(s_own[:, n % 2, :], over(cols[:, 3, m], 1, RP), over(own[:, o], 1, RP), ALU.mult
                                    ).then_inc(pre_v, 1)
                    done += 2
                if n >= 1:
                    dve.wait_ge(win_done, n)
                    v.tensor_copy(cst[:, n - 1, :], ps[(n - 1) % 2][1][:, 0:RP]).then_inc(cst_copied, 1)
            dve.wait_ge(win_done, H)
            v.tensor_copy(cst[:, H - 1, :], ps[(H - 1) % 2][1][:, 0:RP]).then_inc(cst_copied, 1)
            dve.wait_ge(cst_copied, H)
            with dve.Fori(0, turns) as t:
                for s in range(AT_ONCE):
                    dve.wait_ge(multiplied.sem, multiplied.at(t, s + 1))
                    dve.wait_ge(stored[s].sem, stored[s].at(t, 0))
                    dve.sem_inc(apart_v, 1)
                    for c, (a, b) in enumerate(SPLIT):
                        ins = v.tensor_tensor(
                            stage[0:R2, s, a:b, :], ps[s % 2][c][0:R2, 0:(b - a) * WIN].rearrange("p (n j) -> p n j", n=b - a),
                            cst[0:R2, a:b, bass.ds(first_at - 2 * s - t * 2 * AT_ONCE, WIN)], ALU.add)
                    ins.then_inc(staged.sem, 1)

        @block.tensor
        def _(pe):
            pe.wait_ge(w_in, 16 * len(loads))
            pe.wait_ge(made, 2)
            for m in range(NQ):
                if m >= 2:
                    pe.wait_ge(r_copied, m - 1)
                pe.matmul(psX[m % 2][:, 0:RP], wr[:, m * P:(m + 1) * P], peT[:], start=True, stop=True).then_inc(r_done, 1)
            pre = 3 + H if extra else 0
            for n in range(H):
                m = n // NO
                pe.wait_ge(pre_v, pre + (4 if extra else 2) * (n + 1))
                if n >= 2:
                    pe.wait_ge(win_copied, n - 1)
                    pe.wait_ge(cst_copied, n - 1)
                pe.matmul(ps[n % 2][0][:, 0:RP], wqT[:, m, :], r_own[:, n % 2, :], start=True, stop=True)
                mm = pe.matmul(ps[n % 2][1][:, 0:RP], b_rep[:, n % 2, :], r_own[:, n % 2, :], start=True, stop=not extra)
                if extra:
                    mm = pe.matmul(ps[n % 2][1][:, 0:RP], e_rep[:, n % 2, :], s_own[:, n % 2, :], start=False, stop=True)
                mm.then_inc(win_done, 1)
            if seg_out:
                pe.wait_ge(r_copied, NQ)
                for n in range(H):
                    m = n // NO
                    pe.matmul(psX[0][:, n:n + 1], wqT[:, m, :], d_own[:, n:n + 1], start=True, stop=True)
                    mm = pe.matmul(psX[0][:, H + n:H + n + 1], s_rep[:, m, :], d_own[:, n:n + 1], start=True, stop=True)
                mm.then_inc(seg_done, 1)
            pe.wait_ge(win_copied, H)
            pe.wait_ge(cst_copied, H)
            if seg_out:
                pe.wait_ge(seg_copied, 1)

            def transpose(t, s, first=False):
                pe.wait_ge(x_loaded[s].sem, x_loaded[s].at(t, 32))
                if not first:
                    pe.wait_ge(copied.sem, copied.at(t, 0) + s - 1)
                pe.transpose(psX[s % 2][:, 0:R2], xi[0:R2, s, :], ident[0:R2, 0:R2]).then_inc(turned.sem, 1)

            def products(t, s, first=False):
                pe.wait_ge(copied.sem, copied.at(t, s + 1))
                if not first:
                    pe.wait_ge(staged.sem, staged.at(t, 0) + s - 1)
                    pe.sem_inc(apart_p, 1)
                for c, (a, b) in enumerate(SPLIT):
                    mm = pe.matmul(ps[s % 2][c][0:R2, 0:(b - a) * WIN], xiT[:, s, 0:R2],
                                   win[:, a:b, bass.ds(first_at - 2 * s - t * 2 * AT_ONCE, WIN)], start=True, stop=True)
                mm.then_inc(multiplied.sem, 1)

            def turn(t, first=False, last=False):
                for s in range(AT_ONCE):
                    products(t, s, first=first and s < 2)
                    if s + 2 < AT_ONCE:
                        transpose(t, s + 2)
                    elif not last:
                        transpose(t + 1, s + 2 - AT_ONCE)

            for s in range(2):
                transpose(0, s, first=True)
            turn(0, first=True)
            with pe.Fori(1, turns - 1) as t:
                turn(t)
            turn(turns - 1, last=True)
    ph.close()


def experts_phase(nc, name, turns, x_in, x_out, w):
    ph = Phase(nc, name)
    sb = ph.sbuf
    ident = sb("ident", [P, P])
    halfs = sb("halfs", [P, QUAD])
    number = sb("number", [P, E])
    rw = sb("rw", [P, E])
    rb = sb("rb", [P, E])
    xs = sb("xs", [P, 1])
    xb = sb("xb", [P, 1])
    w1 = sb("w1", [P, E, FF * P])
    b1 = sb("b1", [P, E, FF])
    w2 = sb("w2", [P, E, FF * P])
    b2 = sb("b2", [P, E, P])
    x_raw = sb("x_raw", [P, QUAD, P])
    xc = sb("xc", [P, QUAD, P])
    sq = sb("sq", [P, QUAD, P])
    stat = sb("stat", [P, 3, QUAD])
    hT = sb("hT", [P, QUAD * P])
    logit = sb("logit", [P, QUAD, E])
    best = sb("best", [P, QUAD, 8])
    at_u = sb("at_u", [P, QUAD, 8], U32)
    at_f = sb("at_f", [P, QUAD, 8])
    e2 = sb("e2", [P, 5, QUAD])
    pick = sb("pick", [P, 2, QUAD, E])
    gate = sb("gate", [P, QUAD, E])
    u = sb("u", [P, 2, FF, QUAD * P])
    t_sb = sb("t_sb", [P, 2, QUAD, P])
    acc = sb("acc", [P, QUAD, P])
    ps1 = [ph.psum(f"ps1{i}") for i in range(4)]
    ps2 = [ph.psum(f"ps2{i}") for i in range(2)]
    psM = ph.psum("psM")
    psL = ph.psum("psL")

    zeroed, made, w_in = ph.sem("zeroed"), ph.sem("constants_made"), ph.sem("router_weights_loaded")
    w1_in, w2_in = ph.sem("first_layers_loaded"), ph.sem("second_layers_loaded")
    apart = ph.sem("apart")
    x_loaded = ph.counter("x_loaded", 16)
    steps = ph.counter("norm_steps", 7)
    gate_steps = ph.counter("gate_steps", 12)
    powers = ph.counter("inverse_roots", 1)
    turned = ph.counter("transposed", 1)
    copied = ph.counter("transposed_copied", 1)
    logits = ph.counter("logits", 1)
    gap = ph.counter("logit_gap", 1)
    gap_exp = ph.counter("logit_gap_exponential", 1)
    hidden = ph.counter("hidden", E * FF)
    active = ph.counter("activated", E * FF)
    outs = ph.counter("expert_outputs", E)
    taken = ph.counter("expert_outputs_taken", E)
    mixed = ph.counter("outputs_mixed", E)
    stored = ph.counter("x_stored", 16)
    loads = [(rw[:], w["rw"]), (rb[:], w["rb"]), (xs[:], w["xs"]), (xb[:], w["xb"]), (b1[:], w["b1"])]

    with nc.Block() as block:

        @block.gpsimd
        def _(pool):
            make_identity(nc, pool, ident, zeroed, made)
            nc.gpsimd.memset(halfs[:], -0.5).then_inc(made, 1)
            for e in range(E):
                ins = nc.gpsimd.memset(number[:, e:e + 1], float(e))
            ins.then_inc(made, 1)
            with pool.Fori(0, turns) as t:
                pool.wait_ge(steps.sem, steps.at(t, 6))
                nc.gpsimd.tensor_tensor(stat[:, 2, :], stat[:, 1, :], halfs[:], ALU.pow).then_inc(powers.sem, 1)

        @block.sync
        def _(sp):
            def load(t):
                sp.dma_start(x_raw[:], x_in[bass.ds(t * QUAD, QUAD)].rearrange("b p d -> p b d")).then_inc(x_loaded.sem, 16)

            def store(t):
                sp.wait_ge(mixed.sem, mixed.at(t, E))
                sp.dma_start(x_out[bass.ds(t * QUAD, QUAD)].rearrange("b p d -> p b d"), acc[:]).then_inc(stored.sem, 16)

            load(0)
            for t, src in loads:
                sp.dma_start(t, src).then_inc(w_in, 16)
            sp.dma_start(w1[:], w["w1"]).then_inc(w1_in, 16)
            sp.dma_start(w2[:], w["w2"]).then_inc(w2_in, 16)
            sp.dma_start(b2[:], w["b2"]).then_inc(w2_in, 16)
            with sp.Fori(0, turns - 1) as t:
                sp.wait_ge(mixed.sem, mixed.at(t, 1))
                load(t + 1)
                store(t)
            store(turns - 1)
            sp.wait_ge(stored.sem, 16 * turns)

        @block.scalar
        def _(act):
            act.wait_ge(w_in, 16 * len(loads))

            def router(t):
                act.wait_ge(turned.sem, turned.at(t, 1))
                act.wait_ge(hidden.sem, hidden.at(t, 0))
                nc.scalar.activation(hT[:], psM[:], ACT.Identity, bias=xb[:, 0:1], scale=xs[:, 0:1]).then_inc(copied.sem, 1)
                act.wait_ge(gap.sem, gap.at(t, 1))
                nc.scalar.activation(e2[:, 1, :], e2[:, 0, :], ACT.Exp).then_inc(gap_exp.sem, 1)

            def turn(t, first=False, last=False):
                for e in range(E):
                    for f in range(FF):
                        act.wait_ge(hidden.sem, hidden.at(t, e * FF + f + 1))
                        if e >= 2 or not first:
                            act.wait_ge(outs.sem, outs.at(t, 0) + e - 1)
                        nc.scalar.activation(u[:, e % 2, f, :], ps1[f][:], ACT.Gelu, bias=b1[:, e, f:f + 1]
                                             ).then_inc(active.sem, 1)
                if not last:
                    router(t + 1)

            router(0)
            turn(0, first=True)
            with act.Fori(1, turns - 1) as t:
                turn(t)
            turn(turns - 1, last=True)

        @block.tensor
        def _(pe):
            pe.wait_ge(w_in, 16 * len(loads))
            pe.wait_ge(made, 3)

            def transposes(t):
                pe.wait_ge(steps.sem, steps.at(t, 7))
                pe.wait_ge(copied.sem, copied.at(t, 0))
                for b in range(QUAD):
                    mm = pe.transpose(psM[:, b * P:(b + 1) * P], xc[:, b, :], ident[:])
                mm.then_inc(turned.sem, 1)

            def router(t):
                pe.wait_ge(copied.sem, copied.at(t, 1))
                pe.wait_ge(gate_steps.sem, gate_steps.at(t, 0))
                for b in range(QUAD):
                    mm = pe.matmul(psL[:, b * E:(b + 1) * E], hT[:, b * P:(b + 1) * P], rw[:], start=True, stop=True)
                mm.then_inc(logits.sem, 1)

            def first_layer(t, e):
                for f in range(FF):
                    pe.wait_ge(active.sem, active.at(t, (e - 1) * FF + f + 1))
                    pe.matmul(ps1[f][:], w1[:, e, f * P:(f + 1) * P], hT[:], start=True, stop=True
                              ).then_inc(hidden.sem, 1)

            def second_layer(t, e):
                pe.wait_ge(active.sem, active.at(t, (e + 1) * FF))
                pe.wait_ge(taken.sem, taken.at(t, e - 1))
                for b in range(QUAD):
                    for f in range(FF):
                        mm = pe.matmul(ps2[e % 2][:, b * P:(b + 1) * P], u[:, e % 2, f, b * P:(b + 1) * P],
                                       w2[:, e, f * P:(f + 1) * P], start=(f == 0), stop=(f == FF - 1))
                mm.then_inc(outs.sem, 1)

            def turn(t, last=False):
                for e in range(E):
                    if e + 1 < E:
                        first_layer(t, e + 1)
                    elif not last:
                        router(t + 1)
                        first_layer(t + 1, 0)
                    second_layer(t, e)
                    if e == E - 3 and not last:
                        transposes(t + 1)

            transposes(0)
            router(0)
            pe.wait_ge(w1_in, 16)
            first_layer(0, 0)
            pe.wait_ge(w2_in, 16 * 2)
            with pe.Fori(0, turns - 1) as t:
                turn(t)
            turn(turns - 1, last=True)

        @block.vector
        def _(dve):
            v = nc.vector
            dve.wait_ge(w_in, 16 * len(loads))
            dve.wait_ge(made, 3)

            def norm(t, part):
                step = Steps(dve, steps, t)
                if part == 0:
                    dve.wait_ge(x_loaded.sem, x_loaded.at(t, 16))
                    step(v.reduce_sum(stat[:, 0, :], x_raw[:], AX_X))
                    step(v.tensor_scalar(stat[:, 0, :], stat[:, 0, :], 1.0 / P, None, ALU.mult))
                    dve.wait_ge(turned.sem, turned.at(t, 0))
                    step(v.tensor_tensor(xc[:], x_raw[:], over(stat[:, 0, :], 2, P), ALU.subtract))
                if part == 1:
                    step.k = 3
                    step(v.tensor_tensor(sq[:], xc[:], xc[:], ALU.mult))
                    step(v.reduce_sum(stat[:, 1, :], sq[:], AX_X))
                    step(v.tensor_scalar(stat[:, 1, :], stat[:, 1, :], 1.0 / P, w["eps"], ALU.mult, ALU.add))
                if part == 2:
                    step.k = 6
                    dve.wait_ge(powers.sem, powers.at(t, 1))
                    step(v.tensor_tensor(xc[:], xc[:], over(stat[:, 2, :], 2, P), ALU.mult))
                    step.end()

            def choose(t):
                step = Steps(dve, gate_steps, t)
                dve.wait_ge(logits.sem, logits.at(t, 1))
                step(v.tensor_tensor(logit[:], psL[:, 0:QUAD * E].rearrange("p (b e) -> p b e", b=QUAD),
                                     over(rb[:], 1, QUAD), ALU.add))
                dve.sem_inc(apart, 1)
                for b in range(QUAD):
                    ins = v.max(best[:, b, :], logit[:, b, :])
                step(ins)
                dve.sem_inc(apart, 1)
                for b in range(QUAD):
                    ins = v.max_index(at_u[:, b, :], best[:, b, :], logit[:, b, :])
                step(ins)
                dve.wait_ge(gap_exp.sem, gap_exp.at(t, 0))
                v.tensor_tensor(e2[:, 0, :], best[:, :, 1], best[:, :, 0], ALU.subtract).then_inc(gap.sem, 1)
                step(v.tensor_copy(at_f[:], at_u[:]))
                dve.wait_ge(gap_exp.sem, gap_exp.at(t, 1))
                step(v.tensor_scalar(e2[:, 2, :], e2[:, 1, :], 1.0, None, ALU.add))
                step(v.reciprocal(e2[:, 3, :], e2[:, 2, :]))
                step(v.tensor_tensor(e2[:, 4, :], e2[:, 3, :], e2[:, 1, :], ALU.mult))

            def gates(t):
                step = Steps(dve, gate_steps, t)
                step.k = 7
                for i in range(2):
                    step(v.tensor_tensor(pick[:, i], over(at_f[:, :, i], 2, E), over(number[:], 1, QUAD), ALU.is_equal))
                    step(v.tensor_tensor(pick[:, i], pick[:, i], over(e2[:, 3 + i, :], 2, E), ALU.mult))
                dve.wait_ge(mixed.sem, mixed.at(t, 0))
                step(v.tensor_tensor(gate[:], pick[:, 0], pick[:, 1], ALU.add))
                step.end()

            def mix(t, e):
                dve.wait_ge(outs.sem, outs.at(t, e + 1))
                v.tensor_tensor(t_sb[:, e % 2], ps2[e % 2][:].rearrange("p (b d) -> p b d", b=QUAD),
                                over(b2[:, e, :], 1, QUAD), ALU.add).then_inc(taken.sem, 1)
                dve.wait_ge(taken.sem, taken.at(t, e + 1))
                dve.wait_ge(mixed.sem, mixed.at(t, e))
                if e == 0:
                    dve.wait_ge(stored.sem, stored.at(t, 0))
                for b in range(QUAD):
                    ins = v.scalar_tensor_tensor(out=acc[:, b, :], in0=t_sb[:, e % 2, b, :], scalar=gate[:, b, e:e + 1],
                                                 in1=(acc if e else x_raw)[:, b, :], op0=ALU.mult, op1=ALU.add)
                ins.then_inc(mixed.sem, 1)

            def turn(t, last=False):
                for e in range(E):
                    if e == E - 1 and not last:
                        choose(t + 1)
                    mix(t, e)
                    if not last and 2 <= e < 5:
                        norm(t + 1, e - 2)
                if not last:
                    gates(t + 1)

            for part in range(3):
                norm(0, part)
            choose(0)
            gates(0)
            dve.wait_ge(w2_in, 16 * 2)
            with dve.Fori(0, turns - 1) as t:
                turn(t)
            turn(turns - 1, last=True)
    ph.close()


def build(nc, a, out, turns=16, layers=9):
    B = turns * QUAD
    x = [nc.dram_tensor(f"x_{i}", [B, P, P], F32, kind="Internal").ap() for i in range(6)]
    pos = nc.dram_tensor("shifted_scores", [B, P, ROW], F32, kind="Internal").ap()
    seg = nc.dram_tensor("segment_terms", [2, P, H], F32, kind="Internal").ap()
    row = lambda name: a[name].rearrange("(o d) -> o d", o=1).broadcast_to([P, a[name].shape[0]])
    col = lambda name: a[name].rearrange("(d o) -> d o", o=1)
    ctxT = a["ctxT"]
    dst = lambda i: out if i == layers else x[i]

    position_phase(nc, "pos0", B, a["x"], pos, dict(
        wr=a["L0_Wr"], wqT=a["L0_WqT"], peT=a["L0_peT"], own=a["own64"], pb=a["L0_pb"], sb=a["L0_sb"],
        cb=a["L0_cb"], se0=a["L0_se0"], se1=a["L0_se1"]), big=True, first_at=P - 1, seg_out=seg)
    attention_phase(nc, "att0", turns, a["x"], out if layers == 0 else x[0], dict(
        wq=a["L0_Wq"], wk=a["L0_Wk"], wv=a["L0_Wv"], wo=a["L0_Wo"], bq=a["L0_cb"], bk=a["L0_se0"],
        w1=a["L0_W1"], b1=a["L0_b1"], w2=a["L0_W2"], g1=row("L0_g1"), be1=row("L0_be1"), b2=row("L0_b2"),
        g2=row("L0_g2"), be2=row("L0_be2"), eps1=1e-12, eps2=1e-12,
        seg_w=seg[0], seg_c=seg[1], seg_m=a["seg_mask"], neg_m=a["mask"]),
        dim=64, keys=S2, ctxT=ctxT, pos=pos, post=ACT.Relu, scale=0.125, segments=True)
    if layers == 0:
        return
    attention_phase(nc, "att1", turns, x[0], out if layers == 1 else x[1], dict(
        wq=a["L1_wq"], wk=a["L1_wk"], wv=a["L1_wv"], wo=a["L1_wo"], xs=col("L1_norm_w"), eps=1e-6),
        dim=64, keys=S2, ctxT=ctxT, pre="rms")
    if layers == 1:
        return
    position_phase(nc, "pos2", B, x[1], pos, dict(
        wr=a["L2_w_r"], wqT=a["L2_w_qT"], peT=a["L2_peT"], own=a["own8"], pb=a["L2_rr"]), big=False, first_at=P - 2)
    attention_phase(nc, "att2", turns, x[1], out if layers == 2 else x[2], dict(
        wq=a["L2_w_q"], wk=a["L2_w_k"], wv=a["L2_w_v"], wo=a["L2_w_o"], bq=a["L2_rw"], own=a["own8"],
        w1=a["L2_W1"], b1=a["L2_b1"], w2=a["L2_W2"], g1=row("L2_g1"), be1=row("L2_be1"), b2=row("L2_b2"),
        g2=row("L2_g2"), be2=row("L2_be2"), eps1=1e-9, eps2=1e-9),
        dim=8, keys=S2, ctxT=ctxT, pos=pos, post=ACT.Gelu_apprx_tanh, scale=8.0 ** -0.5)
    if layers == 2:
        return
    attention_phase(nc, "att3", turns, x[2], out if layers == 3 else x[3], dict(
        wq=a["sa_wq"], wk=a["sa_wk"], wv=a["sa_wv"], wo=a["sa_wo"], bq=a["sa_bq"], bk=a["sa_bk"], bv=row("sa_bv"),
        bo=row("sa_bo"), own=a["own8"], xs=col("sa_g"), xb=col("sa_b"), eps=1e-5),
        dim=8, keys=P, pre="ln", scale=8.0 ** -0.5)
    if layers == 3:
        return
    attention_phase(nc, "att4", turns, x[3], out if layers == 4 else x[4], dict(
        wq=a["ca_wq"], wk=a["ca_wk"], wv=a["ca_wv"], wo=a["ca_wo"], bq=a["ca_bq"], bk=a["ca_bk"], bv=row("ca_bv"),
        bo=row("ca_bo"), own=a["own8"], xs=col("ca_qg"), xb=col("ca_qb"), cs=col("ca_kg"), cb=col("ca_kb"),
        eps=1e-5, ceps=1e-5), dim=8, keys=S2, ctx=a["ctx"], pre="ln", scale=8.0 ** -0.5)
    if layers == 4:
        return
    experts_phase(nc, "moe", turns, x[4], out, dict(
        rw=a["rwT"], rb=row("rb"), xs=col("moe_g"), xb=col("moe_b"), w1=a["e_w1"], b1=a["e_b1"], w2=a["e_w2"],
        b2=a["e_b2"].rearrange("(o e) d -> o (e d)", o=1).broadcast_to([P, E * P]).rearrange("p (e d) -> p e d", e=E), eps=1e-5))


def lay_out(i):
    A = np.ascontiguousarray
    L0, L1, L2, L3 = (lambda n, k=k: np.asarray(i[f"L{k}_xattn_{n}"]) for k in range(4))
    o = {}
    o["x"] = np.asarray(i["x"])
    o["ctx"] = np.asarray(i["ctx_1024"])
    o["ctxT"] = o["ctx"].transpose(0, 2, 1)
    o["mask"] = np.asarray(i["mask_1x1xSxS2_ff0"])[0, 0]
    o["seg_mask"] = np.asarray(i["mask_1xSxS2_bk1"])[0]
    o["own64"] = np.repeat(np.eye(2, dtype=np.float32), 64, axis=0)
    o["own8"] = np.repeat(np.eye(H, dtype=np.float32), 8, axis=0)
    chunk = lambda m: m.reshape(-1, P, m.shape[-1]).transpose(1, 0, 2)
    heads = lambda m: m.reshape(-1, P).T
    for n in ("Wq", "Wk", "Wv", "Wr"):
        o["L0_" + n] = L0(n).reshape(P, -1)
    o["L0_WqT"] = chunk(o["L0_Wq"].T)
    o["L0_Wo"] = chunk(L0("Wo").reshape(P, -1).T).reshape(P, -1)
    o["L0_peT"] = L0("position_encoding")[0, :RP].T
    for n, s in (("pb", L0("position_bias")), ("sb", L0("segment_bias")), ("cb", L0("content_bias")),
                 ("se0", L0("segment_encoding")[0]), ("se1", L0("segment_encoding")[1])):
        o["L0_" + n] = heads(s)
    o["L0_W1"], o["L0_b1"], o["L0_W2"] = L0("W1"), heads(L0("b1")), chunk(L0("W2"))
    o["L0_b2"], o["L0_g1"], o["L0_be1"], o["L0_g2"], o["L0_be2"] = (
        L0("b2"), L0("ln1_gamma"), L0("ln1_beta"), L0("ln2_gamma"), L0("ln2_beta"))
    for n in ("wq", "wk", "wv"):
        o["L1_" + n] = L1(n)
    o["L1_wo"] = chunk(L1("wo")).reshape(P, -1)
    o["L1_norm_w"] = L1("norm_w")
    for n in ("w_q", "w_k", "w_v", "w_r"):
        o["L2_" + n] = L2(n).reshape(P, P)
    o["L2_w_qT"] = chunk(o["L2_w_q"].T)

    def spaced(m):
        s = np.zeros((G, 32, G, P), np.float32)
        s[:, :8] = m.reshape(G, G, 8, P).transpose(1, 2, 0, 3)
        return s.reshape(P, G * P)

    o["L2_w_o"] = spaced(L2("w_o").reshape(P, P))
    pe = L2("pos_emb")
    at = (np.arange(204) - 51) % pe.shape[0]
    o["L2_peT"] = np.concatenate([pe[at], pe[:1]]).T
    o["L2_rw"], o["L2_rr"] = heads(L2("r_w_bias")), heads(L2("r_r_bias"))
    o["L2_W1"], o["L2_b1"], o["L2_W2"] = L2("ffn_w1"), heads(L2("ffn_b1")), chunk(L2("ffn_w2"))
    o["L2_b2"], o["L2_g1"], o["L2_be1"], o["L2_g2"], o["L2_be2"] = (
        L2("ffn_b2"), L2("ln1_g"), L2("ln1_b"), L2("ln2_g"), L2("ln2_b"))
    for k in ("sa", "ca"):
        iw, ib = L3(f"{k}_in_w"), L3(f"{k}_in_b")
        o[f"{k}_wq"], o[f"{k}_wk"], o[f"{k}_wv"] = iw[:P].T, iw[P:2 * P].T, iw[2 * P:].T
        o[f"{k}_bq"], o[f"{k}_bk"], o[f"{k}_bv"] = ib[:P, None], ib[P:2 * P, None], ib[2 * P:]
        o[f"{k}_wo"] = spaced(L3(f"{k}_out_w").T)
        o[f"{k}_bo"] = L3(f"{k}_out_b")
    o["sa_g"], o["sa_b"] = L3("sa_ln_g"), L3("sa_ln_b")
    o["ca_qg"], o["ca_qb"], o["ca_kg"], o["ca_kb"] = L3("ca_q_ln_g"), L3("ca_q_ln_b"), L3("ca_kv_ln_g"), L3("ca_kv_ln_b")
    o["moe_g"], o["moe_b"], o["rwT"], o["rb"] = L3("moe_ln_g"), L3("moe_ln_b"), L3("router_w").T, L3("router_b")
    o["e_w1"] = L3("e_fc1_w").transpose(2, 0, 1)
    o["e_b1"] = L3("e_fc1_b").reshape(E, FF, P).transpose(2, 0, 1)
    o["e_w2"] = L3("e_fc2_w").reshape(E, P, FF, P).transpose(3, 0, 2, 1).reshape(P, E, FF * P)
    o["e_b2"] = L3("e_fc2_b")
    return {k: A(v) for k, v in o.items()}


def kernel(**inputs):
    import concourse.bacc as bacc
    from concourse.bass_utils import run_bass_kernel_spmd

    arrays = lay_out(inputs)
    nc = bacc.Bacc("TRN2", target_bir_lowering=False, num_devices=1)
    args = {n: nc.dram_tensor(f"in_{n}", v.shape, mybir.dt.from_np(v.dtype), kind="ExternalInput").ap()
            for n, v in arrays.items()}
    out = nc.dram_tensor("out_0", (64, P, P), F32, kind="ExternalOutput").ap()
    build(nc, args, out)
    r = run_bass_kernel_spmd(nc, [{f"in_{n}": v for n, v in arrays.items()}], core_ids=[0])
    return r.results[0]["out_0"]
```
